# Optimizing a Trainium2 kernel written in Bass

```python
import numpy as np
import jax
import jax.numpy as jnp

def _softmax(x, axis=-1):
    return jax.nn.softmax(x, axis=axis)

def _gelu(x):
    return jax.nn.gelu(x, approximate=True)

def _silu(x):
    return jax.nn.silu(x)

def _sigmoid(x):
    return jax.nn.sigmoid(x)

def _layernorm(x, axis=-1, eps=1e-05):
    m = jnp.mean(x, axis=axis, keepdims=True)
    v = jnp.var(x, axis=axis, keepdims=True)
    return (x - m) / jnp.sqrt(v + eps)

def _scatter_add(tgt, idx, src, axis=0):
    return tgt.at[idx].add(src)

def _segment_sum(src, seg, n):
    return jax.ops.segment_sum(src, seg, n)
kernel_name = 'mk_decoder_preln_d2_seqx_r4_004f61'

def setup_inputs(seed: int=0):
    np.random.seed(seed)
    _w = jnp.asarray

    def _rec_inputs():
        import jax
        import jax.numpy as jnp
        _rk = jax.random.key(seed)
        x = -0.0005146 + 1 * jax.random.normal(jax.random.fold_in(_rk, 1), (32, 100, 256), jnp.float32)
        _lenS = 100 - jax.random.randint(jax.random.fold_in(_rk, 7), (32,), 0, max(1, 100 // 4) + 1, jnp.int32)
        _lenS2 = 361 - jax.random.randint(jax.random.fold_in(_rk, 8), (32,), 0, max(1, 361 // 4) + 1, jnp.int32)
        _ctx_768P = jax.random.normal(jax.random.fold_in(_rk, 11), (32, 16, 192), jnp.float32)
        _ctx_768c = jax.random.dirichlet(jax.random.fold_in(_rk, 511), 0.3 * jnp.ones((16,), jnp.float32), (32, 361))
        _ctx_768t = jnp.einsum('bsk,bkd->bsd', _ctx_768c, _ctx_768P)
        _ctx_768t = _ctx_768t * jax.lax.rsqrt(jnp.mean(jnp.square(_ctx_768t)) + 1e-12) * 0.953939
        ctx_768 = -0.00040386 + 0.999972 * (_ctx_768t + 0.3 * jax.random.normal(jax.random.fold_in(_rk, 611), (32, 361, 192), jnp.float32))
        _validS = jnp.arange(100)[None, :] < _lenS[:, None]
        _validS2 = jnp.arange(361)[None, :] < _lenS2[:, None]
        _causal = jnp.tril(jnp.ones((100, 100), dtype=bool))
        mask_BxS2_bk0 = jnp.logical_not(jnp.broadcast_to(_validS2[:, :], (32, 361)))
        mask_1x1xSxS2_bk0 = jnp.logical_not(jnp.broadcast_to(_validS2[0:1, None, None, :], (1, 1, 100, 361)))
        return (x, ctx_768, mask_BxS2_bk0, mask_1x1xSxS2_bk0)
    x, ctx_768, mask_BxS2_bk0, mask_1x1xSxS2_bk0 = _rec_inputs()

    def _L0_attn_setup():
        import math
        import jax, jax.numpy as jnp
        import numpy as np
        B, T, D, H = (4, 512, 256, 16)
        HD = D // H
        key = jax.random.key(seed)
        k1, k2, k3 = jax.random.split(key, 3)
        x = jax.random.normal(k1, (B, T, D), dtype=jnp.float32)
        w_qkv = jax.random.normal(k2, (D, 3 * D), dtype=jnp.float32) * (1.0 / math.sqrt(D))
        w_proj = jax.random.normal(k3, (D, D), dtype=jnp.float32) * (1.0 / math.sqrt(D))
        return {'x': x, 'w_qkv': w_qkv, 'w_proj': w_proj}
    _L0_attn_all = _L0_attn_setup()
    _L0_attn_in = {k: v for k, v in _L0_attn_all.items() if k in ('w_qkv', 'w_proj')}
    del _L0_attn_all

    def _L0_xattn_setup():
        import jax, jax.numpy as jnp
        import numpy as np
        DIM_IN, DIM_LAT, DIM_HEAD = (192, 256, 64)
        INNER = max(DIM_LAT, DIM_IN)
        HEADS = INNER // DIM_HEAD
        SCALE = DIM_HEAD ** (-0.5)
        RMS_EPS = 1e-08
        LN_EPS = 1e-05

        def layernorm(x, g, b):
            mu = jnp.mean(x, axis=-1, keepdims=True)
            var = jnp.mean((x - mu) ** 2, axis=-1, keepdims=True)
            return (x - mu) * jax.lax.rsqrt(var + LN_EPS) * g + b

        def rmsnorm(x, gamma):
            norm = jnp.sqrt(jnp.sum(x * x, axis=-1, keepdims=True)) * x.shape[-1] ** (-0.5)
            return x / jnp.maximum(norm, RMS_EPS) * gamma
        key = jax.random.key(seed)
        ks = jax.random.split(key, 12)
        b, n, m = (4, 1024, 128)
        x = jax.random.normal(ks[0], (b, n, DIM_IN), jnp.float32)
        latents = jax.random.normal(ks[1], (b, m, DIM_LAT), jnp.float32)
        mask = jax.random.randint(ks[2], (b, n), 0, 2).astype(bool)
        s = lambda k, sh, fan: jax.random.normal(k, sh, jnp.float32) * fan ** (-0.5)
        return {'x': x, 'latents': latents, 'mask': mask, 'ln_x_g': jnp.ones((DIM_IN,), jnp.float32), 'ln_x_b': jnp.zeros((DIM_IN,), jnp.float32), 'ln_l_g': jnp.ones((DIM_LAT,), jnp.float32), 'ln_l_b': jnp.zeros((DIM_LAT,), jnp.float32), 'qn_g': jnp.ones((DIM_HEAD,), jnp.float32), 'kn_g': jnp.ones((DIM_HEAD,), jnp.float32), 'Wq': s(ks[3], (INNER, DIM_LAT), DIM_LAT), 'Wkv': s(ks[4], (2 * INNER, DIM_IN), DIM_IN), 'Wlkv': s(ks[5], (2 * INNER, DIM_LAT), DIM_LAT), 'Wo': s(ks[6], (DIM_LAT, INNER), INNER), 'bo': jnp.zeros((DIM_LAT,), jnp.float32)}
    _L0_xattn_all = _L0_xattn_setup()
    _L0_xattn_in = {k: v for k, v in _L0_xattn_all.items() if k in ('ln_x_g', 'ln_x_b', 'ln_l_g', 'ln_l_b', 'qn_g', 'kn_g', 'Wq', 'Wkv', 'Wlkv', 'Wo', 'bo')}
    del _L0_xattn_all

    def _L0_ffn_setup():
        import jax, jax.numpy as jnp
        import numpy as np
        NUM_HEADS = 16
        TOP_K = 2
        ROPE_BASE = 10000.0
        LN_EPS = 1e-05

        def _rope_sin_cos(S, D, dtype):
            inv_freq = 1.0 / ROPE_BASE ** (jnp.arange(0, D, 2, dtype=jnp.float32) / D)
            freqs = jnp.arange(S, dtype=jnp.float32)[:, None] * inv_freq[None, :]
            sin = jnp.sin(freqs).astype(dtype)[None, :, None, :]
            cos = jnp.cos(freqs).astype(dtype)[None, :, None, :]
            return (sin, cos)

        def _apply_rope(x, sin, cos):
            x1, x2 = (x[..., 0::2], x[..., 1::2])
            r1 = x1 * cos - x2 * sin
            r2 = x1 * sin + x2 * cos
            return jnp.stack([r1, r2], axis=-1).reshape(x.shape)

        def _layer_norm(x, w, b):
            mu = jnp.mean(x, axis=-1, keepdims=True)
            var = jnp.mean(jnp.square(x - mu), axis=-1, keepdims=True)
            return (x - mu) * jax.lax.rsqrt(var + LN_EPS) * w + b
        key = jax.random.key(seed)
        ks = jax.random.split(key, 8)
        B, S, E, NE = (2, 512, 256, 8)
        s = 0.02
        return {'x': jax.random.normal(ks[0], (B, S, E), dtype=jnp.float32), 'in_proj_w': jax.random.normal(ks[1], (3 * E, E), dtype=jnp.float32) * s, 'in_proj_b': jnp.zeros((3 * E,), dtype=jnp.float32), 'out_proj_w': jax.random.normal(ks[2], (E, E), dtype=jnp.float32) * s, 'out_proj_b': jnp.zeros((E,), dtype=jnp.float32), 'gate_w': jax.random.normal(ks[3], (NE, E), dtype=jnp.float32) * s, 'gate_b': jnp.zeros((NE,), dtype=jnp.float32), 'expert_w': jax.random.normal(ks[4], (NE, E, E), dtype=jnp.float32) * s, 'expert_b': jnp.zeros((NE, E), dtype=jnp.float32), 'ln1_w': jnp.ones((E,), dtype=jnp.float32), 'ln1_b': jnp.zeros((E,), dtype=jnp.float32), 'ln2_w': jnp.ones((E,), dtype=jnp.float32), 'ln2_b': jnp.zeros((E,), dtype=jnp.float32)}
    _L0_ffn_all = _L0_ffn_setup()
    _L0_ffn_in = {k: v for k, v in _L0_ffn_all.items() if k in ('in_proj_w', 'in_proj_b', 'out_proj_w', 'out_proj_b', 'gate_w', 'gate_b', 'expert_w', 'expert_b', 'ln1_w', 'ln1_b', 'ln2_w', 'ln2_b')}
    del _L0_ffn_all

    def _L1_attn_setup():
        import jax, jax.numpy as jnp
        import numpy as np
        B, S, D = (16, 128, 256)
        H, NQ = (16, 8)
        HD = D // H
        key = jax.random.key(seed)
        ks = jax.random.split(key, 8)

        def lin(k, fi, fo):
            return (jax.random.normal(k, (fi, fo), jnp.float32) / np.sqrt(fi)).astype(jnp.float32)
        x = jax.random.normal(ks[0], (B, S, D), jnp.float32)
        wq, wk, wv, wo = (lin(ks[1], D, D), lin(ks[2], D, D), lin(ks[3], D, D), lin(ks[4], D, D))
        bq = jnp.zeros((D,), jnp.float32)
        bk = jnp.zeros((D,), jnp.float32)
        bv = jnp.zeros((D,), jnp.float32)
        bo = jnp.zeros((D,), jnp.float32)
        w1 = lin(ks[5], HD, D)
        b1 = jnp.zeros((D,), jnp.float32)
        w2 = lin(ks[6], D, 2 * NQ)
        b2 = jnp.zeros((2 * NQ,), jnp.float32)
        i = jnp.arange(NQ, dtype=jnp.float32)
        hadamard = jnp.ones((NQ, NQ), jnp.float32) / np.sqrt(NQ) * jnp.cos(2 * np.pi * i / NQ)[:, None]
        rot = jax.random.uniform(ks[7], (H, NQ, 3), jnp.float32, -np.pi, np.pi)
        return dict(x=x, wq=wq, bq=bq, wk=wk, bk=bk, wv=wv, bv=bv, wo=wo, bo=bo, w1=w1, b1=b1, w2=w2, b2=b2, hadamard=hadamard, rot=rot)
    _L1_attn_all = _L1_attn_setup()
    _L1_attn_in = {k: v for k, v in _L1_attn_all.items() if k in ('wq', 'bq', 'wk', 'bk', 'wv', 'bv', 'wo', 'bo', 'w1', 'b1', 'w2', 'b2', 'hadamard', 'rot')}
    del _L1_attn_all

    def _L1_xattn_setup():
        import jax, jax.numpy as jnp
        import numpy as np
        B, T, Q_DIM, KV_DIM = (4, 512, 256, 192)
        HEADS, DIM_HEAD = (16, 64)
        INNER = HEADS * DIM_HEAD
        NUM_FRAMES, NUM_PATCHES = (8, 64)
        LN_EPS = 1e-05

        def diagonal_frame_mask(num_patches, num_frames):
            fid = np.repeat(np.arange(num_frames), num_patches)
            m = fid[:, None] == fid[None, :]
            return jnp.asarray(m[None, None])
        key = jax.random.key(seed)
        ks = jax.random.split(key, 6)
        s = lambda d: 1.0 / np.sqrt(d)
        return {'x': jax.random.normal(ks[0], (B, T, Q_DIM), jnp.float32), 'context': jax.random.normal(ks[1], (B, T, KV_DIM), jnp.float32), 'ln_gamma': jnp.ones((Q_DIM,), jnp.float32), 'ln_beta': jnp.zeros((Q_DIM,), jnp.float32), 'Wq': jax.random.normal(ks[2], (Q_DIM, INNER), jnp.float32) * s(Q_DIM), 'Wkv': jax.random.normal(ks[3], (KV_DIM, 2 * INNER), jnp.float32) * s(KV_DIM), 'Wo': jax.random.normal(ks[4], (INNER, Q_DIM), jnp.float32) * s(INNER), 'bo': jnp.zeros((Q_DIM,), jnp.float32), 'mask': diagonal_frame_mask(NUM_PATCHES, NUM_FRAMES)}
    _L1_xattn_all = _L1_xattn_setup()
    _L1_xattn_in = {k: v for k, v in _L1_xattn_all.items() if k in ('ln_gamma', 'ln_beta', 'Wq', 'Wkv', 'Wo', 'bo')}
    del _L1_xattn_all

    def _L1_ffn_setup():
        import jax, jax.numpy as jnp
        import numpy as np
        D_MODEL = 256
        N_EXPERTS = 8
        TOP_K = 2
        HIDDEN = 4 * D_MODEL
        key = jax.random.key(seed)
        ks = jax.random.split(key, 6)
        B, S = (2, 512)
        x = jax.random.normal(ks[0], (B, S, D_MODEL), dtype=jnp.float32)
        shared_w1 = jax.random.normal(ks[1], (HIDDEN, D_MODEL), dtype=jnp.float32) * 0.02
        shared_w2 = jax.random.normal(ks[2], (D_MODEL, HIDDEN), dtype=jnp.float32) * 0.02
        experts_w1 = jax.random.normal(ks[3], (N_EXPERTS, HIDDEN, D_MODEL), dtype=jnp.float32) * 0.02
        experts_w2 = jax.random.normal(ks[4], (N_EXPERTS, D_MODEL, HIDDEN), dtype=jnp.float32) * 0.02
        gate_w = jax.random.normal(ks[5], (N_EXPERTS, D_MODEL), dtype=jnp.float32) * 0.02
        return {'x': x, 'shared_w1': shared_w1, 'shared_w2': shared_w2, 'experts_w1': experts_w1, 'experts_w2': experts_w2, 'gate_w': gate_w}
    _L1_ffn_all = _L1_ffn_setup()
    _L1_ffn_in = {k: v for k, v in _L1_ffn_all.items() if k in ('shared_w1', 'shared_w2', 'experts_w1', 'experts_w2', 'gate_w')}
    del _L1_ffn_all
    return {'x': x, 'ctx_768': ctx_768, 'mask_BxS2_bk0': mask_BxS2_bk0, 'mask_1x1xSxS2_bk0': mask_1x1xSxS2_bk0, 'L0_attn_w_qkv': _L0_attn_in['w_qkv'], 'L0_attn_w_proj': _L0_attn_in['w_proj'], 'L0_xattn_ln_x_g': _L0_xattn_in['ln_x_g'], 'L0_xattn_ln_x_b': _L0_xattn_in['ln_x_b'], 'L0_xattn_ln_l_g': _L0_xattn_in['ln_l_g'], 'L0_xattn_ln_l_b': _L0_xattn_in['ln_l_b'], 'L0_xattn_qn_g': _L0_xattn_in['qn_g'], 'L0_xattn_kn_g': _L0_xattn_in['kn_g'], 'L0_xattn_Wq': _L0_xattn_in['Wq'], 'L0_xattn_Wkv': _L0_xattn_in['Wkv'], 'L0_xattn_Wlkv': _L0_xattn_in['Wlkv'], 'L0_xattn_Wo': _L0_xattn_in['Wo'], 'L0_xattn_bo': _L0_xattn_in['bo'], 'L0_ffn_in_proj_w': _L0_ffn_in['in_proj_w'], 'L0_ffn_in_proj_b': _L0_ffn_in['in_proj_b'], 'L0_ffn_out_proj_w': _L0_ffn_in['out_proj_w'], 'L0_ffn_out_proj_b': _L0_ffn_in['out_proj_b'], 'L0_ffn_gate_w': _L0_ffn_in['gate_w'], 'L0_ffn_gate_b': _L0_ffn_in['gate_b'], 'L0_ffn_expert_w': _L0_ffn_in['expert_w'], 'L0_ffn_expert_b': _L0_ffn_in['expert_b'], 'L0_ffn_ln1_w': _L0_ffn_in['ln1_w'], 'L0_ffn_ln1_b': _L0_ffn_in['ln1_b'], 'L0_ffn_ln2_w': _L0_ffn_in['ln2_w'], 'L0_ffn_ln2_b': _L0_ffn_in['ln2_b'], 'L1_attn_wq': _L1_attn_in['wq'], 'L1_attn_bq': _L1_attn_in['bq'], 'L1_attn_wk': _L1_attn_in['wk'], 'L1_attn_bk': _L1_attn_in['bk'], 'L1_attn_wv': _L1_attn_in['wv'], 'L1_attn_bv': _L1_attn_in['bv'], 'L1_attn_wo': _L1_attn_in['wo'], 'L1_attn_bo': _L1_attn_in['bo'], 'L1_attn_w1': _L1_attn_in['w1'], 'L1_attn_b1': _L1_attn_in['b1'], 'L1_attn_w2': _L1_attn_in['w2'], 'L1_attn_b2': _L1_attn_in['b2'], 'L1_attn_hadamard': _L1_attn_in['hadamard'], 'L1_attn_rot': _L1_attn_in['rot'], 'L1_xattn_ln_gamma': _L1_xattn_in['ln_gamma'], 'L1_xattn_ln_beta': _L1_xattn_in['ln_beta'], 'L1_xattn_Wq': _L1_xattn_in['Wq'], 'L1_xattn_Wkv': _L1_xattn_in['Wkv'], 'L1_xattn_Wo': _L1_xattn_in['Wo'], 'L1_xattn_bo': _L1_xattn_in['bo'], 'L1_ffn_shared_w1': _L1_ffn_in['shared_w1'], 'L1_ffn_shared_w2': _L1_ffn_in['shared_w2'], 'L1_ffn_experts_w1': _L1_ffn_in['experts_w1'], 'L1_ffn_experts_w2': _L1_ffn_in['experts_w2'], 'L1_ffn_gate_w': _L1_ffn_in['gate_w']}

def reference(x, ctx_768, mask_BxS2_bk0, mask_1x1xSxS2_bk0, L0_attn_w_qkv, L0_attn_w_proj, L0_xattn_ln_x_g, L0_xattn_ln_x_b, L0_xattn_ln_l_g, L0_xattn_ln_l_b, L0_xattn_qn_g, L0_xattn_kn_g, L0_xattn_Wq, L0_xattn_Wkv, L0_xattn_Wlkv, L0_xattn_Wo, L0_xattn_bo, L0_ffn_in_proj_w, L0_ffn_in_proj_b, L0_ffn_out_proj_w, L0_ffn_out_proj_b, L0_ffn_gate_w, L0_ffn_gate_b, L0_ffn_expert_w, L0_ffn_expert_b, L0_ffn_ln1_w, L0_ffn_ln1_b, L0_ffn_ln2_w, L0_ffn_ln2_b, L1_attn_wq, L1_attn_bq, L1_attn_wk, L1_attn_bk, L1_attn_wv, L1_attn_bv, L1_attn_wo, L1_attn_bo, L1_attn_w1, L1_attn_b1, L1_attn_w2, L1_attn_b2, L1_attn_hadamard, L1_attn_rot, L1_xattn_ln_gamma, L1_xattn_ln_beta, L1_xattn_Wq, L1_xattn_Wkv, L1_xattn_Wo, L1_xattn_bo, L1_ffn_shared_w1, L1_ffn_shared_w2, L1_ffn_experts_w1, L1_ffn_experts_w2, L1_ffn_gate_w):
    import jax
    import jax.numpy as jnp

    def _L0_attn_ref(x, w_qkv, w_proj):
        import math
        import jax, jax.numpy as jnp
        import numpy as np
        B, T, D, H = (4, 512, 256, 16)
        HD = D // H
        b, t, d = x.shape
        qkv = x @ w_qkv
        q, k, v = jnp.split(qkv, 3, axis=-1)
        q = q.reshape(b, t, H, HD).transpose(0, 2, 1, 3)
        k = k.reshape(b, t, H, HD).transpose(0, 2, 1, 3)
        v = v.reshape(b, t, H, HD).transpose(0, 2, 1, 3)
        scores = jnp.einsum('bhqd,bhkd->bhqk', q, k) / math.sqrt(HD)
        causal = jnp.tril(jnp.ones((t, t), dtype=bool))
        scores = jnp.where(causal[None, None], scores, jnp.float32(-1000000000.0))
        a = jax.nn.softmax(scores, axis=-1)
        o = jnp.einsum('bhqk,bhkd->bhqd', a, v)
        o = o.transpose(0, 2, 1, 3).reshape(b, t, d)
        return o @ w_proj

    def _L0_xattn_ref(x, latents, mask, ln_x_g, ln_x_b, ln_l_g, ln_l_b, qn_g, kn_g, Wq, Wkv, Wlkv, Wo, bo):
        import jax, jax.numpy as jnp
        import numpy as np
        DIM_IN, DIM_LAT, DIM_HEAD = (192, 256, 64)
        INNER = max(DIM_LAT, DIM_IN)
        HEADS = INNER // DIM_HEAD
        SCALE = DIM_HEAD ** (-0.5)
        RMS_EPS = 1e-08
        LN_EPS = 1e-05

        def layernorm(x, g, b):
            mu = jnp.mean(x, axis=-1, keepdims=True)
            var = jnp.mean((x - mu) ** 2, axis=-1, keepdims=True)
            return (x - mu) * jax.lax.rsqrt(var + LN_EPS) * g + b

        def rmsnorm(x, gamma):
            norm = jnp.sqrt(jnp.sum(x * x, axis=-1, keepdims=True)) * x.shape[-1] ** (-0.5)
            return x / jnp.maximum(norm, RMS_EPS) * gamma
        b, n, _ = x.shape
        m = latents.shape[1]
        xn = layernorm(x, ln_x_g, ln_x_b)
        ln = layernorm(latents, ln_l_g, ln_l_b)
        q = ln @ Wq.T
        kv = jnp.concatenate([xn @ Wkv.T, ln @ Wlkv.T], axis=1)
        k, v = (kv[..., :INNER], kv[..., INNER:])
        split_heads = lambda t: t.reshape(t.shape[0], t.shape[1], HEADS, DIM_HEAD).transpose(0, 2, 1, 3)
        q, k, v = (split_heads(q), split_heads(k), split_heads(v))
        qn = rmsnorm(q, qn_g) * SCALE
        kn = rmsnorm(k, kn_g)
        attn = jnp.einsum('bhid,bhjd->bhij', qn, kn)
        full_mask = jnp.pad(mask, ((0, 0), (0, m)), constant_values=True)
        attn = jnp.where(full_mask[:, None, None, :], attn, -jnp.finfo(attn.dtype).max)
        attn = jax.nn.softmax(attn, axis=-1)
        out = jnp.einsum('bhij,bhjd->bhid', attn, v)
        out = out.transpose(0, 2, 1, 3).reshape(b, m, INNER)
        return out @ Wo.T + bo

    def _L0_ffn_ref(x, in_proj_w, in_proj_b, out_proj_w, out_proj_b, gate_w, gate_b, expert_w, expert_b, ln1_w, ln1_b, ln2_w, ln2_b):
        import jax, jax.numpy as jnp
        import numpy as np
        NUM_HEADS = 16
        TOP_K = 2
        ROPE_BASE = 10000.0
        LN_EPS = 1e-05

        def _rope_sin_cos(S, D, dtype):
            inv_freq = 1.0 / ROPE_BASE ** (jnp.arange(0, D, 2, dtype=jnp.float32) / D)
            freqs = jnp.arange(S, dtype=jnp.float32)[:, None] * inv_freq[None, :]
            sin = jnp.sin(freqs).astype(dtype)[None, :, None, :]
            cos = jnp.cos(freqs).astype(dtype)[None, :, None, :]
            return (sin, cos)

        def _apply_rope(x, sin, cos):
            x1, x2 = (x[..., 0::2], x[..., 1::2])
            r1 = x1 * cos - x2 * sin
            r2 = x1 * sin + x2 * cos
            return jnp.stack([r1, r2], axis=-1).reshape(x.shape)

        def _layer_norm(x, w, b):
            mu = jnp.mean(x, axis=-1, keepdims=True)
            var = jnp.mean(jnp.square(x - mu), axis=-1, keepdims=True)
            return (x - mu) * jax.lax.rsqrt(var + LN_EPS) * w + b
        B, S, E = x.shape
        H = NUM_HEADS
        D = E // H
        xh = x.reshape(B, S, H, D)
        sin, cos = _rope_sin_cos(S, D, x.dtype)
        q_in = _apply_rope(xh, sin, cos).reshape(B, S, E)
        k_in = q_in
        v_in = x
        Wq, Wk, Wv = jnp.split(in_proj_w, 3, axis=0)
        bq, bk, bv = jnp.split(in_proj_b, 3, axis=0)
        q = (q_in @ Wq.T + bq).reshape(B, S, H, D)
        k = (k_in @ Wk.T + bk).reshape(B, S, H, D)
        v = (v_in @ Wv.T + bv).reshape(B, S, H, D)
        scale = 1.0 / jnp.sqrt(jnp.asarray(D, dtype=x.dtype))
        scores = jnp.einsum('bqhd,bkhd->bhqk', q, k) * scale
        causal = jnp.tril(jnp.ones((S, S), dtype=bool))
        scores = jnp.where(causal[None, None], scores, jnp.asarray(-jnp.inf, dtype=scores.dtype))
        attn = jax.nn.softmax(scores, axis=-1)
        ctx = jnp.einsum('bhqk,bkhd->bqhd', attn, v).reshape(B, S, E)
        attn_out = ctx @ out_proj_w.T + out_proj_b
        x1 = _layer_norm(x + attn_out, ln1_w, ln1_b)
        gates = jax.nn.softmax(x1 @ gate_w.T + gate_b, axis=-1)
        _, top_idx = jax.lax.top_k(gates, TOP_K)
        top_gates = jnp.take_along_axis(gates, top_idx, axis=-1)
        expert_outputs = jnp.einsum('bsd,efd->bsef', x1, expert_w) + expert_b[None, None]
        sel = jnp.take_along_axis(expert_outputs, top_idx[..., None], axis=2)
        moe_out = jnp.sum(sel * top_gates[..., None], axis=2)
        return _layer_norm(x1 + moe_out, ln2_w, ln2_b)

    def _L1_attn_ref(x, wq, bq, wk, bk, wv, bv, wo, bo, w1, b1, w2, b2, hadamard, rot):
        import jax, jax.numpy as jnp
        import numpy as np
        B, S, D = (16, 128, 256)
        H, NQ = (16, 8)
        HD = D // H
        Bn, Sn, Dn = x.shape
        Hn = rot.shape[0]
        nq = hadamard.shape[0]
        hd = Dn // Hn
        Q = (x @ wq + bq).reshape(Bn, Sn, Hn, hd)
        K = (x @ wk + bk).reshape(Bn, Sn, Hn, hd)
        V = (x @ wv + bv).reshape(Bn, Sn, Hn, hd)

        def prep(t):
            h1 = jnp.tanh(jnp.einsum('bshd,do->bsho', t, w1) + b1)
            return jnp.einsum('bsho,on->bshn', h1, w2) + b2
        qp, kp = (prep(Q), prep(K))
        qc = (qp[..., :nq] + 1j * qp[..., nq:]).astype(jnp.complex64)
        kc = (kp[..., :nq] + 1j * kp[..., nq:]).astype(jnp.complex64)
        Hc = hadamard.astype(jnp.complex64)
        q1 = jnp.einsum('bshn,nm->bshm', qc, Hc)
        k1 = jnp.einsum('bshn,nm->bshm', kc, Hc)
        cos = jnp.cos(rot[:, :nq // 2, 0] / 2).astype(jnp.complex64)
        sin = jnp.sin(rot[:, :nq // 2, 0] / 2).astype(jnp.complex64)
        R = jnp.zeros((Hn, Bn, Bn), jnp.complex64) + jnp.eye(Bn, dtype=jnp.complex64)
        for i in range(nq // 2):
            a, b = (2 * i, 2 * i + 1)
            R = R.at[:, a, a].set(cos[:, i])
            R = R.at[:, a, b].set(-1j * sin[:, i])
            R = R.at[:, b, a].set(-1j * sin[:, i])
            R = R.at[:, b, b].set(cos[:, i])
        qe = jnp.real(jnp.einsum('hcb,bshn->cshn', R, q1))
        ke = jnp.real(jnp.einsum('hcb,bshn->cshn', R, k1))
        qq = jnp.sum(qe ** 2, -1)
        kk = jnp.sum(ke ** 2, -1)
        s = qq[:, :, None, :] * kk[:, None, :, :]
        attn = jax.nn.softmax(s / s, axis=2)
        out = jnp.einsum('bijh,bjhd->bihd', attn, V).reshape(Bn, Sn, Dn)
        return out @ wo + bo

    def _L1_xattn_ref(x, context, ln_gamma, ln_beta, Wq, Wkv, Wo, bo, mask):
        import jax, jax.numpy as jnp
        import numpy as np
        B, T, Q_DIM, KV_DIM = (4, 512, 256, 192)
        HEADS, DIM_HEAD = (16, 64)
        INNER = HEADS * DIM_HEAD
        NUM_FRAMES, NUM_PATCHES = (8, 64)
        LN_EPS = 1e-05

        def diagonal_frame_mask(num_patches, num_frames):
            fid = np.repeat(np.arange(num_frames), num_patches)
            m = fid[:, None] == fid[None, :]
            return jnp.asarray(m[None, None])
        mu = jnp.mean(x, axis=-1, keepdims=True)
        var = jnp.mean(jnp.square(x - mu), axis=-1, keepdims=True)
        xn = (x - mu) * jax.lax.rsqrt(var + LN_EPS) * ln_gamma + ln_beta
        scale = DIM_HEAD ** (-0.5)
        q = xn @ Wq
        kv = context @ Wkv
        k, v = jnp.split(kv, 2, axis=-1)
        split_heads = lambda t: t.reshape(t.shape[0], t.shape[1], HEADS, DIM_HEAD).transpose(0, 2, 1, 3)
        q, k, v = (split_heads(q), split_heads(k), split_heads(v))
        dots = jnp.einsum('bhnd,bhmd->bhnm', q, k) * scale
        dots = jnp.where(mask, dots, -jnp.inf)
        attn = jax.nn.softmax(dots, axis=-1)
        out = jnp.einsum('bhnm,bhmd->bhnd', attn, v)
        out = out.transpose(0, 2, 1, 3).reshape(x.shape[0], x.shape[1], INNER)
        return out @ Wo + bo

    def _L1_ffn_ref(x, shared_w1, shared_w2, experts_w1, experts_w2, gate_w):
        import jax, jax.numpy as jnp
        import numpy as np
        D_MODEL = 256
        N_EXPERTS = 8
        TOP_K = 2
        HIDDEN = 4 * D_MODEL
        B, S, D = x.shape
        T = B * S
        x_flat = x.reshape(T, D)
        shared = jnp.einsum('td,dh->th', x_flat, shared_w1.T)
        shared = jnp.einsum('th,hd->td', jax.nn.silu(shared), shared_w2.T)
        gate_logits = x_flat @ gate_w.T
        top_k_gates, top_k_idx = jax.lax.top_k(gate_logits, TOP_K)
        top_k_gates = jax.nn.softmax(top_k_gates, axis=1)
        gates = jnp.zeros((T, N_EXPERTS), dtype=x.dtype)
        gates = gates.at[jnp.arange(T)[:, None], top_k_idx].set(top_k_gates)
        h = jnp.einsum('td,ehd->teh', x_flat, experts_w1)
        expert_out = jnp.einsum('teh,edh->ted', jax.nn.silu(h), experts_w2)
        selected = jnp.einsum('ted,te->td', expert_out, gates)
        return (shared + selected).reshape(B, S, D)
    x = x + _L0_attn_ref(_layernorm(x, axis=-1), L0_attn_w_qkv, L0_attn_w_proj)
    x = x + _L0_xattn_ref(ctx_768, _layernorm(x, axis=-1), mask_BxS2_bk0, L0_xattn_ln_x_g, L0_xattn_ln_x_b, L0_xattn_ln_l_g, L0_xattn_ln_l_b, L0_xattn_qn_g, L0_xattn_kn_g, L0_xattn_Wq, L0_xattn_Wkv, L0_xattn_Wlkv, L0_xattn_Wo, L0_xattn_bo)
    x = x + _L0_ffn_ref(_layernorm(x, axis=-1), L0_ffn_in_proj_w, L0_ffn_in_proj_b, L0_ffn_out_proj_w, L0_ffn_out_proj_b, L0_ffn_gate_w, L0_ffn_gate_b, L0_ffn_expert_w, L0_ffn_expert_b, L0_ffn_ln1_w, L0_ffn_ln1_b, L0_ffn_ln2_w, L0_ffn_ln2_b)
    x = x + _L1_attn_ref(_layernorm(x, axis=-1), L1_attn_wq, L1_attn_bq, L1_attn_wk, L1_attn_bk, L1_attn_wv, L1_attn_bv, L1_attn_wo, L1_attn_bo, L1_attn_w1, L1_attn_b1, L1_attn_w2, L1_attn_b2, L1_attn_hadamard, L1_attn_rot)
    x = x + _L1_xattn_ref(_layernorm(x, axis=-1), ctx_768, L1_xattn_ln_gamma, L1_xattn_ln_beta, L1_xattn_Wq, L1_xattn_Wkv, L1_xattn_Wo, L1_xattn_bo, mask_1x1xSxS2_bk0)
    x = x + _L1_ffn_ref(_layernorm(x, axis=-1), L1_ffn_shared_w1, L1_ffn_shared_w2, L1_ffn_experts_w1, L1_ffn_experts_w2, L1_ffn_gate_w)
    return x

_drawn_inputs = setup_inputs


def setup_inputs(seed=0):
    import zlib

    import numpy as np

    out = dict(_drawn_inputs(seed))
    spreads = {'L0_xattn_ln_x_g': (1.0, 0.2),
     'L0_xattn_ln_x_b': (0.0, 0.1),
     'L0_xattn_ln_l_g': (1.0, 0.2),
     'L0_xattn_ln_l_b': (0.0, 0.1),
     'L0_xattn_qn_g': (1.0, 0.584),
     'L0_xattn_kn_g': (1.0, 0.6),
     'L0_xattn_bo': (0.0, 0.1),
     'L0_ffn_in_proj_b': (0.0, 0.423),
     'L0_ffn_out_proj_b': (0.0, 0.1),
     'L0_ffn_gate_b': (0.0, 0.34),
     'L0_ffn_expert_b': (0.0, 0.638),
     'L0_ffn_ln1_w': (1.0, 0.2),
     'L0_ffn_ln1_b': (0.0, 0.1),
     'L0_ffn_ln2_w': (1.0, 0.2),
     'L0_ffn_ln2_b': (0.0, 0.1),
     'L1_attn_bq': (0.0, 0.1),
     'L1_attn_bk': (0.0, 0.1),
     'L1_attn_bv': (0.0, 0.1),
     'L1_attn_bo': (0.0, 0.1),
     'L1_attn_b1': (0.0, 0.1),
     'L1_attn_b2': (0.0, 0.1),
     'L1_xattn_ln_gamma': (1.0, 0.6),
     'L1_xattn_ln_beta': (0.0, 0.641),
     'L1_xattn_bo': (0.0, 0.1)}
    factors = {'L0_ffn_in_proj_w': 2.717}
    for name, (base, spread) in spreads.items():
        noise = np.random.default_rng([zlib.crc32(name.encode()), seed]).standard_normal(out[name].shape)
        drawn = base * np.exp(spread * noise) if base else spread * noise
        out[name] = jnp.asarray(drawn.astype(out[name].dtype))
    for name, factor in factors.items():
        out[name] = (out[name] * factor).astype(out[name].dtype)
    return out
```

```python
from contextlib import ExitStack

import numpy as np

import concourse.bass as bass
from concourse import mybir

ALU = mybir.AluOpType
ACT = mybir.ActivationFunctionType
AX = mybir.AxisListType
F32 = mybir.dt.float32
BF16 = mybir.dt.bfloat16
U8 = mybir.dt.uint8
I32 = mybir.dt.int32

B, S, D = 32, 100, 256
P = 128
DC = D // P
CTX, CD = 361, 192
NH, HD = 16, 16
ROWS = 32
RG = P // ROWS
XH, XD = 4, 64
WH, WD = 16, 64
WI = WH * WD
WM = WI // P
NE = 8
HID = 4 * D
HM = HID // P
LANES = 2
PAIRS = B // LANES
BANK = 512
BANKS = 8 // LANES
MASKED = -1e30
CTX_TILES = [(0, P), (P, P), (2 * P, CTX - 2 * P)]
NT = len(CTX_TILES)
CTX_CHUNKS = [(0, P), (P, CD - P)]
QT = NH // RG


class Fields(dict):

    def __getattr__(self, name):
        return self[name]


def head_at(r, e, c):
    return 2 * RG * c + 2 * r + e


def semaphores(nc, ctx, phase, names):
    return Fields(**{n: ctx.enter_context(nc.semaphore(f"{phase}_{n}")) for n in names.split()})


def buffers(nc, ctx, phase, **shapes):
    return Fields(**{n: ctx.enter_context(nc.sbuf_tensor(f"{phase}_{n}", s, F32)) for n, s in shapes.items()})


def lanes_of(eng, pair):
    return [(lane, eng.snap(pair * LANES + lane), eng.snap(pair * LANES + lane + 1)) for lane in range(LANES)]



def norm_of(nc, ctx, name):
    m = buffers(nc, ctx, name, stats=[S, LANES, 6], meanvar=[S, LANES, 2], vareps=[S, LANES, 1], rstd=[S, LANES, 1], hold=[S, 1])
    m.done = semaphores(nc, ctx, name, "stats meanvar vareps rstd")
    return m


def norm_stats(nc, dve, m, lanes, rows):
    for lane, b, n in lanes:
        nc.vector.bn_stats(m.stats[:, lane, :], rows(lane, b)).then_inc(m.done.stats, 1)
    dve.wait_ge(m.done.stats, lanes[-1][2])
    nc.vector.memset(m.hold[:, :], 0.0)
    for lane, b, n in lanes:
        nc.vector.bn_aggr(m.meanvar[:, lane, :], m.stats[:, lane, :]).then_inc(m.done.meanvar, 1)


def norm_root(nc, pool, g, m, lane, n):
    pool.wait_ge(m.done.meanvar, n)
    nc.gpsimd.tensor_tensor(m.vareps[:, lane, :], m.meanvar[:, lane, 1:2], g.eps[0:S, :], ALU.add).then_inc(m.done.vareps, 1)
    pool.wait_ge(m.done.vareps, n)
    nc.gpsimd.tensor_tensor(m.rstd[:, lane, :], m.vareps[:, lane, :], g.neg_half[0:S, 0:1], ALU.pow).then_inc(m.done.rstd, 1)


def norm_apply(nc, dve, m, lane, n, out, rows, done):
    dve.wait_ge(m.done.rstd, n)
    nc.vector.tensor_scalar(out, rows, m.meanvar[:, lane, 0:1], m.rstd[:, lane, :], ALU.subtract, ALU.mult).then_inc(done, 1)


def turn(nc, g, out, rows, chunks):
    for c in range(chunks):
        last = nc.tensor.transpose(out[:, c * S:(c + 1) * S], rows[:, c * P:(c + 1) * P], g.ident[0:S, 0:S])
    return last



def causal_phase(nc, g, w, mixture):
    name = "mix" if mixture else "self"
    with ExitStack() as ctx:
        s = semaphores(nc, ctx, name, "y yT_ready yT qkv_ready q kv scores_ready rowmax shifted probs turned_ready "
                       "probsT_act probsT_dve heads_ready rowsum heads headsT_ready headsT proj_ready ones")
        t = buffers(nc, ctx, name, y=[S, LANES, D], yT=[P, LANES, 2 * DC, S], q=[P, LANES, 2, DC, S], k=[P, LANES, DC, S],
                    v=[S, LANES, NH, HD + 1], rowmax=[S, LANES, NH], probs=[S, LANES, RG, QT * S],
                    probsT=[S, LANES, RG, QT * S], rowsum=[S, LANES, NH], heads=[S, LANES, D], headsT=[P, LANES, DC, S])
        m1 = norm_of(nc, ctx, name + "_ln")
        if mixture:
            z = semaphores(nc, ctx, name, "rope_parts rope after x1_scaled x1 x1T_ready x1T gates_ready gmax gexp gsum grec gates "
                           "cmp ties behind rank coef coefT_ready coefT experts_ready last_ready normed moe_rows out_scaled out_shifted out")
            z.added = [ctx.enter_context(nc.semaphore(f"{name}_added{e}")) for e in range(NE)]
            u = buffers(nc, ctx, name + "_m", rope=[S, LANES, D], rope_a=[S, LANES, D], rope_b=[S, LANES, D], after=[S, LANES, D],
                        x1=[S, LANES, D], x1T=[P, LANES, DC, S], gmax=[S, LANES, 1], gexp=[S, LANES, NE], gsum=[S, LANES, 1],
                        grec=[S, LANES, 1], gates=[S, LANES, NE], above=[S, LANES, NE, NE], equal=[S, LANES, NE, NE],
                        rank=[S, LANES, NE], coef=[S, LANES, NE], coefT=[NE, LANES, S], sum=[S, LANES, D])
            m2, m3 = norm_of(nc, ctx, name + "_ln1"), norm_of(nc, ctx, name + "_ln2")
        bank = lambda lane, k: g.psum[:, lane * BANKS + k, :]
        banks = lambda lane, a, b: g.psum[:, lane * BANKS + a:lane * BANKS + b, :]
        block = ctx.enter_context(nc.Block())

        @block.sync
        def _(sp):
            if not mixture:
                for sem, dst, src in g.loads:
                    sp.dma_start(dst, src).then_inc(sem, 16)

        @block.gpsimd
        def _(pool):
            if not mixture:
                nc.gpsimd.memset(g.eps[:, :], 1e-5).then_inc(g.loaded.filled, 1)
                nc.gpsimd.memset(g.neg_half[:, :], -0.5).then_inc(g.loaded.filled, 1)
            pool.wait_ge(g.loaded.filled, 2)
            nc.gpsimd.memset(t.v[:, :, :, HD:HD + 1], 1.0).then_inc(s.ones, 1)
            if mixture:
                pool.wait_ge(g.loaded.mix, g.total.mix)
            with pool.Fori(0, PAIRS) as pair:
                lanes = lanes_of(pool, pair)
                for lane, b, n in lanes:
                    norm_root(nc, pool, g, m1, lane, n)
                if mixture:
                    for lane, b, n in lanes:
                        pool.wait_ge(s.y, n)
                        y2 = t.y[:, lane, :].rearrange("s (f two) -> s f two", two=2)
                        b2 = u.rope_b[:, lane, :].rearrange("s (f two) -> s f two", two=2)
                        sin2 = w.sin[:, :].rearrange("s (f two) -> s f two", two=2)
                        nc.gpsimd.tensor_tensor(u.rope_a[:, lane, :], t.y[:, lane, :], w.cos[:, :], ALU.mult)
                        nc.gpsimd.tensor_tensor(b2[:, :, 0], y2[:, :, 1], sin2[:, :, 0], ALU.mult)
                        nc.gpsimd.tensor_tensor(b2[:, :, 1], y2[:, :, 0], sin2[:, :, 1], ALU.mult).then_inc(z.rope_parts, 1)
                    for lane, b, n in lanes:
                        pool.wait_ge(z.rope_parts, n)
                        nc.gpsimd.tensor_tensor(u.rope[:, lane, :], u.rope_a[:, lane, :], u.rope_b[:, lane, :], ALU.add).then_inc(z.rope, 1)
                    for lane, b, n in lanes:
                        norm_root(nc, pool, g, m2, lane, n)
                    for lane, b, n in lanes:
                        pool.wait_ge(z.normed, n)
                        nc.gpsimd.tensor_tensor(u.after[:, lane, :], u.after[:, lane, :], w.ln1_w[:, :], ALU.mult).then_inc(z.x1_scaled, 1)
                    for lane, b, n in lanes:
                        pool.wait_ge(z.x1_scaled, n)
                        nc.gpsimd.tensor_tensor(u.x1[:, lane, :], u.after[:, lane, :], w.ln1_b[:, :], ALU.add).then_inc(z.x1, 1)
                    for lane, b, n in lanes:
                        norm_root(nc, pool, g, m3, lane, n)
                    for lane, b, n in lanes:
                        pool.wait_ge(z.out, n)
                        nc.gpsimd.tensor_tensor(u.sum[:, lane, :], u.sum[:, lane, :], w.ln2_w[:, :], ALU.mult).then_inc(z.out_scaled, 1)
                    for lane, b, n in lanes:
                        pool.wait_ge(z.out_scaled, n)
                        nc.gpsimd.tensor_tensor(u.sum[:, lane, :], u.sum[:, lane, :], w.ln2_b[:, :], ALU.add).then_inc(z.out_shifted, 1)
                    for lane, b, n in lanes:
                        pool.wait_ge(z.out_shifted, n)
                        nc.gpsimd.tensor_tensor(g.x[:, b, :], g.x[:, b, :], u.sum[:, lane, :], ALU.add)

        @block.tensor
        def _(pe):
            pe.wait_ge(g.loaded.first, g.total.first)
            pe.wait_ge(s.ones, 1)
            if mixture:
                pe.wait_ge(g.loaded.mix, g.total.mix)
            src = DC if mixture else 0
            with pe.Fori(0, PAIRS) as pair:
                lanes = lanes_of(pe, pair)
                for lane, b, n in lanes:
                    pe.wait_ge(s.y, n)
                    last = turn(nc, g, bank(lane, 0), t.y[:, lane, :], DC)
                    if mixture:
                        pe.wait_ge(z.rope, n)
                        last = turn(nc, g, bank(lane, 0)[:, DC * S:], u.rope[:, lane, :], DC)
                    last.then_inc(s.yT_ready, 1)
                for lane, b, n in lanes:
                    pe.wait_ge(s.yT, n)
                    for m in range(2 * DC):
                        for c in range(DC):
                            nc.tensor.matmul(bank(lane, 1 if m < DC else 3)[:, m % DC * S:(m % DC + 1) * S], w.qkv[:, c, m * P:(m + 1) * P],
                                             t.yT[:, lane, src + c, :], start=(c == 0), stop=(c == DC - 1))
                    for c in range(DC):
                        last = nc.tensor.matmul(bank(lane, 2)[0:S, 0:D], t.yT[:, lane, c, :], w.qkv[:, c, 2 * D:3 * D],
                                                start=(c == 0), stop=(c == DC - 1))
                    last.then_inc(s.qkv_ready, 1)
                for lane, b, n in lanes:
                    pe.wait_ge(s.q, n)
                    pe.wait_ge(s.kv, n)
                    for r in range(RG):
                        nc.tensor.matmul(bank(lane, r)[0:S, 0:QT * S], g.ident_b[0:S, 0:S], g.causal[:, :], start=True, stop=False)
                    for e in range(2):
                        for c in range(DC):
                            for r in range(RG):
                                rows, at = slice(ROWS * r, ROWS * (r + 1)), (e * DC + c) * S
                                last = nc.tensor.matmul(bank(lane, r)[0:S, at:at + S], t.q[rows, lane, e, c, :], t.k[rows, lane, c, :],
                                                        start=False, stop=(e == 1 and c == DC - 1))
                    last.then_inc(s.scores_ready, 1)
                for lane, b, n in lanes:
                    pe.wait_ge(s.probs, n)
                    for r in range(RG):
                        for j in range(QT):
                            last = nc.tensor.transpose(bank(lane, r)[0:S, j * S:(j + 1) * S], t.probs[:, lane, r, j * S:(j + 1) * S],
                                                       g.ident[0:S, 0:S])
                    last.then_inc(s.turned_ready, 1)
                for lane, b, n in lanes:
                    pe.wait_ge(s.probsT_act, n)
                    pe.wait_ge(s.probsT_dve, n)
                    for r in range(RG):
                        for e in range(2):
                            for c in range(DC):
                                h, at = head_at(r, e, c), (e * DC + c) * S
                                last = nc.tensor.matmul(bank(lane, 0)[0:S, h * (HD + 1):(h + 1) * (HD + 1)],
                                                        t.probsT[:, lane, r, at:at + S], t.v[:, lane, h, :], start=True, stop=True)
                    last.then_inc(s.heads_ready, 1)
                for lane, b, n in lanes:
                    pe.wait_ge(s.heads, n)
                    turn(nc, g, bank(lane, 1), t.heads[:, lane, :], DC).then_inc(s.headsT_ready, 1)
                for lane, b, n in lanes:
                    pe.wait_ge(s.headsT, n)
                    for c in range(DC):
                        last = nc.tensor.matmul(bank(lane, 2)[0:S, 0:D], t.headsT[:, lane, c, :], w.proj[:, c, :],
                                                start=(c == 0), stop=(not mixture and c == DC - 1))
                    if mixture:
                        last = nc.tensor.matmul(bank(lane, 2)[0:S, 0:D], g.ones[0:1, 0:S], w.proj_b[:, :], start=False, stop=True)
                    last.then_inc(s.proj_ready, 1)
                if mixture:
                    for lane, b, n in lanes:
                        pe.wait_ge(z.x1, n)
                        turn(nc, g, bank(lane, 3), u.x1[:, lane, :], DC).then_inc(z.x1T_ready, 1)
                    for lane, b, n in lanes:
                        pe.wait_ge(z.x1T, n)
                        for c in range(DC):
                            nc.tensor.matmul(bank(lane, 1)[0:S, 0:NE], u.x1T[:, lane, c, :], w.gate[:, c, :], start=(c == 0), stop=False)
                        nc.tensor.matmul(bank(lane, 1)[0:S, 0:NE], g.ones[0:1, 0:S], w.gate_b[:, :], start=False, stop=True).then_inc(z.gates_ready, 1)
                    for lane, b, n in lanes:
                        pe.wait_ge(z.coef, n)
                        nc.tensor.transpose(bank(lane, 3)[0:NE, 0:S], u.coef[:, lane, :], g.ident[0:S, 0:S]).then_inc(z.coefT_ready, 1)
                    for lane, b, n in lanes:
                        pe.wait_ge(z.coefT, n)
                        for k in range(3):
                            for c in range(DC):
                                nc.tensor.matmul(bank(lane, k)[0:S, :], u.x1T[:, lane, c, :], w.expert[:, c, k * BANK:(k + 1) * BANK],
                                                 start=(c == 0), stop=(c == DC - 1))
                        nc.tensor.matmul(bank(lane, 3)[0:S, 0:D], u.coefT[:, lane, :], w.expert_b[:, :], start=True, stop=True).then_inc(z.experts_ready, 1)
                    for lane, b, n in lanes:
                        pe.wait_ge(z.added[1], n)
                        for c in range(DC):
                            last = nc.tensor.matmul(bank(lane, 0)[0:S, :], u.x1T[:, lane, c, :], w.expert[:, c, 3 * BANK:4 * BANK],
                                                    start=(c == 0), stop=(c == DC - 1))
                        last.then_inc(z.last_ready, 1)

        @block.scalar
        def _(act):
            act.wait_ge(g.loaded.first, g.total.first)
            if mixture:
                act.wait_ge(g.loaded.mix, g.total.mix)
            with act.Fori(0, PAIRS) as pair:
                lanes = lanes_of(act, pair)
                for lane, b, n in lanes:
                    act.wait_ge(s.yT_ready, n)
                    k = 2 * DC if mixture else DC
                    nc.scalar.copy(t.yT[:, lane, 0:k, :], bank(lane, 0)[:, 0:k * S].rearrange("p (c s) -> p c s", s=S)).then_inc(s.yT, 1)
                for lane, b, n in lanes:
                    act.wait_ge(s.qkv_ready, n)
                    kk = bank(lane, 3)[:, 0:DC * S]
                    if mixture:
                        for c in range(DC):
                            nc.scalar.activation(t.k[:, lane, c, :], kk[:, c * S:(c + 1) * S], ACT.Identity, bias=w.in_b[:, DC + c:DC + c + 1])
                    else:
                        nc.scalar.copy(t.k[:, lane, :, :], kk.rearrange("p (c s) -> p c s", s=S))
                    nc.scalar.copy(t.v[:, lane, :, 0:HD], bank(lane, 2)[0:S, 0:D].rearrange("s (h d) -> s h d", d=HD)).then_inc(s.kv, 1)
                for lane, b, n in lanes:
                    act.wait_ge(s.shifted, n)
                    nc.scalar.activation(t.probs[:, lane, :, :], t.probs[:, lane, :, :], ACT.Exp).then_inc(s.probs, 1)
                for lane, b, n in lanes:
                    act.wait_ge(s.turned_ready, n)
                    nc.scalar.copy(t.probsT[:, lane, 0:2, :], banks(lane, 0, 2)[0:S, :, 0:QT * S]).then_inc(s.probsT_act, 1)
                for lane, b, n in lanes:
                    act.wait_ge(s.headsT_ready, n)
                    if mixture:
                        for c in range(DC):
                            last = nc.scalar.activation(t.headsT[:, lane, c, :], bank(lane, 1)[:, c * S:(c + 1) * S], ACT.Identity,
                                                        bias=w.in_b[:, 2 * DC + c:2 * DC + c + 1])
                    else:
                        last = nc.scalar.copy(t.headsT[:, lane, :, :], bank(lane, 1)[:, 0:DC * S].rearrange("p (c s) -> p c s", s=S))
                    last.then_inc(s.headsT, 1)
                if mixture:
                    for lane, b, n in lanes:
                        act.wait_ge(z.x1T_ready, n)
                        nc.scalar.copy(u.x1T[:, lane, :, :], bank(lane, 3)[:, 0:DC * S].rearrange("p (c s) -> p c s", s=S)).then_inc(z.x1T, 1)
                    for lane, b, n in lanes:
                        act.wait_ge(z.gmax, n)
                        nc.scalar.activation(u.gexp[:, lane, :], bank(lane, 1)[0:S, 0:NE], ACT.Exp, bias=u.gmax[:, lane, :]).then_inc(z.gexp, 1)
                    for lane, b, n in lanes:
                        act.wait_ge(z.coefT_ready, n)
                        nc.scalar.copy(u.coefT[:, lane, :], bank(lane, 3)[0:NE, 0:S]).then_inc(z.coefT, 1)

        @block.vector
        def _(dve):
            dve.wait_ge(g.loaded.first, g.total.first)
            if mixture:
                dve.wait_ge(g.loaded.mix, g.total.mix)
            with dve.Fori(0, PAIRS) as pair:
                lanes = lanes_of(dve, pair)
                norm_stats(nc, dve, m1, lanes, lambda lane, b: g.x[:, b, :])
                for lane, b, n in lanes:
                    norm_apply(nc, dve, m1, lane, n, t.y[:, lane, :], g.x[:, b, :], s.y)
                for lane, b, n in lanes:
                    dve.wait_ge(s.qkv_ready, n)
                    for e in range(2):
                        if mixture:
                            for c in range(DC):
                                last = nc.vector.tensor_scalar(t.q[:, lane, e, c, :], bank(lane, 1)[:, c * S:(c + 1) * S], w.in_b[:, c:c + 1],
                                                               g.half_scaled[:, e:e + 1], ALU.add, ALU.mult)
                        else:
                            last = nc.vector.tensor_scalar(t.q[:, lane, e, :, :], bank(lane, 1)[:, 0:DC * S].rearrange("p (c s) -> p c s", s=S),
                                                           g.half_scaled[:, e:e + 1], None, ALU.mult)
                    last.then_inc(s.q, 1)
                for lane, b, n in lanes:
                    dve.wait_ge(s.scores_ready, n)
                    sc = banks(lane, 0, RG)[0:S, :, 0:QT * S].rearrange("s r (j k) -> s r j k", k=S)
                    nc.vector.reduce_max(t.rowmax[:, lane, :].rearrange("s (r j) -> s r j", j=QT), sc, AX.X).then_inc(s.rowmax, 1)
                for lane, b, n in lanes:
                    dve.wait_ge(s.rowmax, n)
                    for r in range(RG):
                        last = nc.vector.tensor_tensor(t.probs[:, lane, r, :].rearrange("s (j k) -> s j k", k=S),
                                                       bank(lane, r)[0:S, 0:QT * S].rearrange("s (j k) -> s j k", k=S),
                                                       t.rowmax[:, lane, r * QT:(r + 1) * QT].unsqueeze(2).broadcast_to([S, QT, S]), ALU.subtract)
                    last.then_inc(s.shifted, 1)
                for lane, b, n in lanes:
                    dve.wait_ge(s.turned_ready, n)
                    nc.vector.tensor_copy(t.probsT[:, lane, 2:4, :], banks(lane, 2, 4)[0:S, :, 0:QT * S]).then_inc(s.probsT_dve, 1)
                for lane, b, n in lanes:
                    dve.wait_ge(s.heads_ready, n)
                    o = bank(lane, 0)[0:S, 0:NH * (HD + 1)].rearrange("s (h d) -> s h d", d=HD + 1)
                    nc.vector.reciprocal(t.rowsum[:, lane, :].unsqueeze(2), o[:, :, HD:HD + 1]).then_inc(s.rowsum, 1)
                for lane, b, n in lanes:
                    dve.wait_ge(s.rowsum, n)
                    o = bank(lane, 0)[0:S, 0:NH * (HD + 1)].rearrange("s (h d) -> s h d", d=HD + 1)
                    nc.vector.tensor_tensor(t.heads[:, lane, :].rearrange("s (h d) -> s h d", d=HD), o[:, :, 0:HD],
                                            t.rowsum[:, lane, :].unsqueeze(2).broadcast_to([S, NH, HD]), ALU.mult).then_inc(s.heads, 1)
                if not mixture:
                    for lane, b, n in lanes:
                        dve.wait_ge(s.proj_ready, n)
                        nc.vector.tensor_tensor(g.x[:, b, :], g.x[:, b, :], bank(lane, 2)[0:S, 0:D], ALU.add)
                else:
                    for lane, b, n in lanes:
                        dve.wait_ge(s.proj_ready, n)
                        nc.vector.tensor_tensor(u.after[:, lane, :], t.y[:, lane, :], bank(lane, 2)[0:S, 0:D], ALU.add).then_inc(z.after, 1)
                    dve.wait_ge(z.after, lanes[-1][2])
                    norm_stats(nc, dve, m2, lanes, lambda lane, b: u.after[:, lane, :])
                    for lane, b, n in lanes:
                        norm_apply(nc, dve, m2, lane, n, u.after[:, lane, :], u.after[:, lane, :], z.normed)
                    for lane, b, n in lanes:
                        dve.wait_ge(z.gates_ready, n)
                        nc.vector.reduce_max(u.gmax[:, lane, :], bank(lane, 1)[0:S, 0:NE], AX.X, negate=True).then_inc(z.gmax, 1)
                    for lane, b, n in lanes:
                        dve.wait_ge(z.gexp, n)
                        nc.vector.reduce_sum(u.gsum[:, lane, :], u.gexp[:, lane, :], AX.X).then_inc(z.gsum, 1)
                    for lane, b, n in lanes:
                        dve.wait_ge(z.gsum, n)
                        nc.vector.reciprocal(u.grec[:, lane, :], u.gsum[:, lane, :]).then_inc(z.grec, 1)
                    for lane, b, n in lanes:
                        dve.wait_ge(z.grec, n)
                        nc.vector.tensor_scalar(u.gates[:, lane, :], u.gexp[:, lane, :], u.grec[:, lane, :], None, ALU.mult).then_inc(z.gates, 1)
                    top_two(nc, dve, g, lanes, u, z, u.gates)
                    for lane, b, n in lanes:
                        dve.wait_ge(z.rank, n)
                        nc.vector.scalar_tensor_tensor(u.coef[:, lane, :], u.rank[:, lane, :], 2.0, u.gates[:, lane, :],
                                                       ALU.is_lt, ALU.mult).then_inc(z.coef, 1)
                    for e in range(NE):
                        for lane, b, n in lanes:
                            if e == 0:
                                dve.wait_ge(z.experts_ready, n)
                            elif e == NE - 2:
                                dve.wait_ge(z.last_ready, n)
                            if e > 0:
                                dve.wait_ge(z.added[e - 1], n)
                            k = e // 2 % 3
                            nc.vector.scalar_tensor_tensor(u.sum[:, lane, :], bank(lane, k)[0:S, e % 2 * D:(e % 2 + 1) * D], u.coef[:, lane, e:e + 1],
                                                           (u.sum if e else u.x1)[:, lane, :], ALU.mult, ALU.add).then_inc(z.added[e], 1)
                    for lane, b, n in lanes:
                        dve.wait_ge(z.added[NE - 1], n)
                        nc.vector.tensor_tensor(u.sum[:, lane, :], u.sum[:, lane, :], bank(lane, 3)[0:S, 0:D], ALU.add).then_inc(z.moe_rows, 1)
                    dve.wait_ge(z.moe_rows, lanes[-1][2])
                    norm_stats(nc, dve, m3, lanes, lambda lane, b: u.sum[:, lane, :])
                    for lane, b, n in lanes:
                        norm_apply(nc, dve, m3, lane, n, u.sum[:, lane, :], u.sum[:, lane, :], z.out)


def top_two(nc, dve, g, lanes, u, z, gates):
    for lane, b, n in lanes:
        dve.wait_ge(z.gates, n)
        mine = gates[:, lane, :].unsqueeze(2).broadcast_to([S, NE, NE])
        other = gates[:, lane, :].unsqueeze(1).broadcast_to([S, NE, NE])
        nc.vector.tensor_tensor(u.above[:, lane, :, :], other, mine, ALU.is_gt)
        nc.vector.tensor_tensor(u.equal[:, lane, :, :], other, mine, ALU.is_equal).then_inc(z.cmp, 1)
    for lane, b, n in lanes:
        dve.wait_ge(z.cmp, n)
        nc.vector.tensor_tensor(u.equal[:, lane, :, :], u.equal[:, lane, :, :], g.before[:, :, :], ALU.mult).then_inc(z.ties, 1)
    for lane, b, n in lanes:
        dve.wait_ge(z.ties, n)
        nc.vector.tensor_tensor(u.above[:, lane, :, :], u.above[:, lane, :, :], u.equal[:, lane, :, :], ALU.add).then_inc(z.behind, 1)
    for lane, b, n in lanes:
        dve.wait_ge(z.behind, n)
        nc.vector.reduce_sum(u.rank[:, lane, :], u.above[:, lane, :, :], AX.X).then_inc(z.rank, 1)



def normed_cross_phase(nc, g, w, ctx_in):
    KT = NT + 1
    KEYS = NT * P + S
    PAD = (CTX, NT * P)
    width = [P] * NT + [S]
    with ExitStack() as ctx:
        s = semaphores(nc, ctx, "cross", "zeroed ones bias gain y yy yT_ready lT cstats cmeanvar cvareps crstd cn ctxT_ready ctxT_act ctxT_dve "
                       "q_ready qsq qsum qclip qroot qn kv_ready kv_act ksum kclip kroot kn kqT_ready kT qT pick scores_ready rowmax "
                       "probs turned_ready probsT_act probsT_dve heads_ready rowsum heads headsT_ready headsT proj_ready")
        raw_loaded = [ctx.enter_context(nc.semaphore(f"cross_ctx_loaded{lane}")) for lane in range(LANES)]
        t = buffers(nc, ctx, "cross", y=[S, LANES, D], yy=[S, LANES, D], lT=[P, LANES, DC, P], raw=[P, LANES, NT, CD], cn=[P, LANES, NT, CD],
                    cstats=[P, LANES, NT, 6], cmeanvar=[P, LANES, NT, 2], cvareps=[P, LANES, NT], crstd=[P, LANES, NT], chold=[P, 1],
                    ctxT0=[P, LANES, NT * P], ctxT1=[CD - P, LANES, NT * P], qsq=[S, LANES, D], qsum=[S, LANES, XH], qclip=[S, LANES, XH],
                    qroot=[S, LANES, XH], ksum=[P, LANES, KT * XH], kclip=[P, LANES, KT * XH],
                    kroot=[P, LANES, KT * XH], v=[P, LANES, KT, XH, XD + 1], kT=[P, LANES, DC, KT * P], qT=[P, LANES, DC, S],
                    rowmax=[S, LANES, XH], probs=[P, LANES, XH, KEYS], probsT=[P, LANES, KT, XH * S], rowsum=[S, LANES, XH],
                    gain=[P, 1])
        t.kn = t.probs[:, :, :, :].rearrange("p l h k -> p l (h k)")[:, :, 0:KT * D].rearrange("p l (t d) -> p l t d", d=D)
        t.ksq, t.qn = t.kn, t.qsq
        t.heads, t.headsT = t.y, t.qT
        bias = ctx.enter_context(nc.sbuf_tensor("cross_bias", [B, KEYS], BF16))
        pick = ctx.enter_context(nc.sbuf_tensor("cross_pick", [B, LANES, S], BF16))
        m1, m2 = norm_of(nc, ctx, "cross_ln"), norm_of(nc, ctx, "cross_ln_l")
        bank = lambda lane, k: g.psum[:, lane * BANKS + k, :]
        banks = lambda lane, a, b: g.psum[:, lane * BANKS + a:lane * BANKS + b, :]
        block = ctx.enter_context(nc.Block())

        def load_ctx(sp, lane, b):
            whole = (NT - 1) * P
            sp.dma_start(t.raw[:, lane, 0:NT - 1, :], ctx_in[b, 0:whole, :].rearrange("(t p) d -> p t d", p=P)).then_inc(raw_loaded[lane], 16)
            sp.dma_start(t.raw[0:CTX - whole, lane, NT - 1, :], ctx_in[b, whole:CTX, :]).then_inc(raw_loaded[lane], 16)

        @block.sync
        def _(sp):
            sp.wait_ge(s.zeroed, 1)
            for lane in range(LANES):
                load_ctx(sp, lane, lane)
            with sp.Fori(1, PAIRS) as pair:
                for lane, b, n in lanes_of(sp, pair):
                    sp.wait_ge(s.cn, sp.snap(b - 1))
                    load_ctx(sp, lane, b)

        @block.gpsimd
        def _(pool):
            nc.gpsimd.memset(t.raw[:, :, NT - 1, :], 0.0).then_inc(s.zeroed, 1)
            nc.gpsimd.memset(t.lT[:, :, :, :], 0.0).then_inc(s.ones, 1)
            nc.gpsimd.memset(t.v[:, :, :, :, XD:XD + 1], 1.0).then_inc(s.ones, 1)
            nc.gpsimd.memset(bias[:, :], MASKED).then_inc(s.ones, 1)
            with pool.Fori(0, PAIRS) as pair:
                lanes = lanes_of(pool, pair)
                for lane, b, n in lanes:
                    norm_root(nc, pool, g, m1, lane, n)
                for lane, b, n in lanes:
                    nc.gpsimd.tensor_copy(pick[:, lane, :], g.ident_b[0:B, b].unsqueeze(1).broadcast_to([B, S])).then_inc(s.pick, 1)
                for lane, b, n in lanes:
                    norm_root(nc, pool, g, m2, lane, n)
                for lane, b, n in lanes:
                    pool.wait_ge(s.cmeanvar, n)
                    nc.gpsimd.tensor_tensor(t.cvareps[:, lane, :], t.cmeanvar[:, lane, :, 1], g.eps[:, :].broadcast_to([P, NT]), ALU.add).then_inc(s.cvareps, 1)
                for lane, b, n in lanes:
                    pool.wait_ge(s.cvareps, n)
                    nc.gpsimd.tensor_tensor(t.crstd[:, lane, :], t.cvareps[:, lane, :], g.neg_half[:, 0:NT], ALU.pow).then_inc(s.crstd, 1)
                for lane, b, n in lanes:
                    pool.wait_ge(s.qclip, n)
                    nc.gpsimd.tensor_tensor(t.qroot[:, lane, :], t.qclip[:, lane, :], g.neg_half[0:S, 0:XH], ALU.pow).then_inc(s.qroot, 1)
                for lane, b, n in lanes:
                    pool.wait_ge(s.kclip, n)
                    nc.gpsimd.tensor_tensor(t.kroot[:, lane, :], t.kclip[:, lane, :], g.neg_half[:, 0:KT * XH], ALU.pow).then_inc(s.kroot, 1)

        @block.tensor
        def _(pe):
            pe.wait_ge(g.loaded.cross, g.total.cross)
            pe.wait_ge(s.ones, 3)
            pe.wait_ge(s.bias, 2)
            with pe.Fori(0, PAIRS) as pair:
                lanes = lanes_of(pe, pair)
                for lane, b, n in lanes:
                    pe.wait_ge(s.yy, n)
                    turn(nc, g, bank(lane, 0), t.yy[:, lane, :], DC).then_inc(s.yT_ready, 1)
                for lane, b, n in lanes:
                    pe.wait_ge(s.lT, n)
                    for c in range(DC):
                        last = nc.tensor.matmul(bank(lane, 3)[0:S, 0:D], t.lT[:, lane, c, 0:S], w.q[:, c, :], start=(c == 0), stop=(c == DC - 1))
                    last.then_inc(s.q_ready, 1)
                for lane, b, n in lanes:
                    pe.wait_ge(s.cn, n)
                    for k, (c0, cw) in enumerate(CTX_CHUNKS):
                        for j in range(NT):
                            last = nc.tensor.transpose(bank(lane, 1 + k)[0:cw, j * P:(j + 1) * P], t.cn[:, lane, j, c0:c0 + cw], g.ident[:, :])
                    last.then_inc(s.ctxT_ready, 1)
                for lane, b, n in lanes:
                    pe.wait_ge(s.ctxT_act, n)
                    pe.wait_ge(s.ctxT_dve, n)
                    pe.wait_ge(s.qn, n)
                    for j in range(NT):
                        nc.tensor.matmul(bank(lane, j), t.ctxT0[:, lane, j * P:(j + 1) * P], w.kv0[:, :], start=True, stop=False)
                        nc.tensor.matmul(bank(lane, j), t.ctxT1[:, lane, j * P:(j + 1) * P], w.kv1[:, :], start=False, stop=True)
                    for c in range(DC):
                        last = nc.tensor.matmul(bank(lane, NT), t.lT[:, lane, c, :], w.lkv[:, c, :], start=(c == 0), stop=(c == DC - 1))
                    last.then_inc(s.kv_ready, 1)
                for lane, b, n in lanes:
                    pe.wait_ge(s.kn, n)
                    for c in range(DC):
                        for j in range(KT):
                            nc.tensor.transpose(bank(lane, c)[:, j * P:(j + 1) * P], t.kn[:, lane, j, c * P:(c + 1) * P], g.ident[:, :])
                    turn(nc, g, bank(lane, 2), t.qn[:, lane, :], DC).then_inc(s.kqT_ready, 1)
                for lane, b, n in lanes:
                    pe.wait_ge(s.kT, n)
                    pe.wait_ge(s.qT, n)
                    pe.wait_ge(s.pick, n)
                    for h in range(XH):
                        nc.tensor.matmul(bank(lane, h)[0:S, 0:KEYS], pick[:, lane, :], bias[:, :], start=True, stop=False)
                    for h in range(XH):
                        rows = slice(XD * (h % 2), XD * (h % 2 + 1))
                        last = nc.tensor.matmul(bank(lane, h)[0:S, 0:KEYS], t.qT[rows, lane, h // 2, :], t.kT[rows, lane, h // 2, 0:KEYS],
                                                start=False, stop=True)
                    last.then_inc(s.scores_ready, 1)
                for lane, b, n in lanes:
                    pe.wait_ge(s.probs, n)
                    for j in range(KT):
                        for h in range(XH):
                            last = nc.tensor.transpose(bank(lane, j)[0:width[j], h * S:(h + 1) * S],
                                                       t.probs[0:S, lane, h, j * P:j * P + width[j]], g.ident[0:S, 0:S])
                    last.then_inc(s.turned_ready, 1)
                for lane, b, n in lanes:
                    pe.wait_ge(s.probsT_act, n)
                    pe.wait_ge(s.probsT_dve, n)
                    for h in range(XH):
                        for j in range(KT):
                            last = nc.tensor.matmul(bank(lane, 0)[0:S, h * (XD + 1):(h + 1) * (XD + 1)], t.probsT[0:width[j], lane, j, h * S:(h + 1) * S],
                                                    t.v[0:width[j], lane, j, h, :], start=(j == 0), stop=(j == KT - 1))
                    last.then_inc(s.heads_ready, 1)
                for lane, b, n in lanes:
                    pe.wait_ge(s.heads, n)
                    turn(nc, g, bank(lane, 1), t.heads[:, lane, :], DC).then_inc(s.headsT_ready, 1)
                for lane, b, n in lanes:
                    pe.wait_ge(s.headsT, n)
                    for c in range(DC):
                        nc.tensor.matmul(bank(lane, 2)[0:S, 0:D], t.headsT[:, lane, c, :], w.proj[:, c, :], start=(c == 0), stop=False)
                    nc.tensor.matmul(bank(lane, 2)[0:S, 0:D], g.ones[0:1, 0:S], w.proj_b[:, :], start=False, stop=True).then_inc(s.proj_ready, 1)

        @block.scalar
        def _(act):
            act.wait_ge(g.loaded.cross, g.total.cross)
            act.wait_ge(s.ones, 3)
            with act.Fori(0, PAIRS) as pair:
                lanes = lanes_of(act, pair)
                for lane, b, n in lanes:
                    act.wait_ge(s.yT_ready, n)
                    for c in range(DC):
                        last = nc.scalar.activation(t.lT[:, lane, c, 0:S], bank(lane, 0)[:, c * S:(c + 1) * S], ACT.Identity,
                                                    bias=w.ln_l[:, DC + c:DC + c + 1], scale=w.ln_l[:, c:c + 1])
                    last.then_inc(s.lT, 1)
                for lane, b, n in lanes:
                    act.wait_ge(s.q_ready, n)
                    nc.scalar.activation(t.qsq[:, lane, :], bank(lane, 3)[0:S, 0:D], ACT.Square).then_inc(s.qsq, 1)
                for lane, b, n in lanes:
                    act.wait_ge(s.ctxT_ready, n)
                    nc.scalar.activation(t.ctxT0[:, lane, :], bank(lane, 1)[:, 0:NT * P], ACT.Identity,
                                         bias=w.ln_x0[:, 1:2], scale=w.ln_x0[:, 0:1]).then_inc(s.ctxT_act, 1)
                for lane, b, n in lanes:
                    act.wait_ge(s.kv_ready, n)
                    nc.scalar.activation(t.ksq[:, lane, :, :], banks(lane, 0, KT)[:, :, 0:D], ACT.Square)
                    nc.scalar.copy(t.v[:, lane, :, :, 0:XD], banks(lane, 0, KT)[:, :, D:2 * D].rearrange("p t (h d) -> p t h d", d=XD)).then_inc(s.kv_act, 1)
                for lane, b, n in lanes:
                    act.wait_ge(s.kqT_ready, n)
                    nc.scalar.copy(t.kT[:, lane, :, :], banks(lane, 0, DC)).then_inc(s.kT, 1)
                for lane, b, n in lanes:
                    act.wait_ge(s.rowmax, n)
                    for h in range(XH):
                        last = nc.scalar.activation(t.probs[0:S, lane, h, :], bank(lane, h)[0:S, 0:KEYS], ACT.Exp, bias=t.rowmax[:, lane, h:h + 1])
                    last.then_inc(s.probs, 1)
                for lane, b, n in lanes:
                    act.wait_ge(s.turned_ready, n)
                    nc.scalar.copy(t.probsT[:, lane, 0:2, :], banks(lane, 0, 2)[:, :, 0:XH * S]).then_inc(s.probsT_act, 1)
                for lane, b, n in lanes:
                    act.wait_ge(s.headsT_ready, n)
                    nc.scalar.copy(t.headsT[:, lane, :, :], bank(lane, 1)[:, 0:DC * S].rearrange("p (c s) -> p c s", s=S)).then_inc(s.headsT, 1)

        @block.vector
        def _(dve):
            dve.wait_ge(g.loaded.cross, g.total.cross)
            dve.wait_ge(s.ones, 3)
            nc.vector.tensor_scalar(bias[:, 0:CTX], w.mask[:, :], 1.0, -MASKED, ALU.subtract, ALU.mult).then_inc(s.bias, 1)
            nc.vector.memset(bias[:, NT * P:KEYS], 0.0).then_inc(s.bias, 1)
            nc.vector.scalar_tensor_tensor(t.gain[:, :], w.qn_g[:, :], XD ** -0.5, w.kn_g[:, :], ALU.mult, ALU.mult).then_inc(s.gain, 1)
            dve.wait_ge(s.gain, 1)
            with dve.Fori(0, PAIRS) as pair:
                lanes = lanes_of(dve, pair)
                norm_stats(nc, dve, m1, lanes, lambda lane, b: g.x[:, b, :])
                for lane, b, n in lanes:
                    dve.wait_ge(raw_loaded[lane], dve.snap(pair * 32 + 32))
                    for j in range(NT):
                        last = nc.vector.bn_stats(t.cstats[:, lane, j, :], t.raw[:, lane, j, :])
                    last.then_inc(s.cstats, 1)
                for lane, b, n in lanes:
                    norm_apply(nc, dve, m1, lane, n, t.y[:, lane, :], g.x[:, b, :], s.y)
                dve.wait_ge(s.y, lanes[-1][2])
                norm_stats(nc, dve, m2, lanes, lambda lane, b: t.y[:, lane, :])
                dve.wait_ge(s.cstats, lanes[-1][2])
                nc.vector.memset(t.chold[:, :], 0.0)
                for lane, b, n in lanes:
                    for j in range(NT):
                        last = nc.vector.bn_aggr(t.cmeanvar[:, lane, j, :], t.cstats[:, lane, j, :])
                    last.then_inc(s.cmeanvar, 1)
                for lane, b, n in lanes:
                    norm_apply(nc, dve, m2, lane, n, t.yy[:, lane, :], t.y[:, lane, :], s.yy)
                for lane, b, n in lanes:
                    dve.wait_ge(s.crstd, n)
                    for j in range(NT):
                        last = nc.vector.tensor_scalar(t.cn[:, lane, j, :], t.raw[:, lane, j, :], t.cmeanvar[:, lane, j, 0:1], t.crstd[:, lane, j:j + 1],
                                                       ALU.subtract, ALU.mult)
                    last.then_inc(s.cn, 1)
                for lane, b, n in lanes:
                    dve.wait_ge(s.qsq, n)
                    nc.vector.reduce_sum(t.qsum[:, lane, :], t.qsq[:, lane, :].rearrange("s (h d) -> s h d", d=XD), AX.X).then_inc(s.qsum, 1)
                for lane, b, n in lanes:
                    dve.wait_ge(s.qsum, n)
                    nc.vector.tensor_scalar(t.qclip[:, lane, :], t.qsum[:, lane, :], 1.0 / XD, 1e-16, ALU.mult, ALU.max).then_inc(s.qclip, 1)
                for lane, b, n in lanes:
                    dve.wait_ge(s.ctxT_ready, n)
                    nc.vector.tensor_scalar(t.ctxT1[:, lane, :], bank(lane, 2)[0:CD - P, 0:NT * P], w.ln_x1[:, 0:1], w.ln_x1[:, 1:2],
                                            ALU.mult, ALU.add).then_inc(s.ctxT_dve, 1)
                for lane, b, n in lanes:
                    dve.wait_ge(s.qroot, n)
                    nc.vector.tensor_tensor(t.qn[:, lane, :].rearrange("s (h d) -> s h d", d=XD), bank(lane, 3)[0:S, 0:D].rearrange("s (h d) -> s h d", d=XD),
                                            t.qroot[:, lane, :].unsqueeze(2).broadcast_to([S, XH, XD]), ALU.mult).then_inc(s.qn, 1)
                for lane, b, n in lanes:
                    dve.wait_ge(s.kv_act, n)
                    nc.vector.reduce_sum(t.ksum[:, lane, :], t.ksq[:, lane, :, :].rearrange("p t (h d) -> p (t h) d", d=XD), AX.X).then_inc(s.ksum, 1)
                for lane, b, n in lanes:
                    dve.wait_ge(s.ksum, n)
                    nc.vector.tensor_scalar(t.kclip[:, lane, :], t.ksum[:, lane, :], 1.0 / XD, 1e-16, ALU.mult, ALU.max).then_inc(s.kclip, 1)
                for lane, b, n in lanes:
                    dve.wait_ge(s.kroot, n)
                    nc.vector.tensor_tensor(t.kn[:, lane, :, :].rearrange("p t (h d) -> p t h d", d=XD),
                                            banks(lane, 0, KT)[:, :, 0:D].rearrange("p t (h d) -> p t h d", d=XD),
                                            t.kroot[:, lane, :].rearrange("p (t h) -> p t h", h=XH).unsqueeze(3).broadcast_to([P, KT, XH, XD]),
                                            ALU.mult).then_inc(s.kn, 1)
                for lane, b, n in lanes:
                    dve.wait_ge(s.kqT_ready, n)
                    nc.vector.tensor_scalar(t.qT[:, lane, :, :], bank(lane, 2)[:, 0:DC * S].rearrange("p (c s) -> p c s", s=S), t.gain[:, :], None,
                                            ALU.mult).then_inc(s.qT, 1)
                for lane, b, n in lanes:
                    dve.wait_ge(s.scores_ready, n)
                    nc.vector.reduce_max(t.rowmax[:, lane, :], banks(lane, 0, XH)[0:S, :, 0:KEYS], AX.X, negate=True).then_inc(s.rowmax, 1)
                for lane, b, n in lanes:
                    dve.wait_ge(s.turned_ready, n)
                    nc.vector.tensor_copy(t.probsT[:, lane, 2, :], bank(lane, 2)[:, 0:XH * S])
                    nc.vector.tensor_copy(t.probsT[0:S, lane, 3, :], bank(lane, 3)[0:S, 0:XH * S]).then_inc(s.probsT_dve, 1)
                for lane, b, n in lanes:
                    dve.wait_ge(s.heads_ready, n)
                    o = bank(lane, 0)[0:S, 0:XH * (XD + 1)].rearrange("s (h d) -> s h d", d=XD + 1)
                    nc.vector.reciprocal(t.rowsum[:, lane, :].unsqueeze(2), o[:, :, XD:XD + 1]).then_inc(s.rowsum, 1)
                for lane, b, n in lanes:
                    dve.wait_ge(s.rowsum, n)
                    o = bank(lane, 0)[0:S, 0:XH * (XD + 1)].rearrange("s (h d) -> s h d", d=XD + 1)
                    nc.vector.tensor_tensor(t.heads[:, lane, :].rearrange("s (h d) -> s h d", d=XD), o[:, :, 0:XD],
                                            t.rowsum[:, lane, :].unsqueeze(2).broadcast_to([S, XH, XD]), ALU.mult).then_inc(s.heads, 1)
                for lane, b, n in lanes:
                    dve.wait_ge(s.proj_ready, n)
                    nc.vector.tensor_tensor(g.x[:, b, :], g.x[:, b, :], bank(lane, 2)[0:S, 0:D], ALU.add)



TWO_PI_HI = float(np.float32(6.28125))
TWO_PI_LO = float(2 * np.pi - 6.28125)
PI_BELOW = float(np.nextafter(np.float32(np.pi), np.float32(0)))
NQ = 8


def rotation_phase(nc, g, w):
    ROUNDS = 8
    with ExitStack() as ctx:
        s = semaphores(nc, ctx, "rot", "filled folded_ready folded turns whole_i whole near angle size cosine sine k_bias y yT_ready yT qkv_ready q kv "
                       "vectors_ready vectors turned mixed_im mixed squares norms kT_ready kmax kmin spread_in spread_ready ends inverse ratios ratio mean_ready heads "
                       "headsT_ready headsT proj_ready")
        h_ready = [ctx.enter_context(nc.semaphore(f"rot_tanh_in_ready{k}")) for k in range(ROUNDS)]
        h_done = [ctx.enter_context(nc.semaphore(f"rot_tanh{k}")) for k in range(ROUNDS)]
        VW = 2 * NQ
        t = buffers(nc, ctx, "rot", y=[S, LANES, D], yT=[P, LANES, DC, S], q=[P, LANES, 2, 2 * DC * S], v=[S, LANES, D],
                    h=[P, LANES, 2, DC, 2, QT * S], w2=[P, DC, VW], b2=[S, VW], k_bias=[P, 2, DC], cos=[S, PAIRS, NH], sin=[S, PAIRS, NH],
                    turns=[S, 4, NH], near=[S, 4, NH], angle=[S, 4, NH], size=[S, 4, NH],
                    vec=[S, LANES, 2, NH, VW], by_cos=[S, LANES, 2, NH, NQ], by_sin=[S, LANES, 2, NH, NQ], mixed=[S, LANES, 2, NH, NQ],
                    norms=[S, LANES, 2, NH], ends=[NH, LANES, 2], spread=[NH, LANES, 2, NH], span=[S, LANES, 2, NH],
                    ratios=[S, LANES, 2, NH], inverse=[S, LANES, 2, NH], ratio=[S, LANES, NH], heads=[S, LANES, D], headsT=[P, LANES, DC, S])
        whole = ctx.enter_context(nc.sbuf_tensor("rot_whole", [S, 4, NH], I32))
        m1 = norm_of(nc, ctx, "rot_ln")
        bank = lambda lane, k: g.psum[:, lane * BANKS + k, :]
        banks = lambda lane, a, b: g.psum[:, lane * BANKS + a:lane * BANKS + b, :]
        block = ctx.enter_context(nc.Block())

        @block.gpsimd
        def _(pool):
            nc.gpsimd.memset(t.cos[:, :, :], 1.0).then_inc(s.filled, 1)
            nc.gpsimd.memset(t.sin[:, :, :], 0.0).then_inc(s.filled, 1)
            with pool.Fori(0, PAIRS) as pair:
                for lane, b, n in lanes_of(pool, pair):
                    norm_root(nc, pool, g, m1, lane, n)

        @block.tensor
        def _(pe):
            pe.wait_ge(g.loaded.rot, g.total.rot)
            for part in range(2):
                for c in range(DC):
                    at = c * VW + part * NQ
                    nc.tensor.matmul(bank(0, 0)[:, at:at + NQ], w.w2T[:, part, c * P:(c + 1) * P], w.hadamard[:, :], start=True, stop=True)
                last = nc.tensor.matmul(bank(0, 1)[0:S, part * NQ:(part + 1) * NQ], w.b2[:, part, :], w.hadamard[:, :], start=True, stop=True)
            last.then_inc(s.folded_ready, 1)
            pe.wait_ge(s.folded, 1)
            with pe.Fori(0, PAIRS) as pair:
                lanes = lanes_of(pe, pair)
                for lane, b, n in lanes:
                    pe.wait_ge(s.y, n)
                    turn(nc, g, bank(lane, 0), t.y[:, lane, :], DC).then_inc(s.yT_ready, 1)
                for lane, b, n in lanes:
                    pe.wait_ge(s.yT, n)
                    for m in range(2 * DC):
                        for c in range(DC):
                            nc.tensor.matmul(bank(lane, 1 if m < DC else 3)[:, m % DC * S:(m % DC + 1) * S], w.qkv[:, c, m * P:(m + 1) * P],
                                             t.yT[:, lane, c, :], start=(c == 0), stop=(c == DC - 1))
                    for c in range(DC):
                        nc.tensor.matmul(bank(lane, 2)[0:S, 0:D], t.yT[:, lane, c, :], w.qkv[:, c, 2 * D:3 * D], start=(c == 0), stop=False)
                    nc.tensor.matmul(bank(lane, 2)[0:S, 0:D], g.ones[0:1, 0:S], w.v_b[:, :], start=False, stop=True).then_inc(s.qkv_ready, 1)

                def last_layer(lane, n, k):
                    part, half = k // 4, k // 2 % 2
                    pe.wait_ge(h_done[k], n)
                    for j in range(2):
                        for e in range(2):
                            for c in range(DC):
                                at, o = (e * DC + c) * S, (part * NH + head_at(2 * half + j, e, c)) * VW
                                for m in range(DC):
                                    last = nc.tensor.matmul(bank(lane, 3)[0:S, o:o + VW], t.h[:, lane, k // 2 % 2, m, j, at:at + S], t.w2[:, m, :],
                                                            start=(m == 0), stop=(m == DC - 1))
                    return last

                for k in range(ROUNDS):
                    part, half, m = k // 4, k // 2 % 2, k % 2
                    for lane, b, n in lanes:
                        if k == 0:
                            pe.wait_ge(s.q, n)
                            pe.wait_ge(s.kv, n)
                        else:
                            pe.wait_ge(h_done[k - 1], n)
                        for j in range(2):
                            r = 2 * half + j
                            rows = slice(ROWS * r, ROWS * (r + 1))
                            last = nc.tensor.matmul(bank(lane, j)[:, 0:QT * S], w.w1[rows, m * P:(m + 1) * P], t.q[rows, lane, part, :], start=True, stop=True)
                        last.then_inc(h_ready[k], 1)
                    if k % 2 == 0 and k:
                        for lane, b, n in lanes:
                            last_layer(lane, n, k - 1)
                for lane, b, n in lanes:
                    last_layer(lane, n, ROUNDS - 1).then_inc(s.vectors_ready, 1)
                for lane, b, n in lanes:
                    nc.tensor.matmul(bank(lane, 2)[0:S, 0:D], w.uniform[:, :], t.v[:, lane, :], start=True, stop=True).then_inc(s.mean_ready, 1)
                for lane, b, n in lanes:
                    pe.wait_ge(s.norms, n)
                    nc.tensor.transpose(bank(lane, 0)[0:NH, 0:S], t.norms[:, lane, 1, :], g.ident[0:S, 0:S]).then_inc(s.kT_ready, 1)
                for lane, b, n in lanes:
                    pe.wait_ge(s.spread_in, n)
                    nc.tensor.matmul(bank(lane, 1)[0:S, 0:2 * NH], g.ones[0:NH, 0:S], t.spread[:, lane, :, :].rearrange("h a b -> h (a b)"),
                                     start=True, stop=True).then_inc(s.spread_ready, 1)
                for lane, b, n in lanes:
                    pe.wait_ge(s.heads, n)
                    turn(nc, g, bank(lane, 1), t.heads[:, lane, :], DC).then_inc(s.headsT_ready, 1)
                for lane, b, n in lanes:
                    pe.wait_ge(s.headsT, n)
                    for c in range(DC):
                        nc.tensor.matmul(bank(lane, 2)[0:S, 0:D], t.headsT[:, lane, c, :], w.proj[:, c, :], start=(c == 0), stop=False)
                    nc.tensor.matmul(bank(lane, 2)[0:S, 0:D], g.ones[0:1, 0:S], w.proj_b[:, :], start=False, stop=True).then_inc(s.proj_ready, 1)

        @block.scalar
        def _(act):
            act.wait_ge(s.filled, 2)
            act.wait_ge(s.angle, 1)
            nc.scalar.activation(t.sin[:, 0:NQ // 2, :], t.angle[:, :, :], ACT.Sin).then_inc(s.sine, 1)
            act.wait_ge(s.size, 2)
            nc.scalar.activation(t.cos[:, 0:NQ // 2, :], t.size[:, :, :], ACT.Sin).then_inc(s.cosine, 1)
            act.wait_ge(s.k_bias, 1)
            with act.Fori(0, PAIRS) as pair:
                lanes = lanes_of(act, pair)
                for lane, b, n in lanes:
                    act.wait_ge(s.yT_ready, n)
                    nc.scalar.copy(t.yT[:, lane, :, :], bank(lane, 0)[:, 0:DC * S].rearrange("p (c s) -> p c s", s=S)).then_inc(s.yT, 1)
                for lane, b, n in lanes:
                    act.wait_ge(s.qkv_ready, n)
                    for e in range(2):
                        for c in range(DC):
                            at = (e * DC + c) * S
                            nc.scalar.activation(t.q[:, lane, 1, at:at + S], bank(lane, 3)[:, c * S:(c + 1) * S], ACT.Identity,
                                                 bias=t.k_bias[:, e, c:c + 1], scale=w.half[:, e:e + 1])
                    nc.scalar.copy(t.v[:, lane, :], bank(lane, 2)[0:S, 0:D]).then_inc(s.kv, 1)
                for k in range(ROUNDS):
                    for lane, b, n in lanes:
                        act.wait_ge(h_ready[k], n)
                        nc.scalar.activation(t.h[:, lane, k // 2 % 2, k % 2, :, :], banks(lane, 0, 2)[:, :, 0:QT * S], ACT.Tanh,
                                             bias=w.b1[:, k % 2:k % 2 + 1]).then_inc(h_done[k], 1)
                for lane, b, n in lanes:
                    act.wait_ge(s.headsT_ready, n)
                    nc.scalar.copy(t.headsT[:, lane, :, :], bank(lane, 1)[:, 0:DC * S].rearrange("p (c s) -> p c s", s=S)).then_inc(s.headsT, 1)

        @block.vector
        def _(dve):
            dve.wait_ge(g.loaded.rot, g.total.rot)
            nc.vector.tensor_scalar(t.turns[:, :, :], w.rot[:, :, :], 0.25 / np.pi, None, ALU.mult).then_inc(s.turns, 1)
            dve.wait_ge(s.turns, 1)
            nc.vector.tensor_copy(whole[:, :, :], t.turns[:, :, :]).then_inc(s.whole_i, 1)
            dve.wait_ge(s.whole_i, 1)
            nc.vector.tensor_copy(t.turns[:, :, :], whole[:, :, :]).then_inc(s.whole, 1)
            nc.vector.tensor_scalar(t.near[:, :, :], w.rot[:, :, :], 0.5, None, ALU.mult).then_inc(s.whole, 1)
            dve.wait_ge(s.whole, 2)
            nc.vector.scalar_tensor_tensor(t.near[:, :, :], t.turns[:, :, :], -TWO_PI_HI, t.near[:, :, :], ALU.mult, ALU.add).then_inc(s.near, 1)
            dve.wait_ge(s.near, 1)
            nc.vector.scalar_tensor_tensor(t.near[:, :, :], t.turns[:, :, :], -TWO_PI_LO, t.near[:, :, :], ALU.mult, ALU.add).then_inc(s.near, 1)
            dve.wait_ge(s.near, 2)
            nc.vector.tensor_scalar(t.angle[:, :, :], t.near[:, :, :], PI_BELOW, -PI_BELOW, ALU.min, ALU.max).then_inc(s.angle, 1)
            dve.wait_ge(s.angle, 1)
            nc.vector.scalar_tensor_tensor(t.size[:, :, :], t.angle[:, :, :], -1.0, t.angle[:, :, :], ALU.mult, ALU.max).then_inc(s.size, 1)
            dve.wait_ge(s.size, 1)
            nc.vector.tensor_scalar(t.size[:, :, :], t.size[:, :, :], -1.0, float(np.pi / 2), ALU.mult, ALU.add).then_inc(s.size, 1)
            for e in range(2):
                last = nc.vector.tensor_scalar(t.k_bias[:, e, :], w.qk_b[:, DC:2 * DC], w.half[:, e:e + 1], None, ALU.mult)
            last.then_inc(s.k_bias, 1)
            dve.wait_ge(s.folded_ready, 1)
            nc.vector.tensor_copy(t.w2[:, :, :], bank(0, 0)[:, 0:DC * VW].rearrange("p (c v) -> p c v", v=VW))
            nc.vector.tensor_copy(t.b2[:, :], bank(0, 1)[0:S, 0:VW]).then_inc(s.folded, 1)
            dve.wait_ge(s.folded, 1)
            dve.wait_ge(s.sine, 1)
            dve.wait_ge(s.cosine, 1)
            with dve.Fori(0, PAIRS) as pair:
                lanes = lanes_of(dve, pair)
                both = lanes[-1][2]
                norm_stats(nc, dve, m1, lanes, lambda lane, b: g.x[:, b, :])
                for lane, b, n in lanes:
                    norm_apply(nc, dve, m1, lane, n, t.y[:, lane, :], g.x[:, b, :], s.y)
                for lane, b, n in lanes:
                    dve.wait_ge(s.qkv_ready, n)
                    for e in range(2):
                        for c in range(DC):
                            at = (e * DC + c) * S
                            last = nc.vector.tensor_scalar(t.q[:, lane, 0, at:at + S], bank(lane, 1)[:, c * S:(c + 1) * S], w.qk_b[:, c:c + 1],
                                                           w.half[:, e:e + 1], ALU.add, ALU.mult)
                    last.then_inc(s.q, 1)
                for lane, b, n in lanes:
                    dve.wait_ge(s.vectors_ready, n)
                    nc.vector.tensor_tensor(t.vec[:, lane, :, :, :].rearrange("s a h v -> s (a h) v"), bank(lane, 3)[0:S, :].rearrange("s (i v) -> s i v", v=VW),
                                            t.b2[:, :].unsqueeze(1).broadcast_to([S, 2 * NH, VW]), ALU.add).then_inc(s.vectors, 1)
                for lane, b, n in lanes:
                    dve.wait_ge(s.vectors, both)
                    for part in range(2):
                        turn_by = lambda table: table[:, pair, :].unsqueeze(2).broadcast_to([S, NH, NQ])
                        nc.vector.tensor_tensor(t.by_cos[:, lane, part, :, :], t.vec[:, lane, part, :, 0:NQ], turn_by(t.cos), ALU.mult)
                        last = nc.vector.tensor_tensor(t.by_sin[:, lane, part, :, :], t.vec[:, 1 - lane, part, :, NQ:VW], turn_by(t.sin), ALU.mult)
                    last.then_inc(s.turned, 1)
                for lane, b, n in lanes:
                    dve.wait_ge(s.turned, n)
                    nc.vector.tensor_tensor(t.mixed[:, lane, :, :, :], t.by_cos[:, lane, :, :, :], t.by_sin[:, lane, :, :, :], ALU.add).then_inc(s.mixed, 1)
                for lane, b, n in lanes:
                    dve.wait_ge(s.mixed, n)
                    nc.vector.tensor_tensor(t.by_cos[:, lane, :, :, :], t.mixed[:, lane, :, :, :], t.mixed[:, lane, :, :, :], ALU.mult).then_inc(s.squares, 1)
                for lane, b, n in lanes:
                    dve.wait_ge(s.squares, n)
                    nc.vector.reduce_sum(t.norms[:, lane, :, :], t.by_cos[:, lane, :, :, :], AX.X).then_inc(s.norms, 1)
                for lane, b, n in lanes:
                    dve.wait_ge(s.kT_ready, n)
                    nc.vector.reduce_max(t.ends[:, lane, 0:1], bank(lane, 0)[0:NH, 0:S], AX.X)
                    nc.vector.tensor_reduce(t.ends[:, lane, 1:2], bank(lane, 0)[0:NH, 0:S], AX.X, ALU.min).then_inc(s.kmin, 1)
                for lane, b, n in lanes:
                    dve.wait_ge(s.kmin, n)
                    for k in range(2):
                        last = nc.vector.tensor_scalar(t.spread[:, lane, k, :], g.ident[0:NH, 0:NH], t.ends[:, lane, k:k + 1], None, ALU.mult)
                    last.then_inc(s.spread_in, 1)
                for lane, b, n in lanes:
                    dve.wait_ge(s.spread_ready, n)
                    nc.vector.tensor_tensor(t.span[:, lane, :, :], bank(lane, 1)[0:S, 0:2 * NH].rearrange("s (k h) -> s k h", h=NH),
                                            t.norms[:, lane, 0, :].unsqueeze(1).broadcast_to([S, 2, NH]), ALU.mult).then_inc(s.ends, 1)
                for lane, b, n in lanes:
                    dve.wait_ge(s.ends, n)
                    nc.vector.reciprocal(t.inverse[:, lane, :, :], t.span[:, lane, :, :]).then_inc(s.inverse, 1)
                for lane, b, n in lanes:
                    dve.wait_ge(s.inverse, n)
                    nc.vector.tensor_tensor(t.ratios[:, lane, :, :], t.span[:, lane, :, :], t.inverse[:, lane, :, :], ALU.mult).then_inc(s.ratios, 1)
                for lane, b, n in lanes:
                    dve.wait_ge(s.ratios, n)
                    nc.vector.tensor_tensor(t.ratio[:, lane, :], t.ratios[:, lane, 0, :], t.ratios[:, lane, 1, :], ALU.mult).then_inc(s.ratio, 1)
                for lane, b, n in lanes:
                    dve.wait_ge(s.ratio, n)
                    dve.wait_ge(s.mean_ready, n)
                    nc.vector.tensor_tensor(t.heads[:, lane, :].rearrange("s (h d) -> s h d", d=HD), bank(lane, 2)[0:S, 0:D].rearrange("s (h d) -> s h d", d=HD),
                                            t.ratio[:, lane, :].unsqueeze(2).broadcast_to([S, NH, HD]), ALU.mult).then_inc(s.heads, 1)
                for lane, b, n in lanes:
                    dve.wait_ge(s.proj_ready, n)
                    nc.vector.tensor_tensor(g.x[:, b, :], g.x[:, b, :], bank(lane, 2)[0:S, 0:D], ALU.add)



def wide_cross_phase(nc, g, w, ctxT_in):
    GROUP = 4
    GROUPS = WH // GROUP
    with ExitStack() as ctx:
        s = semaphores(nc, ctx, "wide", "ones bias any_key any_inverse any y yT_ready yT k_ready0 k_act0 k_dve0 k_ready1 k_act1 k_dve1 v_ready0 v_act0 v_dve0 "
                       "vq_ready v_act1 q headsT_ready headsT_act headsT_dve proj_ready")
        a = [semaphores(nc, ctx, f"wide{k}", "scores_ready rowmax probs turned_ready probsT_act probsT_dve heads_ready rowsum heads") for k in range(GROUPS)]
        ctx_loaded = [ctx.enter_context(nc.semaphore(f"wide_ctx_loaded{lane}")) for lane in range(LANES)]
        t = buffers(nc, ctx, "wide", y=[S, LANES, D], yT=[P, LANES, DC, S], c0=[P, LANES, CTX], c1=[CD - P, LANES, CTX], kT=[P, LANES, WM, CTX],
                    v=[P, LANES, NT, WH, WD + 1], qT=[P, LANES, WM, S], rowmax=[S, LANES, GROUP], probs=[S, LANES, GROUP, CTX],
                    probsT=[P, LANES, NT, GROUP * S], rowsum=[S, LANES, GROUP], heads=[S, LANES, WI], headsT=[P, LANES, WM, S], any_key=[S, 1], any_inverse=[S, 1], any=[S, 1])
        bias = ctx.enter_context(nc.sbuf_tensor("wide_bias", [S, CTX], BF16))
        m1 = norm_of(nc, ctx, "wide_ln")
        bank = lambda lane, k: g.psum[:, lane * BANKS + k, :]
        banks = lambda lane, a, b: g.psum[:, lane * BANKS + a:lane * BANKS + b, :]
        block = ctx.enter_context(nc.Block())

        def load_ctx(sp, lane, b):
            sp.dma_start(t.c0[:, lane, :], ctxT_in[0:P, b, :]).then_inc(ctx_loaded[lane], 16)
            sp.dma_start(t.c1[:, lane, :], ctxT_in[P:CD, b, :]).then_inc(ctx_loaded[lane], 16)

        @block.sync
        def _(sp):
            for lane in range(LANES):
                load_ctx(sp, lane, lane)
            with sp.Fori(1, PAIRS) as pair:
                for lane, b, n in lanes_of(sp, pair):
                    sp.wait_ge(s.vq_ready, sp.snap(b - 1))
                    load_ctx(sp, lane, b)

        @block.gpsimd
        def _(pool):
            nc.gpsimd.memset(t.v[:, :, :, :, WD:WD + 1], 1.0).then_inc(s.ones, 1)
            with pool.Fori(0, PAIRS) as pair:
                for lane, b, n in lanes_of(pool, pair):
                    norm_root(nc, pool, g, m1, lane, n)

        @block.tensor
        def _(pe):
            pe.wait_ge(g.loaded.wide, g.total.wide)
            pe.wait_ge(s.ones, 1)
            pe.wait_ge(s.bias, 1)
            with pe.Fori(0, PAIRS) as pair:
                lanes = lanes_of(pe, pair)

                def v_tile(lane, j, first):
                    k0, kw = CTX_TILES[j]
                    for half in range(2):
                        cols = slice(half * BANK, (half + 1) * BANK)
                        nc.tensor.matmul(bank(lane, first + half)[0:kw, :], t.c0[:, lane, k0:k0 + kw], w.v0[:, cols], start=True, stop=False)
                        last = nc.tensor.matmul(bank(lane, first + half)[0:kw, :], t.c1[:, lane, k0:k0 + kw], w.v1[:, cols], start=False, stop=True)
                    return last

                for lane, b, n in lanes:
                    pe.wait_ge(s.y, n)
                    turn(nc, g, bank(lane, 0), t.y[:, lane, :], DC).then_inc(s.yT_ready, 1)
                for half, done in enumerate((s.k_ready0, s.k_ready1)):
                    for lane, b, n in lanes:
                        if half == 0:
                            pe.wait_ge(ctx_loaded[lane], pe.snap(pair * 32 + 32))
                            pe.wait_ge(s.yT, n)
                        else:
                            pe.wait_ge(s.k_act0, n)
                            pe.wait_ge(s.k_dve0, n)
                        for j in range(BANKS):
                            cols = slice((half * BANKS + j) * P, (half * BANKS + j + 1) * P)
                            nc.tensor.matmul(bank(lane, j)[:, 0:CTX], w.k0[:, cols], t.c0[:, lane, :], start=True, stop=False)
                            last = nc.tensor.matmul(bank(lane, j)[:, 0:CTX], w.k1[:, cols], t.c1[:, lane, :], start=False, stop=True)
                        last.then_inc(done, 1)
                for lane, b, n in lanes:
                    pe.wait_ge(s.k_act1, n)
                    pe.wait_ge(s.k_dve1, n)
                    v_tile(lane, 0, 0)
                    v_tile(lane, 1, 2).then_inc(s.v_ready0, 1)
                for lane, b, n in lanes:
                    pe.wait_ge(s.v_act0, n)
                    pe.wait_ge(s.v_dve0, n)
                    v_tile(lane, 2, 0)
                    for m in range(WM):
                        for c in range(DC):
                            last = nc.tensor.matmul(bank(lane, 2 + m // 4)[:, m % 4 * S:(m % 4 + 1) * S], w.q[:, c, m * P:(m + 1) * P], t.yT[:, lane, c, :],
                                                    start=(c == 0), stop=(c == DC - 1))
                    last.then_inc(s.vq_ready, 1)
                for k in range(GROUPS):
                    for lane, b, n in lanes:
                        if k == 0:
                            pe.wait_ge(s.v_act1, n)
                            pe.wait_ge(s.q, n)
                        else:
                            pe.wait_ge(a[k - 1].heads, n)
                        for j in range(GROUP):
                            nc.tensor.matmul(bank(lane, j)[0:S, 0:CTX], g.ident_b[0:S, 0:S], bias[:, :], start=True, stop=False)
                        for j in range(GROUP):
                            h = k * GROUP + j
                            rows = slice(WD * (h % 2), WD * (h % 2 + 1))
                            last = nc.tensor.matmul(bank(lane, j)[0:S, 0:CTX], t.qT[rows, lane, h // 2, :], t.kT[rows, lane, h // 2, :], start=False, stop=True)
                        last.then_inc(a[k].scores_ready, 1)
                    for lane, b, n in lanes:
                        pe.wait_ge(a[k].probs, n)
                        for i, (k0, kw) in enumerate(CTX_TILES):
                            for j in range(GROUP):
                                last = nc.tensor.transpose(bank(lane, i)[0:kw, j * S:(j + 1) * S], t.probs[:, lane, j, k0:k0 + kw], g.ident[0:S, 0:S])
                        last.then_inc(a[k].turned_ready, 1)
                    for lane, b, n in lanes:
                        pe.wait_ge(a[k].probsT_act, n)
                        pe.wait_ge(a[k].probsT_dve, n)
                        for j in range(GROUP):
                            for i, (k0, kw) in enumerate(CTX_TILES):
                                last = nc.tensor.matmul(bank(lane, 3)[0:S, j * (WD + 1):(j + 1) * (WD + 1)], t.probsT[0:kw, lane, i, j * S:(j + 1) * S],
                                                        t.v[0:kw, lane, i, k * GROUP + j, :], start=(i == 0), stop=(i == NT - 1))
                        last.then_inc(a[k].heads_ready, 1)
                for lane, b, n in lanes:
                    pe.wait_ge(a[GROUPS - 1].heads, n)
                    for m in range(WM):
                        last = nc.tensor.transpose(bank(lane, m // 4)[:, m % 4 * S:(m % 4 + 1) * S], t.heads[:, lane, m * P:(m + 1) * P], g.ident[0:S, 0:S])
                    last.then_inc(s.headsT_ready, 1)
                for lane, b, n in lanes:
                    pe.wait_ge(s.headsT_act, n)
                    pe.wait_ge(s.headsT_dve, n)
                    for m in range(WM):
                        nc.tensor.matmul(bank(lane, 2)[0:S, 0:D], t.headsT[:, lane, m, :], w.proj[:, m, :], start=(m == 0), stop=False)
                    nc.tensor.matmul(bank(lane, 2)[0:S, 0:D], g.ones[0:1, 0:S], w.proj_b[:, :], start=False, stop=True).then_inc(s.proj_ready, 1)

        def v_rows(v, j, lane, psum):
            kw = CTX_TILES[j][1]
            return v[0:kw, lane, j, :, 0:WD].rearrange("k (b h) d -> k b h d", b=2), psum[0:kw, :, :].rearrange("k b (h d) -> k b h d", d=WD)

        @block.scalar
        def _(act):
            act.wait_ge(g.loaded.wide, g.total.wide)
            act.wait_ge(s.ones, 1)
            with act.Fori(0, PAIRS) as pair:
                lanes = lanes_of(act, pair)
                for lane, b, n in lanes:
                    act.wait_ge(s.yT_ready, n)
                    for c in range(DC):
                        last = nc.scalar.activation(t.yT[:, lane, c, :], bank(lane, 0)[:, c * S:(c + 1) * S], ACT.Identity,
                                                    bias=w.ln[:, DC + c:DC + c + 1], scale=w.ln[:, c:c + 1])
                    last.then_inc(s.yT, 1)
                for half, (ready, done) in enumerate(((s.k_ready0, s.k_act0), (s.k_ready1, s.k_act1))):
                    for lane, b, n in lanes:
                        act.wait_ge(ready, n)
                        nc.scalar.copy(t.kT[:, lane, half * BANKS:half * BANKS + 2, :], banks(lane, 0, 2)[:, :, 0:CTX]).then_inc(done, 1)
                for j, (ready, done) in enumerate(((s.v_ready0, s.v_act0), (s.vq_ready, s.v_act1))):
                    for lane, b, n in lanes:
                        act.wait_ge(ready, n)
                        nc.scalar.copy(*v_rows(t.v, 2 * j, lane, banks(lane, 0, 2))).then_inc(done, 1)
                for k in range(GROUPS):
                    for lane, b, n in lanes:
                        act.wait_ge(a[k].rowmax, n)
                        for j in range(GROUP):
                            last = nc.scalar.activation(t.probs[:, lane, j, :], bank(lane, j)[0:S, 0:CTX], ACT.Exp, bias=t.rowmax[:, lane, j:j + 1])
                        last.then_inc(a[k].probs, 1)
                    for lane, b, n in lanes:
                        act.wait_ge(a[k].turned_ready, n)
                        nc.scalar.copy(t.probsT[:, lane, 0, :], bank(lane, 0)[:, 0:GROUP * S]).then_inc(a[k].probsT_act, 1)
                for lane, b, n in lanes:
                    act.wait_ge(s.headsT_ready, n)
                    nc.scalar.copy(t.headsT[:, lane, 0:4, :], bank(lane, 0)[:, 0:4 * S].rearrange("p (c s) -> p c s", s=S)).then_inc(s.headsT_act, 1)

        @block.vector
        def _(dve):
            dve.wait_ge(g.loaded.wide, g.total.wide)
            nc.vector.tensor_scalar(bias[:, :], w.mask[:, :], 1.0, -MASKED, ALU.subtract, ALU.mult).then_inc(s.bias, 1)
            nc.vector.reduce_max(t.any_key[:, :], w.mask[:, :], AX.X).then_inc(s.any_key, 1)
            dve.wait_ge(s.any_key, 1)
            nc.vector.reciprocal(t.any_inverse[:, :], t.any_key[:, :]).then_inc(s.any_inverse, 1)
            dve.wait_ge(s.any_inverse, 1)
            nc.vector.tensor_tensor(t.any[:, :], t.any_key[:, :], t.any_inverse[:, :], ALU.mult).then_inc(s.any, 1)
            dve.wait_ge(s.any, 1)
            dve.wait_ge(s.ones, 1)
            with dve.Fori(0, PAIRS) as pair:
                lanes = lanes_of(dve, pair)
                norm_stats(nc, dve, m1, lanes, lambda lane, b: g.x[:, b, :])
                for lane, b, n in lanes:
                    norm_apply(nc, dve, m1, lane, n, t.y[:, lane, :], g.x[:, b, :], s.y)
                for half, (ready, done) in enumerate(((s.k_ready0, s.k_dve0), (s.k_ready1, s.k_dve1))):
                    for lane, b, n in lanes:
                        dve.wait_ge(ready, n)
                        nc.vector.tensor_copy(t.kT[:, lane, half * BANKS + 2:half * BANKS + 4, :], banks(lane, 2, 4)[:, :, 0:CTX]).then_inc(done, 1)
                for lane, b, n in lanes:
                    dve.wait_ge(s.v_ready0, n)
                    nc.vector.tensor_copy(*v_rows(t.v, 1, lane, banks(lane, 2, 4))).then_inc(s.v_dve0, 1)
                for lane, b, n in lanes:
                    dve.wait_ge(s.vq_ready, n)
                    nc.vector.tensor_scalar(t.qT[:, lane, :, :].rearrange("p (b c) s -> p b (c s)", b=2), banks(lane, 2, 4)[:, :, 0:4 * S], WD ** -0.5, None,
                                            ALU.mult).then_inc(s.q, 1)
                for k in range(GROUPS):
                    for lane, b, n in lanes:
                        dve.wait_ge(a[k].scores_ready, n)
                        nc.vector.reduce_max(t.rowmax[:, lane, :], banks(lane, 0, GROUP)[0:S, :, 0:CTX], AX.X, negate=True).then_inc(a[k].rowmax, 1)
                    for lane, b, n in lanes:
                        dve.wait_ge(a[k].turned_ready, n)
                        for i in (1, 2):
                            kw = CTX_TILES[i][1]
                            last = nc.vector.tensor_copy(t.probsT[0:kw, lane, i, :], bank(lane, i)[0:kw, 0:GROUP * S])
                        last.then_inc(a[k].probsT_dve, 1)
                    for lane, b, n in lanes:
                        dve.wait_ge(a[k].heads_ready, n)
                        o = bank(lane, 3)[0:S, 0:GROUP * (WD + 1)].rearrange("s (h d) -> s h d", d=WD + 1)
                        nc.vector.reciprocal(t.rowsum[:, lane, :].unsqueeze(2), o[:, :, WD:WD + 1]).then_inc(a[k].rowsum, 1)
                    for lane, b, n in lanes:
                        dve.wait_ge(a[k].rowsum, n)
                        o = bank(lane, 3)[0:S, 0:GROUP * (WD + 1)].rearrange("s (h d) -> s h d", d=WD + 1)
                        nc.vector.tensor_tensor(t.heads[:, lane, k * GROUP * WD:(k + 1) * GROUP * WD].rearrange("s (h d) -> s h d", d=WD), o[:, :, 0:WD],
                                                t.rowsum[:, lane, :].unsqueeze(2).broadcast_to([S, GROUP, WD]), ALU.mult).then_inc(a[k].heads, 1)
                for lane, b, n in lanes:
                    dve.wait_ge(s.headsT_ready, n)
                    nc.vector.tensor_copy(t.headsT[:, lane, 4:8, :], bank(lane, 1)[:, 0:4 * S].rearrange("p (c s) -> p c s", s=S)).then_inc(s.headsT_dve, 1)
                for lane, b, n in lanes:
                    dve.wait_ge(s.proj_ready, n)
                    nc.vector.scalar_tensor_tensor(g.x[:, b, :], bank(lane, 2)[0:S, 0:D], t.any[:, :], g.x[:, b, :], ALU.mult, ALU.add)



EXPERTS = NE + 1
RING = 3
UNIT = 4
UT = UNIT * S
UNITS = B // UNIT


def gate_phase(nc, g, w, f):
    with ExitStack() as ctx:
        z = semaphores(nc, ctx, "gate", "ones y yT_ready yT kept gates_ready gates gmax gexp cmp ties behind rank chosen gsum grec coef coefT_ready coefT")
        u = buffers(nc, ctx, "gate", y=[S, LANES, D], yT=[P, LANES, DC, S], gates=[S, LANES, NE], gmax=[S, LANES, 1], gexp=[S, LANES, NE],
                    above=[S, LANES, NE, NE], equal=[S, LANES, NE, NE], rank=[S, LANES, NE], chosen=[S, LANES, NE], gsum=[S, LANES, 1],
                    grec=[S, LANES, 1], coef=[S, LANES, EXPERTS])
        m1 = norm_of(nc, ctx, "gate_ln")
        bank = lambda lane, k: g.psum[:, lane * BANKS + k, :]
        block = ctx.enter_context(nc.Block())

        @block.gpsimd
        def _(pool):
            nc.gpsimd.memset(u.coef[:, :, 0:1], 1.0).then_inc(z.ones, 1)
            nc.gpsimd.memset(f.sum[:, :, :], 0.0)
            with pool.Fori(0, PAIRS) as pair:
                lanes = lanes_of(pool, pair)
                for lane, b, n in lanes:
                    norm_root(nc, pool, g, m1, lane, n)
                for lane, b, n in lanes:
                    pool.wait_ge(z.yT, n)
                    nc.gpsimd.tensor_copy(f.yT[:, :, bass.ds(b * S, S)], u.yT[:, lane, :, :]).then_inc(z.kept, 1)

        @block.tensor
        def _(pe):
            pe.wait_ge(g.loaded.moe, g.total.moe)
            with pe.Fori(0, PAIRS) as pair:
                lanes = lanes_of(pe, pair)
                for lane, b, n in lanes:
                    pe.wait_ge(z.y, n)
                    turn(nc, g, bank(lane, 0), u.y[:, lane, :], DC).then_inc(z.yT_ready, 1)
                for lane, b, n in lanes:
                    pe.wait_ge(z.yT, n)
                    for c in range(DC):
                        last = nc.tensor.matmul(bank(lane, 1)[0:S, 0:NE], u.yT[:, lane, c, :], w.gate[:, c, :], start=(c == 0), stop=(c == DC - 1))
                    last.then_inc(z.gates_ready, 1)
                for lane, b, n in lanes:
                    pe.wait_ge(z.coef, n)
                    pe.wait_ge(z.kept, n)
                    nc.tensor.transpose(bank(lane, 2)[0:EXPERTS, 0:S], u.coef[:, lane, :], g.ident[0:S, 0:S]).then_inc(z.coefT_ready, 1)

        @block.scalar
        def _(act):
            with act.Fori(0, PAIRS) as pair:
                lanes = lanes_of(act, pair)
                for lane, b, n in lanes:
                    act.wait_ge(z.yT_ready, n)
                    nc.scalar.copy(u.yT[:, lane, :, :], bank(lane, 0)[:, 0:DC * S].rearrange("p (c s) -> p c s", s=S)).then_inc(z.yT, 1)
                for lane, b, n in lanes:
                    act.wait_ge(z.gmax, n)
                    nc.scalar.activation(u.gexp[:, lane, :], u.gates[:, lane, :], ACT.Exp, bias=u.gmax[:, lane, :]).then_inc(z.gexp, 1)
                for lane, b, n in lanes:
                    act.wait_ge(z.coefT_ready, n)
                    nc.scalar.copy(f.coefT[:, bass.ds(b * S, S)], bank(lane, 2)[0:EXPERTS, 0:S]).then_inc(z.coefT, 1)

        @block.vector
        def _(dve):
            dve.wait_ge(z.ones, 1)
            with dve.Fori(0, PAIRS) as pair:
                lanes = lanes_of(dve, pair)
                norm_stats(nc, dve, m1, lanes, lambda lane, b: g.x[:, b, :])
                for lane, b, n in lanes:
                    norm_apply(nc, dve, m1, lane, n, u.y[:, lane, :], g.x[:, b, :], z.y)
                for lane, b, n in lanes:
                    dve.wait_ge(z.gates_ready, n)
                    nc.vector.tensor_copy(u.gates[:, lane, :], bank(lane, 1)[0:S, 0:NE]).then_inc(z.gates, 1)
                for lane, b, n in lanes:
                    dve.wait_ge(z.gates, n)
                    nc.vector.reduce_max(u.gmax[:, lane, :], u.gates[:, lane, :], AX.X, negate=True).then_inc(z.gmax, 1)
                top_two(nc, dve, g, lanes, u, z, u.gates)
                for lane, b, n in lanes:
                    dve.wait_ge(z.rank, n)
                    dve.wait_ge(z.gexp, n)
                    nc.vector.scalar_tensor_tensor(u.chosen[:, lane, :], u.rank[:, lane, :], 2.0, u.gexp[:, lane, :], ALU.is_lt, ALU.mult).then_inc(z.chosen, 1)
                for lane, b, n in lanes:
                    dve.wait_ge(z.chosen, n)
                    nc.vector.reduce_sum(u.gsum[:, lane, :], u.chosen[:, lane, :], AX.X).then_inc(z.gsum, 1)
                for lane, b, n in lanes:
                    dve.wait_ge(z.gsum, n)
                    nc.vector.reciprocal(u.grec[:, lane, :], u.gsum[:, lane, :]).then_inc(z.grec, 1)
                for lane, b, n in lanes:
                    dve.wait_ge(z.grec, n)
                    nc.vector.tensor_scalar(u.coef[:, lane, 1:EXPERTS], u.chosen[:, lane, :], u.grec[:, lane, :], None, ALU.mult).then_inc(z.coef, 1)


def experts_phase(nc, g, w, f, w1_in, w2_in):
    with ExitStack() as ctx:
        s = semaphores(nc, ctx, "moe", "row gate gate_ready hidden_ready hidden out_ready0 out_ready1 scaled0 scaled1 added0 added1")
        w_loaded = [ctx.enter_context(nc.semaphore(f"moe_w_loaded{k}")) for k in range(RING)]
        t = buffers(nc, ctx, "moe", w1=[P, RING, DC, HID], w2=[P, RING, HM, D], row=[EXPERTS, LANES, UT], hidden=[P, LANES, HM, UT],
                    scaled=[P, LANES, DC, UT], gate=[P, LANES, UT])
        HB = 4
        out_ready, scaled, added = (s.out_ready0, s.out_ready1), (s.scaled0, s.scaled1), (s.added0, s.added1)
        block = ctx.enter_context(nc.Block())
        UPAIRS = UNITS // LANES

        def units(eng, turn_, k, pair):
            base = turn_ * (RING * UNITS) + pair * LANES
            return [(lane, eng.snap(pair * LANES + lane), eng.snap(base + (k * UNITS + lane))) for lane in range(LANES)]

        @block.sync
        def _(sp):
            def load(k, e):
                sp.dma_start(t.w1[:, k, :, :], w1_in[e]).then_inc(w_loaded[k], 16)
                sp.dma_start(t.w2[:, k, :, :], w2_in[e]).then_inc(w_loaded[k], 16)

            for k in range(RING):
                load(k, k)
            with sp.Fori(1, EXPERTS // RING) as turn_:
                for k in range(RING):
                    sp.wait_ge(s.out_ready1, sp.snap((turn_ - 1) * (RING * UNITS) + (k + 1) * UNITS))
                    load(k, sp.snap(turn_ * RING + k))

        @block.tensor
        def _(pe):
            with pe.Fori(0, EXPERTS // RING) as turn_:
                for k in range(RING):
                    with pe.Fori(0, UPAIRS) as pair:
                        todo = units(pe, turn_, k, pair)
                        pe.wait_ge(w_loaded[k], pe.snap(turn_ * 32 + 32))
                        for lane, unit, n in todo:
                            for m in range(HM):
                                if m >= HB or lane > 0:
                                    pe.wait_ge(s.hidden, pe.snap(n * HM + (m - HB + 1)))
                                for c in range(DC):
                                    last = nc.tensor.matmul(g.psum[:, m % HB, 0:UT], t.w1[:, k, c, m * P:(m + 1) * P],
                                                            f.yT[:, c, bass.ds(unit * UT, UT)], start=(c == 0), stop=(c == DC - 1))
                                last.then_inc(s.hidden_ready, 1)
                            pe.wait_ge(s.row, pe.snap(n + 1))
                            nc.tensor.matmul(g.psum[:, 6 + lane, 0:UT], g.ones[0:EXPERTS, :], t.row[:, lane, :], start=True, stop=True).then_inc(s.gate_ready, 1)
                        for lane, unit, n in todo:
                            pe.wait_ge(s.hidden, pe.snap(n * HM + HM))
                            for c in range(DC):
                                if lane > 0:
                                    pe.wait_ge(scaled[c], n)
                                for m in range(HM):
                                    last = nc.tensor.matmul(g.psum[:, 4 + c, 0:UT], t.w2[:, k, m, c * P:(c + 1) * P], t.hidden[:, lane, m, :],
                                                            start=(m == 0), stop=(m == HM - 1))
                                last.then_inc(out_ready[c], 1)

        @block.scalar
        def _(act):
            with act.Fori(0, EXPERTS // RING) as turn_:
                for k in range(RING):
                    with act.Fori(0, UPAIRS) as pair:
                        for lane, unit, n in units(act, turn_, k, pair):
                            for m in range(HM):
                                act.wait_ge(s.hidden_ready, act.snap(n * HM + (m + 1)))
                                nc.scalar.activation(t.hidden[:, lane, m, :], g.psum[:, m % HB, 0:UT], ACT.Silu).then_inc(s.hidden, 1)

        @block.gpsimd
        def _(pool):
            with pool.Fori(0, EXPERTS // RING) as turn_:
                for k in range(RING):
                    with pool.Fori(0, UPAIRS) as pair:
                        for lane, unit, n in units(pool, turn_, k, pair):
                            for c in range(DC):
                                pool.wait_ge(scaled[c], pool.snap(n + 1))
                                part = f.sum[:, c, bass.ds(unit * UT, UT)]
                                nc.gpsimd.tensor_tensor(part, part, t.scaled[:, lane, c, :], ALU.add).then_inc(added[c], 1)

        @block.vector
        def _(dve):
            with dve.Fori(0, EXPERTS // RING) as turn_:
                for k in range(RING):
                    with dve.Fori(0, UPAIRS) as pair:
                        todo = units(dve, turn_, k, pair)
                        for lane, unit, n in todo:
                            nc.vector.tensor_scalar(t.row[:, lane, :], f.coefT[:, bass.ds(unit * UT, UT)], g.ident[0:EXPERTS, turn_ * RING + k].unsqueeze(1), None,
                                                    ALU.mult).then_inc(s.row, 1)
                        for lane, unit, n in todo:
                            dve.wait_ge(s.gate_ready, dve.snap(n + 1))
                            nc.vector.tensor_copy(t.gate[:, lane, :], g.psum[:, 6 + lane, 0:UT]).then_inc(s.gate, 1)
                            dve.wait_ge(s.gate, dve.snap(n + 1))
                            for c in range(DC):
                                dve.wait_ge(out_ready[c], dve.snap(n + 1))
                                nc.vector.tensor_tensor(t.scaled[:, lane, c, :], g.psum[:, 4 + c, 0:UT], t.gate[:, lane, :], ALU.mult).then_inc(scaled[c], 1)
                        dve.wait_ge(added[DC - 1], dve.snap(todo[-1][2] + 1))


def finish_phase(nc, g, f, out):
    with ExitStack() as ctx:
        s = semaphores(nc, ctx, "finish", "part turned_ready rows")
        stored = [ctx.enter_context(nc.semaphore(f"finish_stored{lane}")) for lane in range(LANES)]
        t = buffers(nc, ctx, "finish", part=[P, LANES, DC, S])
        bank = lambda lane, k: g.psum[:, lane * BANKS + k, :]
        block = ctx.enter_context(nc.Block())

        @block.gpsimd
        def _(pool):
            for b in range(LANES):
                nc.gpsimd.tensor_copy(t.part[:, b, :, :], f.sum[:, :, b * S:(b + 1) * S]).then_inc(s.part, 1)
            with pool.Fori(1, PAIRS) as pair:
                for lane, b, n in lanes_of(pool, pair):
                    pool.wait_ge(s.rows, pool.snap(b - 1))
                    nc.gpsimd.tensor_copy(t.part[:, lane, :, :], f.sum[:, :, bass.ds(b * S, S)]).then_inc(s.part, 1)

        @block.tensor
        def _(pe):
            with pe.Fori(0, PAIRS) as pair:
                for lane, b, n in lanes_of(pe, pair):
                    pe.wait_ge(s.part, n)
                    for c in range(DC):
                        last = nc.tensor.transpose(bank(lane, 0)[0:S, c * P:(c + 1) * P], t.part[:, lane, c, :], g.ident[:, :])
                    last.then_inc(s.turned_ready, 1)

        @block.vector
        def _(dve):
            with dve.Fori(0, PAIRS) as pair:
                for lane, b, n in lanes_of(dve, pair):
                    dve.wait_ge(s.turned_ready, n)
                    nc.vector.tensor_tensor(g.x[:, b, :], g.x[:, b, :], bank(lane, 0)[0:S, 0:D], ALU.add).then_inc(s.rows, 1)

        @block.sync
        def _(sp):
            with sp.Fori(0, PAIRS) as pair:
                for lane, b, n in lanes_of(sp, pair):
                    sp.wait_ge(s.rows, n)
                    sp.dma_start(out[b], g.x[:, b, :]).then_inc(stored[lane], 16)
            for lane in range(LANES):
                sp.wait_ge(stored[lane], 16 * PAIRS)


def clear_semaphores(nc):
    with nc.Block() as block:
        @block.gpsimd
        def _(pool):
            nc.gpsimd.sem_clear(range(min(nc.free_semaphores), max(nc.free_semaphores) + 1))


def decoder(nc, i, out):
    with ExitStack() as ctx:
        sb = lambda n, shape, dt=F32: ctx.enter_context(nc.sbuf_tensor(n, shape, dt))
        g = Fields(x=sb("x", [S, B, D]), ident=sb("ident", [P, P]), ident_b=sb("ident_b", [P, P], BF16),
                            causal=sb("causal", [S, QT * S], BF16), half_scaled=sb("half_scaled", [P, 2]), ones=sb("ones", [NH, P]),
                            before=sb("before", [S, NE, NE]), eps=sb("eps", [P, 1]), neg_half=sb("neg_half", [P, 32]))
        g.psum = ctx.enter_context(nc.psum_tensor("banks", [P, 8, BANK], F32))
        sets = "first cross mix rot wide moe"
        g.loaded = Fields(**{n: ctx.enter_context(nc.semaphore("loaded_" + n)) for n in sets.split() + ["filled"]})
        g.total = Fields(**{n: 0 for n in sets.split()})
        g.loads = []

        def load(which, dst, src):
            g.loads.append((g.loaded[which], dst, src))
            g.total[which] += 16

        def weight(stack, which, name, shape, dt=F32):
            dst = stack.enter_context(nc.sbuf_tensor("w_" + name, shape, dt))
            load(which, dst[tuple(slice(None) for _ in shape)], i[name])
            return dst

        with ExitStack() as late, ExitStack() as early:
            moe_w = Fields(gate=sb("w_moe_gate", [P, DC, NE]))
            load("moe", moe_w.gate[:, :, :], i["moe_gate"])
            wide_w = Fields(mask=weight(late, "wide", "wide_mask", [S, CTX], U8), **{n: weight(late, "wide", "wide_" + n, shape) for n, shape in dict(
                q=[P, DC, WI], k0=[P, WI], k1=[CD - P, WI], v0=[P, WI], v1=[CD - P, WI], proj=[P, WM, D], proj_b=[1, D], ln=[P, 2 * DC]).items()})
            wide_loads, g.loads = g.loads, []
            load("first", g.x[:, 0:2, :], i["x"][0:2].rearrange("b s d -> s b d"))
            for n in ("ident", "ident_b", "causal", "half_scaled", "ones", "before"):
                t = g[n]
                load("first", t[tuple(slice(None) for _ in t.shape)], i[n].bitcast(t.dtype))
            self_w = Fields(qkv=weight(early, "first", "self_qkv", [P, DC, 3 * D]), proj=weight(early, "first", "self_proj", [P, DC, D]))
            load("first", g.x[:, 2:B, :], i["x"][2:B].rearrange("b s d -> s b d"))
            cross_w = Fields(**{n: weight(early, "cross", "cross_" + n, shape) for n, shape in dict(
                q=[P, DC, D], kv0=[P, 2 * D], kv1=[CD - P, 2 * D], lkv=[P, DC, 2 * D], proj=[P, DC, D], proj_b=[1, D], ln_l=[P, 2 * DC],
                ln_x0=[P, 2], ln_x1=[CD - P, 2], qn_g=[P, 1], kn_g=[P, 1]).items()}, mask=weight(early, "cross", "cross_mask", [B, CTX], U8))
            mix_w = Fields(**{n: weight(early, "mix", "mix_" + n, shape) for n, shape in dict(
                qkv=[P, DC, 3 * D], in_b=[P, 3 * DC], proj=[P, DC, D], proj_b=[1, D], gate=[P, DC, NE], gate_b=[1, NE], expert=[P, DC, NE * D],
                expert_b=[NE, D], ln1_w=[S, D], ln1_b=[S, D], ln2_w=[S, D], ln2_b=[S, D], cos=[S, D], sin=[S, D]).items()})
            rot_w = Fields(**{n: weight(early, "rot", "rot_" + n, shape) for n, shape in dict(
                qkv=[P, DC, 3 * D], qk_b=[P, 2 * DC], v_b=[1, D], proj=[P, DC, D], proj_b=[1, D], w1=[P, D], b1=[P, DC], w2T=[NQ, 2, D],
                b2=[NQ, 2, S], hadamard=[NQ, NQ], rot=[S, 4, NH], half=[P, 2], uniform=[S, S]).items()})
            g.loads += wide_loads
            causal_phase(nc, g, self_w, False)
            clear_semaphores(nc)
            normed_cross_phase(nc, g, cross_w, i["ctx"])
            clear_semaphores(nc)
            causal_phase(nc, g, mix_w, True)
            clear_semaphores(nc)
            rotation_phase(nc, g, rot_w)
            early.close()
            clear_semaphores(nc)
            wide_cross_phase(nc, g, wide_w, i["ctxT"])
            late.close()
            f = Fields(yT=sb("moe_yT", [P, DC, B * S]), coefT=sb("moe_coefT", [EXPERTS, B * S]), sum=sb("moe_sum", [P, DC, B * S]))
            clear_semaphores(nc)
            gate_phase(nc, g, moe_w, f)
            clear_semaphores(nc)
            experts_phase(nc, g, moe_w, f, i["moe_w1"], i["moe_w2"])
            clear_semaphores(nc)
            finish_phase(nc, g, f, out)


def program(nc, arrays, out_shape):
    import concourse.mybir as mybir
    ins = {n: nc.dram_tensor(f"in_{n}", a.shape, mybir.dt.from_np(a.dtype), kind="ExternalInput").ap() for n, a in arrays.items()}
    out = nc.dram_tensor("out", out_shape, F32, kind="ExternalOutput").ap()
    decoder(nc, ins, out)



def constants():
    f = np.float32
    short = lambda v: (v.astype(f).view(np.uint32) >> 16).astype(np.uint16)
    i = np.arange(S)
    inv = (1.0 / f(10000.0) ** (np.arange(0, HD, 2, dtype=f) / f(HD))).astype(f)
    ang = (i.astype(f)[:, None] * inv[None, :]).astype(f)
    cos, sin = np.cos(ang).astype(f), np.sin(ang).astype(f)
    half = (np.arange(P)[:, None] // HD % 2 == np.arange(2)[None, :]).astype(f)
    e = np.arange(NE)
    return dict(
        ident=np.eye(P, dtype=f), ident_b=short(np.eye(P, dtype=f)),
        causal=short(np.tile(np.where(i[None, :] > i[:, None], f(MASKED), f(0)), (1, QT))),
        half_scaled=half * f(HD ** -0.5), rot_half=half, rot_uniform=np.full((S, S), 1.0 / S, f), ones=np.ones((NH, P), f),
        before=np.broadcast_to((e[None, :] < e[:, None]).astype(f), (S, NE, NE)).copy(),
        mix_cos=np.tile(np.repeat(cos, 2, axis=1), (1, NH)), mix_sin=np.tile(np.stack([-sin, sin], -1).reshape(S, HD), (1, NH)))


def kernel(**inputs):
    import concourse.bacc as bacc
    from concourse.bass_utils import run_bass_kernel_spmd

    a = {n: np.asarray(v) for n, v in inputs.items()}
    rows = lambda m: np.ascontiguousarray(m.reshape(m.shape[0] // P, P, m.shape[1]).transpose(1, 0, 2))
    cols = lambda v: np.ascontiguousarray(v.reshape(-1, P).T)
    wide = lambda v: np.ascontiguousarray(np.broadcast_to(v, (S, v.shape[-1])))
    arrays = dict(constants(), x=a["x"],
        self_qkv=rows(a["L0_attn_w_qkv"]), self_proj=rows(a["L0_attn_w_proj"]),
        mix_qkv=rows(a["L0_ffn_in_proj_w"].T), mix_in_b=cols(a["L0_ffn_in_proj_b"]), mix_proj=rows(a["L0_ffn_out_proj_w"].T),
        mix_proj_b=a["L0_ffn_out_proj_b"].reshape(1, D), mix_gate=rows(a["L0_ffn_gate_w"].T), mix_gate_b=a["L0_ffn_gate_b"].reshape(1, NE),
        mix_expert=rows(a["L0_ffn_expert_w"].transpose(2, 0, 1).reshape(D, NE * D)), mix_expert_b=a["L0_ffn_expert_b"],
        mix_ln1_w=wide(a["L0_ffn_ln1_w"]), mix_ln1_b=wide(a["L0_ffn_ln1_b"]), mix_ln2_w=wide(a["L0_ffn_ln2_w"]), mix_ln2_b=wide(a["L0_ffn_ln2_b"]),
        ctx=a["ctx_768"], cross_mask=a["mask_BxS2_bk0"],
        cross_q=rows(a["L0_xattn_Wq"].T), cross_kv0=np.ascontiguousarray(a["L0_xattn_Wkv"].T[0:P]), cross_kv1=np.ascontiguousarray(a["L0_xattn_Wkv"].T[P:CD]),
        cross_lkv=rows(a["L0_xattn_Wlkv"].T), cross_proj=rows(a["L0_xattn_Wo"].T), cross_proj_b=a["L0_xattn_bo"].reshape(1, D),
        cross_ln_l=np.concatenate([cols(a["L0_xattn_ln_l_g"]), cols(a["L0_xattn_ln_l_b"])], 1),
        cross_ln_x0=np.stack([a["L0_xattn_ln_x_g"][0:P], a["L0_xattn_ln_x_b"][0:P]], 1), cross_ln_x1=np.stack([a["L0_xattn_ln_x_g"][P:], a["L0_xattn_ln_x_b"][P:]], 1),
        cross_qn_g=np.tile(a["L0_xattn_qn_g"], P // XD).reshape(P, 1), cross_kn_g=np.tile(a["L0_xattn_kn_g"], P // XD).reshape(P, 1),
        rot_qkv=rows(np.concatenate([a["L1_attn_wq"], a["L1_attn_wk"], a["L1_attn_wv"]], 1)),
        rot_qk_b=np.concatenate([cols(a["L1_attn_bq"]), cols(a["L1_attn_bk"])], 1), rot_v_b=a["L1_attn_bv"].reshape(1, D),
        rot_proj=rows(a["L1_attn_wo"]), rot_proj_b=a["L1_attn_bo"].reshape(1, D), rot_w1=np.tile(a["L1_attn_w1"], (P // HD, 1)),
        rot_b1=cols(a["L1_attn_b1"]), rot_w2T=np.ascontiguousarray(a["L1_attn_w2"].T.reshape(2, NQ, D).transpose(1, 0, 2)),
        rot_b2=np.ascontiguousarray(np.broadcast_to(a["L1_attn_b2"].reshape(2, NQ).T[:, :, None], (NQ, 2, S))), rot_hadamard=a["L1_attn_hadamard"],
        rot_rot=np.ascontiguousarray(np.broadcast_to(a["L1_attn_rot"][:, :NQ // 2, 0].T, (S, NQ // 2, NH))),
        ctxT=np.ascontiguousarray(a["ctx_768"].transpose(2, 0, 1)), wide_mask=a["mask_1x1xSxS2_bk0"].reshape(S, CTX),
        wide_q=rows(a["L1_xattn_Wq"]), wide_k0=a["L1_xattn_Wkv"][0:P, 0:WI], wide_k1=a["L1_xattn_Wkv"][P:CD, 0:WI],
        wide_v0=a["L1_xattn_Wkv"][0:P, WI:], wide_v1=a["L1_xattn_Wkv"][P:CD, WI:], wide_proj=rows(a["L1_xattn_Wo"]),
        wide_proj_b=a["L1_xattn_bo"].reshape(1, D), wide_ln=np.concatenate([cols(a["L1_xattn_ln_gamma"]), cols(a["L1_xattn_ln_beta"])], 1),
        moe_gate=rows(a["L1_ffn_gate_w"].T),
        moe_w1=np.stack([rows(m.T) for m in [a["L1_ffn_shared_w1"], *a["L1_ffn_experts_w1"]]]),
        moe_w2=np.stack([rows(m.T) for m in [a["L1_ffn_shared_w2"], *a["L1_ffn_experts_w2"]]]),
    )
    arrays = {n: np.ascontiguousarray(v) for n, v in arrays.items()}
    nc = bacc.Bacc("TRN2", target_bir_lowering=False, num_devices=1)
    program(nc, arrays, (B, S, D))
    r = run_bass_kernel_spmd(nc, [{f"in_{n}": v for n, v in arrays.items()}], core_ids=[0])
    return r.results[0]["out"]
```

```python
from contextlib import ExitStack

import numpy as np

import concourse.bass as bass
from concourse import mybir

ALU = mybir.AluOpType
ACT = mybir.ActivationFunctionType
AX = mybir.AxisListType
F32 = mybir.dt.float32
BF16 = mybir.dt.bfloat16
U8 = mybir.dt.uint8
I32 = mybir.dt.int32

B, S, D = 32, 100, 256
P = 128
DC = D // P
CTX, CD = 361, 192
NH, HD = 16, 16
ROWS = 32
RG = P // ROWS
XH, XD = 4, 64
WH, WD = 16, 64
WI = WH * WD
WM = WI // P
NE = 8
HID = 4 * D
HM = HID // P
LANES = 2
PAIRS = B // LANES
BANK = 512
BANKS = 8 // LANES
MASKED = -1e30
CTX_TILES = [(0, P), (P, P), (2 * P, CTX - 2 * P)]
NT = len(CTX_TILES)
CTX_CHUNKS = [(0, P), (P, CD - P)]
QT = NH // RG


class Fields(dict):

    def __getattr__(self, name):
        return self[name]


def head_at(r, e, c):
    return 2 * RG * c + 2 * r + e


def semaphores(nc, ctx, phase, names):
    return Fields(**{n: ctx.enter_context(nc.semaphore(f"{phase}_{n}")) for n in names.split()})


def buffers(nc, ctx, phase, **shapes):
    return Fields(**{n: ctx.enter_context(nc.sbuf_tensor(f"{phase}_{n}", s, F32)) for n, s in shapes.items()})


def lanes_of(eng, pair):
    return [(lane, eng.snap(pair * LANES + lane), eng.snap(pair * LANES + lane + 1)) for lane in range(LANES)]



def norm_of(nc, ctx, name):
    m = buffers(nc, ctx, name, stats=[S, LANES, 6], meanvar=[S, LANES, 2], vareps=[S, LANES, 1], rstd=[S, LANES, 1], hold=[S, 1])
    m.done = semaphores(nc, ctx, name, "stats meanvar vareps rstd")
    return m


def norm_stats(nc, dve, m, lanes, rows):
    for lane, b, n in lanes:
        nc.vector.bn_stats(m.stats[:, lane, :], rows(lane, b)).then_inc(m.done.stats, 1)
    dve.wait_ge(m.done.stats, lanes[-1][2])
    nc.vector.memset(m.hold[:, :], 0.0)
    for lane, b, n in lanes:
        nc.vector.bn_aggr(m.meanvar[:, lane, :], m.stats[:, lane, :]).then_inc(m.done.meanvar, 1)


def norm_root(nc, pool, g, m, lane, n):
    pool.wait_ge(m.done.meanvar, n)
    nc.gpsimd.tensor_tensor(m.vareps[:, lane, :], m.meanvar[:, lane, 1:2], g.eps[0:S, :], ALU.add).then_inc(m.done.vareps, 1)
    pool.wait_ge(m.done.vareps, n)
    nc.gpsimd.tensor_tensor(m.rstd[:, lane, :], m.vareps[:, lane, :], g.neg_half[0:S, 0:1], ALU.pow).then_inc(m.done.rstd, 1)


def norm_apply(nc, dve, m, lane, n, out, rows, done):
    dve.wait_ge(m.done.rstd, n)
    nc.vector.tensor_scalar(out, rows, m.meanvar[:, lane, 0:1], m.rstd[:, lane, :], ALU.subtract, ALU.mult).then_inc(done, 1)


def turn(nc, g, out, rows, chunks):
    for c in range(chunks):
        last = nc.tensor.transpose(out[:, c * S:(c + 1) * S], rows[:, c * P:(c + 1) * P], g.ident[0:S, 0:S])
    return last



def causal_phase(nc, g, w, mixture):
    name = "mix" if mixture else "self"
    with ExitStack() as ctx:
        s = semaphores(nc, ctx, name, "y yT_ready yT qkv_ready q kv scores_ready rowmax shifted probs turned_ready "
                       "probsT_act probsT_dve heads_ready rowsum heads headsT_ready headsT proj_ready ones")
        t = buffers(nc, ctx, name, y=[S, LANES, D], yT=[P, LANES, 2 * DC, S], q=[P, LANES, 2, DC, S], k=[P, LANES, DC, S],
                    v=[S, LANES, NH, HD + 1], rowmax=[S, LANES, NH], probs=[S, LANES, RG, QT * S],
                    probsT=[S, LANES, RG, QT * S], rowsum=[S, LANES, NH], heads=[S, LANES, D], headsT=[P, LANES, DC, S])
        m1 = norm_of(nc, ctx, name + "_ln")
        if mixture:
            z = semaphores(nc, ctx, name, "rope_parts rope after x1_scaled x1 x1T_ready x1T gates_ready gmax gexp gsum grec gates "
                           "cmp ties behind rank coef coefT_ready coefT experts_ready last_ready normed moe_rows out_scaled out_shifted out")
            z.added = [ctx.enter_context(nc.semaphore(f"{name}_added{e}")) for e in range(NE)]
            u = buffers(nc, ctx, name + "_m", rope=[S, LANES, D], rope_a=[S, LANES, D], rope_b=[S, LANES, D], after=[S, LANES, D],
                        x1=[S, LANES, D], x1T=[P, LANES, DC, S], gmax=[S, LANES, 1], gexp=[S, LANES, NE], gsum=[S, LANES, 1],
                        grec=[S, LANES, 1], gates=[S, LANES, NE], above=[S, LANES, NE, NE], equal=[S, LANES, NE, NE],
                        rank=[S, LANES, NE], coef=[S, LANES, NE], coefT=[NE, LANES, S], sum=[S, LANES, D])
            m2, m3 = norm_of(nc, ctx, name + "_ln1"), norm_of(nc, ctx, name + "_ln2")
        bank = lambda lane, k: g.psum[:, lane * BANKS + k, :]
        banks = lambda lane, a, b: g.psum[:, lane * BANKS + a:lane * BANKS + b, :]
        block = ctx.enter_context(nc.Block())

        @block.sync
        def _(sp):
            if not mixture:
                for sem, dst, src in g.loads:
                    sp.dma_start(dst, src).then_inc(sem, 16)

        @block.gpsimd
        def _(pool):
            if not mixture:
                nc.gpsimd.memset(g.eps[:, :], 1e-5).then_inc(g.loaded.filled, 1)
                nc.gpsimd.memset(g.neg_half[:, :], -0.5).then_inc(g.loaded.filled, 1)
            pool.wait_ge(g.loaded.filled, 2)
            nc.gpsimd.memset(t.v[:, :, :, HD:HD + 1], 1.0).then_inc(s.ones, 1)
            if mixture:
                pool.wait_ge(g.loaded.mix, g.total.mix)
            with pool.Fori(0, PAIRS) as pair:
                lanes = lanes_of(pool, pair)
                for lane, b, n in lanes:
                    norm_root(nc, pool, g, m1, lane, n)
                if mixture:
                    for lane, b, n in lanes:
                        pool.wait_ge(s.y, n)
                        y2 = t.y[:, lane, :].rearrange("s (f two) -> s f two", two=2)
                        b2 = u.rope_b[:, lane, :].rearrange("s (f two) -> s f two", two=2)
                        sin2 = w.sin[:, :].rearrange("s (f two) -> s f two", two=2)
                        nc.gpsimd.tensor_tensor(u.rope_a[:, lane, :], t.y[:, lane, :], w.cos[:, :], ALU.mult)
                        nc.gpsimd.tensor_tensor(b2[:, :, 0], y2[:, :, 1], sin2[:, :, 0], ALU.mult)
                        nc.gpsimd.tensor_tensor(b2[:, :, 1], y2[:, :, 0], sin2[:, :, 1], ALU.mult).then_inc(z.rope_parts, 1)
                    for lane, b, n in lanes:
                        pool.wait_ge(z.rope_parts, n)
                        nc.gpsimd.tensor_tensor(u.rope[:, lane, :], u.rope_a[:, lane, :], u.rope_b[:, lane, :], ALU.add).then_inc(z.rope, 1)
                    for lane, b, n in lanes:
                        norm_root(nc, pool, g, m2, lane, n)
                    for lane, b, n in lanes:
                        pool.wait_ge(z.normed, n)
                        nc.gpsimd.tensor_tensor(u.after[:, lane, :], u.after[:, lane, :], w.ln1_w[:, :], ALU.mult).then_inc(z.x1_scaled, 1)
                    for lane, b, n in lanes:
                        pool.wait_ge(z.x1_scaled, n)
                        nc.gpsimd.tensor_tensor(u.x1[:, lane, :], u.after[:, lane, :], w.ln1_b[:, :], ALU.add).then_inc(z.x1, 1)
                    for lane, b, n in lanes:
                        norm_root(nc, pool, g, m3, lane, n)
                    for lane, b, n in lanes:
                        pool.wait_ge(z.out, n)
                        nc.gpsimd.tensor_tensor(u.sum[:, lane, :], u.sum[:, lane, :], w.ln2_w[:, :], ALU.mult).then_inc(z.out_scaled, 1)
                    for lane, b, n in lanes:
                        pool.wait_ge(z.out_scaled, n)
                        nc.gpsimd.tensor_tensor(u.sum[:, lane, :], u.sum[:, lane, :], w.ln2_b[:, :], ALU.add).then_inc(z.out_shifted, 1)
                    for lane, b, n in lanes:
                        pool.wait_ge(z.out_shifted, n)
                        nc.gpsimd.tensor_tensor(g.x[:, b, :], g.x[:, b, :], u.sum[:, lane, :], ALU.add)

        @block.tensor
        def _(pe):
            pe.wait_ge(g.loaded.first, g.total.first)
            pe.wait_ge(s.ones, 1)
            if mixture:
                pe.wait_ge(g.loaded.mix, g.total.mix)
            src = DC if mixture else 0
            with pe.Fori(0, PAIRS) as pair:
                lanes = lanes_of(pe, pair)
                for lane, b, n in lanes:
                    pe.wait_ge(s.y, n)
                    last = turn(nc, g, bank(lane, 0), t.y[:, lane, :], DC)
                    if mixture:
                        pe.wait_ge(z.rope, n)
                        last = turn(nc, g, bank(lane, 0)[:, DC * S:], u.rope[:, lane, :], DC)
                    last.then_inc(s.yT_ready, 1)
                for lane, b, n in lanes:
                    pe.wait_ge(s.yT, n)
                    for m in range(2 * DC):
                        for c in range(DC):
                            nc.tensor.matmul(bank(lane, 1 if m < DC else 3)[:, m % DC * S:(m % DC + 1) * S], w.qkv[:, c, m * P:(m + 1) * P],
                                             t.yT[:, lane, src + c, :], start=(c == 0), stop=(c == DC - 1))
                    for c in range(DC):
                        last = nc.tensor.matmul(bank(lane, 2)[0:S, 0:D], t.yT[:, lane, c, :], w.qkv[:, c, 2 * D:3 * D],
                                                start=(c == 0), stop=(c == DC - 1))
                    last.then_inc(s.qkv_ready, 1)
                for lane, b, n in lanes:
                    pe.wait_ge(s.q, n)
                    pe.wait_ge(s.kv, n)
                    for r in range(RG):
                        nc.tensor.matmul(bank(lane, r)[0:S, 0:QT * S], g.ident_b[0:S, 0:S], g.causal[:, :], start=True, stop=False)
                    for e in range(2):
                        for c in range(DC):
                            for r in range(RG):
                                rows, at = slice(ROWS * r, ROWS * (r + 1)), (e * DC + c) * S
                                last = nc.tensor.matmul(bank(lane, r)[0:S, at:at + S], t.q[rows, lane, e, c, :], t.k[rows, lane, c, :],
                                                        start=False, stop=(e == 1 and c == DC - 1))
                    last.then_inc(s.scores_ready, 1)
                for lane, b, n in lanes:
                    pe.wait_ge(s.probs, n)
                    for r in range(RG):
                        for j in range(QT):
                            last = nc.tensor.transpose(bank(lane, r)[0:S, j * S:(j + 1) * S], t.probs[:, lane, r, j * S:(j + 1) * S],
                                                       g.ident[0:S, 0:S])
                    last.then_inc(s.turned_ready, 1)
                for lane, b, n in lanes:
                    pe.wait_ge(s.probsT_act, n)
                    pe.wait_ge(s.probsT_dve, n)
                    for r in range(RG):
                        for e in range(2):
                            for c in range(DC):
                                h, at = head_at(r, e, c), (e * DC + c) * S
                                last = nc.tensor.matmul(bank(lane, 0)[0:S, h * (HD + 1):(h + 1) * (HD + 1)],
                                                        t.probsT[:, lane, r, at:at + S], t.v[:, lane, h, :], start=True, stop=True)
                    last.then_inc(s.heads_ready, 1)
                for lane, b, n in lanes:
                    pe.wait_ge(s.heads, n)
                    turn(nc, g, bank(lane, 1), t.heads[:, lane, :], DC).then_inc(s.headsT_ready, 1)
                for lane, b, n in lanes:
                    pe.wait_ge(s.headsT, n)
                    for c in range(DC):
                        last = nc.tensor.matmul(bank(lane, 2)[0:S, 0:D], t.headsT[:, lane, c, :], w.proj[:, c, :],
                                                start=(c == 0), stop=(not mixture and c == DC - 1))
                    if mixture:
                        last = nc.tensor.matmul(bank(lane, 2)[0:S, 0:D], g.ones[0:1, 0:S], w.proj_b[:, :], start=False, stop=True)
                    last.then_inc(s.proj_ready, 1)
                if mixture:
                    for lane, b, n in lanes:
                        pe.wait_ge(z.x1, n)
                        turn(nc, g, bank(lane, 3), u.x1[:, lane, :], DC).then_inc(z.x1T_ready, 1)
                    for lane, b, n in lanes:
                        pe.wait_ge(z.x1T, n)
                        for c in range(DC):
                            nc.tensor.matmul(bank(lane, 1)[0:S, 0:NE], u.x1T[:, lane, c, :], w.gate[:, c, :], start=(c == 0), stop=False)
                        nc.tensor.matmul(bank(lane, 1)[0:S, 0:NE], g.ones[0:1, 0:S], w.gate_b[:, :], start=False, stop=True).then_inc(z.gates_ready, 1)
                    for lane, b, n in lanes:
                        pe.wait_ge(z.coef, n)
                        nc.tensor.transpose(bank(lane, 3)[0:NE, 0:S], u.coef[:, lane, :], g.ident[0:S, 0:S]).then_inc(z.coefT_ready, 1)
                    for lane, b, n in lanes:
                        pe.wait_ge(z.coefT, n)
                        for k in range(3):
                            for c in range(DC):
                                nc.tensor.matmul(bank(lane, k)[0:S, :], u.x1T[:, lane, c, :], w.expert[:, c, k * BANK:(k + 1) * BANK],
                                                 start=(c == 0), stop=(c == DC - 1))
                        nc.tensor.matmul(bank(lane, 3)[0:S, 0:D], u.coefT[:, lane, :], w.expert_b[:, :], start=True, stop=True).then_inc(z.experts_ready, 1)
                    for lane, b, n in lanes:
                        pe.wait_ge(z.added[1], n)
                        for c in range(DC):
                            last = nc.tensor.matmul(bank(lane, 0)[0:S, :], u.x1T[:, lane, c, :], w.expert[:, c, 3 * BANK:4 * BANK],
                                                    start=(c == 0), stop=(c == DC - 1))
                        last.then_inc(z.last_ready, 1)

        @block.scalar
        def _(act):
            act.wait_ge(g.loaded.first, g.total.first)
            if mixture:
                act.wait_ge(g.loaded.mix, g.total.mix)
            with act.Fori(0, PAIRS) as pair:
                lanes = lanes_of(act, pair)
                for lane, b, n in lanes:
                    act.wait_ge(s.yT_ready, n)
                    k = 2 * DC if mixture else DC
                    nc.scalar.copy(t.yT[:, lane, 0:k, :], bank(lane, 0)[:, 0:k * S].rearrange("p (c s) -> p c s", s=S)).then_inc(s.yT, 1)
                for lane, b, n in lanes:
                    act.wait_ge(s.qkv_ready, n)
                    kk = bank(lane, 3)[:, 0:DC * S]
                    if mixture:
                        for c in range(DC):
                            nc.scalar.activation(t.k[:, lane, c, :], kk[:, c * S:(c + 1) * S], ACT.Identity, bias=w.in_b[:, DC + c:DC + c + 1])
                    else:
                        nc.scalar.copy(t.k[:, lane, :, :], kk.rearrange("p (c s) -> p c s", s=S))
                    nc.scalar.copy(t.v[:, lane, :, 0:HD], bank(lane, 2)[0:S, 0:D].rearrange("s (h d) -> s h d", d=HD)).then_inc(s.kv, 1)
                for lane, b, n in lanes:
                    act.wait_ge(s.shifted, n)
                    nc.scalar.activation(t.probs[:, lane, :, :], t.probs[:, lane, :, :], ACT.Exp).then_inc(s.probs, 1)
                for lane, b, n in lanes:
                    act.wait_ge(s.turned_ready, n)
                    nc.scalar.copy(t.probsT[:, lane, 0:2, :], banks(lane, 0, 2)[0:S, :, 0:QT * S]).then_inc(s.probsT_act, 1)
                for lane, b, n in lanes:
                    act.wait_ge(s.headsT_ready, n)
                    if mixture:
                        for c in range(DC):
                            last = nc.scalar.activation(t.headsT[:, lane, c, :], bank(lane, 1)[:, c * S:(c + 1) * S], ACT.Identity,
                                                        bias=w.in_b[:, 2 * DC + c:2 * DC + c + 1])
                    else:
                        last = nc.scalar.copy(t.headsT[:, lane, :, :], bank(lane, 1)[:, 0:DC * S].rearrange("p (c s) -> p c s", s=S))
                    last.then_inc(s.headsT, 1)
                if mixture:
                    for lane, b, n in lanes:
                        act.wait_ge(z.x1T_ready, n)
                        nc.scalar.copy(u.x1T[:, lane, :, :], bank(lane, 3)[:, 0:DC * S].rearrange("p (c s) -> p c s", s=S)).then_inc(z.x1T, 1)
                    for lane, b, n in lanes:
                        act.wait_ge(z.gmax, n)
                        nc.scalar.activation(u.gexp[:, lane, :], bank(lane, 1)[0:S, 0:NE], ACT.Exp, bias=u.gmax[:, lane, :]).then_inc(z.gexp, 1)
                    for lane, b, n in lanes:
                        act.wait_ge(z.coefT_ready, n)
                        nc.scalar.copy(u.coefT[:, lane, :], bank(lane, 3)[0:NE, 0:S]).then_inc(z.coefT, 1)

        @block.vector
        def _(dve):
            dve.wait_ge(g.loaded.first, g.total.first)
            if mixture:
                dve.wait_ge(g.loaded.mix, g.total.mix)
            with dve.Fori(0, PAIRS) as pair:
                lanes = lanes_of(dve, pair)
                norm_stats(nc, dve, m1, lanes, lambda lane, b: g.x[:, b, :])
                for lane, b, n in lanes:
                    norm_apply(nc, dve, m1, lane, n, t.y[:, lane, :], g.x[:, b, :], s.y)
                for lane, b, n in lanes:
                    dve.wait_ge(s.qkv_ready, n)
                    for e in range(2):
                        if mixture:
                            for c in range(DC):
                                last = nc.vector.tensor_scalar(t.q[:, lane, e, c, :], bank(lane, 1)[:, c * S:(c + 1) * S], w.in_b[:, c:c + 1],
                                                               g.half_scaled[:, e:e + 1], ALU.add, ALU.mult)
                        else:
                            last = nc.vector.tensor_scalar(t.q[:, lane, e, :, :], bank(lane, 1)[:, 0:DC * S].rearrange("p (c s) -> p c s", s=S),
                                                           g.half_scaled[:, e:e + 1], None, ALU.mult)
                    last.then_inc(s.q, 1)
                for lane, b, n in lanes:
                    dve.wait_ge(s.scores_ready, n)
                    sc = banks(lane, 0, RG)[0:S, :, 0:QT * S].rearrange("s r (j k) -> s r j k", k=S)
                    nc.vector.reduce_max(t.rowmax[:, lane, :].rearrange("s (r j) -> s r j", j=QT), sc, AX.X).then_inc(s.rowmax, 1)
                for lane, b, n in lanes:
                    dve.wait_ge(s.rowmax, n)
                    for r in range(RG):
                        last = nc.vector.tensor_tensor(t.probs[:, lane, r, :].rearrange("s (j k) -> s j k", k=S),
                                                       bank(lane, r)[0:S, 0:QT * S].rearrange("s (j k) -> s j k", k=S),
                                                       t.rowmax[:, lane, r * QT:(r + 1) * QT].unsqueeze(2).broadcast_to([S, QT, S]), ALU.subtract)
                    last.then_inc(s.shifted, 1)
                for lane, b, n in lanes:
                    dve.wait_ge(s.turned_ready, n)
                    nc.vector.tensor_copy(t.probsT[:, lane, 2:4, :], banks(lane, 2, 4)[0:S, :, 0:QT * S]).then_inc(s.probsT_dve, 1)
                for lane, b, n in lanes:
                    dve.wait_ge(s.heads_ready, n)
                    o = bank(lane, 0)[0:S, 0:NH * (HD + 1)].rearrange("s (h d) -> s h d", d=HD + 1)
                    nc.vector.reciprocal(t.rowsum[:, lane, :].unsqueeze(2), o[:, :, HD:HD + 1]).then_inc(s.rowsum, 1)
                for lane, b, n in lanes:
                    dve.wait_ge(s.rowsum, n)
                    o = bank(lane, 0)[0:S, 0:NH * (HD + 1)].rearrange("s (h d) -> s h d", d=HD + 1)
                    nc.vector.tensor_tensor(t.heads[:, lane, :].rearrange("s (h d) -> s h d", d=HD), o[:, :, 0:HD],
                                            t.rowsum[:, lane, :].unsqueeze(2).broadcast_to([S, NH, HD]), ALU.mult).then_inc(s.heads, 1)
                if not mixture:
                    for lane, b, n in lanes:
                        dve.wait_ge(s.proj_ready, n)
                        nc.vector.tensor_tensor(g.x[:, b, :], g.x[:, b, :], bank(lane, 2)[0:S, 0:D], ALU.add)
                else:
                    for lane, b, n in lanes:
                        dve.wait_ge(s.proj_ready, n)
                        nc.vector.tensor_tensor(u.after[:, lane, :], t.y[:, lane, :], bank(lane, 2)[0:S, 0:D], ALU.add).then_inc(z.after, 1)
                    dve.wait_ge(z.after, lanes[-1][2])
                    norm_stats(nc, dve, m2, lanes, lambda lane, b: u.after[:, lane, :])
                    for lane, b, n in lanes:
                        norm_apply(nc, dve, m2, lane, n, u.after[:, lane, :], u.after[:, lane, :], z.normed)
                    for lane, b, n in lanes:
                        dve.wait_ge(z.gates_ready, n)
                        nc.vector.reduce_max(u.gmax[:, lane, :], bank(lane, 1)[0:S, 0:NE], AX.X, negate=True).then_inc(z.gmax, 1)
                    for lane, b, n in lanes:
                        dve.wait_ge(z.gexp, n)
                        nc.vector.reduce_sum(u.gsum[:, lane, :], u.gexp[:, lane, :], AX.X).then_inc(z.gsum, 1)
                    for lane, b, n in lanes:
                        dve.wait_ge(z.gsum, n)
                        nc.vector.reciprocal(u.grec[:, lane, :], u.gsum[:, lane, :]).then_inc(z.grec, 1)
                    for lane, b, n in lanes:
                        dve.wait_ge(z.grec, n)
                        nc.vector.tensor_scalar(u.gates[:, lane, :], u.gexp[:, lane, :], u.grec[:, lane, :], None, ALU.mult).then_inc(z.gates, 1)
                    top_two(nc, dve, g, lanes, u, z, u.gates)
                    for lane, b, n in lanes:
                        dve.wait_ge(z.rank, n)
                        nc.vector.scalar_tensor_tensor(u.coef[:, lane, :], u.rank[:, lane, :], 2.0, u.gates[:, lane, :],
                                                       ALU.is_lt, ALU.mult).then_inc(z.coef, 1)
                    for e in range(NE):
                        for lane, b, n in lanes:
                            if e == 0:
                                dve.wait_ge(z.experts_ready, n)
                            elif e == NE - 2:
                                dve.wait_ge(z.last_ready, n)
                            if e > 0:
                                dve.wait_ge(z.added[e - 1], n)
                            k = e // 2 % 3
                            nc.vector.scalar_tensor_tensor(u.sum[:, lane, :], bank(lane, k)[0:S, e % 2 * D:(e % 2 + 1) * D], u.coef[:, lane, e:e + 1],
                                                           (u.sum if e else u.x1)[:, lane, :], ALU.mult, ALU.add).then_inc(z.added[e], 1)
                    for lane, b, n in lanes:
                        dve.wait_ge(z.added[NE - 1], n)
                        nc.vector.tensor_tensor(u.sum[:, lane, :], u.sum[:, lane, :], bank(lane, 3)[0:S, 0:D], ALU.add).then_inc(z.moe_rows, 1)
                    dve.wait_ge(z.moe_rows, lanes[-1][2])
                    norm_stats(nc, dve, m3, lanes, lambda lane, b: u.sum[:, lane, :])
                    for lane, b, n in lanes:
                        norm_apply(nc, dve, m3, lane, n, u.sum[:, lane, :], u.sum[:, lane, :], z.out)


def top_two(nc, dve, g, lanes, u, z, gates):
    for lane, b, n in lanes:
        dve.wait_ge(z.gates, n)
        mine = gates[:, lane, :].unsqueeze(2).broadcast_to([S, NE, NE])
        other = gates[:, lane, :].unsqueeze(1).broadcast_to([S, NE, NE])
        nc.vector.tensor_tensor(u.above[:, lane, :, :], other, mine, ALU.is_gt)
        nc.vector.tensor_tensor(u.equal[:, lane, :, :], other, mine, ALU.is_equal).then_inc(z.cmp, 1)
    for lane, b, n in lanes:
        dve.wait_ge(z.cmp, n)
        nc.vector.tensor_tensor(u.equal[:, lane, :, :], u.equal[:, lane, :, :], g.before[:, :, :], ALU.mult).then_inc(z.ties, 1)
    for lane, b, n in lanes:
        dve.wait_ge(z.ties, n)
        nc.vector.tensor_tensor(u.above[:, lane, :, :], u.above[:, lane, :, :], u.equal[:, lane, :, :], ALU.add).then_inc(z.behind, 1)
    for lane, b, n in lanes:
        dve.wait_ge(z.behind, n)
        nc.vector.reduce_sum(u.rank[:, lane, :], u.above[:, lane, :, :], AX.X).then_inc(z.rank, 1)



def normed_cross_phase(nc, g, w, ctx_in):
    KT = NT + 1
    KEYS = NT * P + S
    PAD = (CTX, NT * P)
    width = [P] * NT + [S]
    with ExitStack() as ctx:
        s = semaphores(nc, ctx, "cross", "zeroed ones bias gain y yy yT_ready lT cstats cmeanvar cvareps crstd cn ctxT_ready ctxT_act ctxT_dve "
                       "q_ready qsq qsum qclip qroot qn kv_ready kv_act ksum kclip kroot kn kqT_ready kT qT pick scores_ready rowmax "
                       "probs turned_ready probsT_act probsT_dve heads_ready rowsum heads headsT_ready headsT proj_ready")
        raw_loaded = [ctx.enter_context(nc.semaphore(f"cross_ctx_loaded{lane}")) for lane in range(LANES)]
        t = buffers(nc, ctx, "cross", y=[S, LANES, D], yy=[S, LANES, D], lT=[P, LANES, DC, P], raw=[P, LANES, NT, CD], cn=[P, LANES, NT, CD],
                    cstats=[P, LANES, NT, 6], cmeanvar=[P, LANES, NT, 2], cvareps=[P, LANES, NT], crstd=[P, LANES, NT], chold=[P, 1],
                    ctxT0=[P, LANES, NT * P], ctxT1=[CD - P, LANES, NT * P], qsq=[S, LANES, D], qsum=[S, LANES, XH], qclip=[S, LANES, XH],
                    qroot=[S, LANES, XH], ksum=[P, LANES, KT * XH], kclip=[P, LANES, KT * XH],
                    kroot=[P, LANES, KT * XH], v=[P, LANES, KT, XH, XD + 1], kT=[P, LANES, DC, KT * P], qT=[P, LANES, DC, S],
                    rowmax=[S, LANES, XH], probs=[P, LANES, XH, KEYS], probsT=[P, LANES, KT, XH * S], rowsum=[S, LANES, XH],
                    gain=[P, 1])
        t.kn = t.probs[:, :, :, :].rearrange("p l h k -> p l (h k)")[:, :, 0:KT * D].rearrange("p l (t d) -> p l t d", d=D)
        t.ksq, t.qn = t.kn, t.qsq
        t.heads, t.headsT = t.y, t.qT
        bias = ctx.enter_context(nc.sbuf_tensor("cross_bias", [B, KEYS], BF16))
        pick = ctx.enter_context(nc.sbuf_tensor("cross_pick", [B, LANES, S], BF16))
        m1, m2 = norm_of(nc, ctx, "cross_ln"), norm_of(nc, ctx, "cross_ln_l")
        bank = lambda lane, k: g.psum[:, lane * BANKS + k, :]
        banks = lambda lane, a, b: g.psum[:, lane * BANKS + a:lane * BANKS + b, :]
        block = ctx.enter_context(nc.Block())

        def load_ctx(sp, lane, b):
            whole = (NT - 1) * P
            sp.dma_start(t.raw[:, lane, 0:NT - 1, :], ctx_in[b, 0:whole, :].rearrange("(t p) d -> p t d", p=P)).then_inc(raw_loaded[lane], 16)
            sp.dma_start(t.raw[0:CTX - whole, lane, NT - 1, :], ctx_in[b, whole:CTX, :]).then_inc(raw_loaded[lane], 16)

        @block.sync
        def _(sp):
            sp.wait_ge(s.zeroed, 1)
            for lane in range(LANES):
                load_ctx(sp, lane, lane)
            with sp.Fori(1, PAIRS) as pair:
                for lane, b, n in lanes_of(sp, pair):
                    sp.wait_ge(s.cn, sp.snap(b - 1))
                    load_ctx(sp, lane, b)

        @block.gpsimd
        def _(pool):
            nc.gpsimd.memset(t.raw[:, :, NT - 1, :], 0.0).then_inc(s.zeroed, 1)
            nc.gpsimd.memset(t.lT[:, :, :, :], 0.0).then_inc(s.ones, 1)
            nc.gpsimd.memset(t.v[:, :, :, :, XD:XD + 1], 1.0).then_inc(s.ones, 1)
            nc.gpsimd.memset(bias[:, :], MASKED).then_inc(s.ones, 1)
            with pool.Fori(0, PAIRS) as pair:
                lanes = lanes_of(pool, pair)
                for lane, b, n in lanes:
                    norm_root(nc, pool, g, m1, lane, n)
                for lane, b, n in lanes:
                    nc.gpsimd.tensor_copy(pick[:, lane, :], g.ident_b[0:B, b].unsqueeze(1).broadcast_to([B, S])).then_inc(s.pick, 1)
                for lane, b, n in lanes:
                    norm_root(nc, pool, g, m2, lane, n)
                for lane, b, n in lanes:
                    pool.wait_ge(s.cmeanvar, n)
                    nc.gpsimd.tensor_tensor(t.cvareps[:, lane, :], t.cmeanvar[:, lane, :, 1], g.eps[:, :].broadcast_to([P, NT]), ALU.add).then_inc(s.cvareps, 1)
                for lane, b, n in lanes:
                    pool.wait_ge(s.cvareps, n)
                    nc.gpsimd.tensor_tensor(t.crstd[:, lane, :], t.cvareps[:, lane, :], g.neg_half[:, 0:NT], ALU.pow).then_inc(s.crstd, 1)
                for lane, b, n in lanes:
                    pool.wait_ge(s.qclip, n)
                    nc.gpsimd.tensor_tensor(t.qroot[:, lane, :], t.qclip[:, lane, :], g.neg_half[0:S, 0:XH], ALU.pow).then_inc(s.qroot, 1)
                for lane, b, n in lanes:
                    pool.wait_ge(s.kclip, n)
                    nc.gpsimd.tensor_tensor(t.kroot[:, lane, :], t.kclip[:, lane, :], g.neg_half[:, 0:KT * XH], ALU.pow).then_inc(s.kroot, 1)

        @block.tensor
        def _(pe):
            pe.wait_ge(g.loaded.cross, g.total.cross)
            pe.wait_ge(s.ones, 3)
            pe.wait_ge(s.bias, 2)
            with pe.Fori(0, PAIRS) as pair:
                lanes = lanes_of(pe, pair)
                for lane, b, n in lanes:
                    pe.wait_ge(s.yy, n)
                    turn(nc, g, bank(lane, 0), t.yy[:, lane, :], DC).then_inc(s.yT_ready, 1)
                for lane, b, n in lanes:
                    pe.wait_ge(s.lT, n)
                    for c in range(DC):
                        last = nc.tensor.matmul(bank(lane, 3)[0:S, 0:D], t.lT[:, lane, c, 0:S], w.q[:, c, :], start=(c == 0), stop=(c == DC - 1))
                    last.then_inc(s.q_ready, 1)
                for lane, b, n in lanes:
                    pe.wait_ge(s.cn, n)
                    for k, (c0, cw) in enumerate(CTX_CHUNKS):
                        for j in range(NT):
                            last = nc.tensor.transpose(bank(lane, 1 + k)[0:cw, j * P:(j + 1) * P], t.cn[:, lane, j, c0:c0 + cw], g.ident[:, :])
                    last.then_inc(s.ctxT_ready, 1)
                for lane, b, n in lanes:
                    pe.wait_ge(s.ctxT_act, n)
                    pe.wait_ge(s.ctxT_dve, n)
                    pe.wait_ge(s.qn, n)
                    for j in range(NT):
                        nc.tensor.matmul(bank(lane, j), t.ctxT0[:, lane, j * P:(j + 1) * P], w.kv0[:, :], start=True, stop=False)
                        nc.tensor.matmul(bank(lane, j), t.ctxT1[:, lane, j * P:(j + 1) * P], w.kv1[:, :], start=False, stop=True)
                    for c in range(DC):
                        last = nc.tensor.matmul(bank(lane, NT), t.lT[:, lane, c, :], w.lkv[:, c, :], start=(c == 0), stop=(c == DC - 1))
                    last.then_inc(s.kv_ready, 1)
                for lane, b, n in lanes:
                    pe.wait_ge(s.kn, n)
                    for c in range(DC):
                        for j in range(KT):
                            nc.tensor.transpose(bank(lane, c)[:, j * P:(j + 1) * P], t.kn[:, lane, j, c * P:(c + 1) * P], g.ident[:, :])
                    turn(nc, g, bank(lane, 2), t.qn[:, lane, :], DC).then_inc(s.kqT_ready, 1)
                for lane, b, n in lanes:
                    pe.wait_ge(s.kT, n)
                    pe.wait_ge(s.qT, n)
                    pe.wait_ge(s.pick, n)
                    for h in range(XH):
                        nc.tensor.matmul(bank(lane, h)[0:S, 0:KEYS], pick[:, lane, :], bias[:, :], start=True, stop=False)
                    for h in range(XH):
                        rows = slice(XD * (h % 2), XD * (h % 2 + 1))
                        last = nc.tensor.matmul(bank(lane, h)[0:S, 0:KEYS], t.qT[rows, lane, h // 2, :], t.kT[rows, lane, h // 2, 0:KEYS],
                                                start=False, stop=True)
                    last.then_inc(s.scores_ready, 1)
                for lane, b, n in lanes:
                    pe.wait_ge(s.probs, n)
                    for j in range(KT):
                        for h in range(XH):
                            last = nc.tensor.transpose(bank(lane, j)[0:width[j], h * S:(h + 1) * S],
                                                       t.probs[0:S, lane, h, j * P:j * P + width[j]], g.ident[0:S, 0:S])
                    last.then_inc(s.turned_ready, 1)
                for lane, b, n in lanes:
                    pe.wait_ge(s.probsT_act, n)
                    pe.wait_ge(s.probsT_dve, n)
                    for h in range(XH):
                        for j in range(KT):
                            last = nc.tensor.matmul(bank(lane, 0)[0:S, h * (XD + 1):(h + 1) * (XD + 1)], t.probsT[0:width[j], lane, j, h * S:(h + 1) * S],
                                                    t.v[0:width[j], lane, j, h, :], start=(j == 0), stop=(j == KT - 1))
                    last.then_inc(s.heads_ready, 1)
                for lane, b, n in lanes:
                    pe.wait_ge(s.heads, n)
                    turn(nc, g, bank(lane, 1), t.heads[:, lane, :], DC).then_inc(s.headsT_ready, 1)
                for lane, b, n in lanes:
                    pe.wait_ge(s.headsT, n)
                    for c in range(DC):
                        nc.tensor.matmul(bank(lane, 2)[0:S, 0:D], t.headsT[:, lane, c, :], w.proj[:, c, :], start=(c == 0), stop=False)
                    nc.tensor.matmul(bank(lane, 2)[0:S, 0:D], g.ones[0:1, 0:S], w.proj_b[:, :], start=False, stop=True).then_inc(s.proj_ready, 1)

        @block.scalar
        def _(act):
            act.wait_ge(g.loaded.cross, g.total.cross)
            act.wait_ge(s.ones, 3)
            with act.Fori(0, PAIRS) as pair:
                lanes = lanes_of(act, pair)
                for lane, b, n in lanes:
                    act.wait_ge(s.yT_ready, n)
                    for c in range(DC):
                        last = nc.scalar.activation(t.lT[:, lane, c, 0:S], bank(lane, 0)[:, c * S:(c + 1) * S], ACT.Identity,
                                                    bias=w.ln_l[:, DC + c:DC + c + 1], scale=w.ln_l[:, c:c + 1])
                    last.then_inc(s.lT, 1)
                for lane, b, n in lanes:
                    act.wait_ge(s.q_ready, n)
                    nc.scalar.activation(t.qsq[:, lane, :], bank(lane, 3)[0:S, 0:D], ACT.Square).then_inc(s.qsq, 1)
                for lane, b, n in lanes:
                    act.wait_ge(s.ctxT_ready, n)
                    nc.scalar.activation(t.ctxT0[:, lane, :], bank(lane, 1)[:, 0:NT * P], ACT.Identity,
                                         bias=w.ln_x0[:, 1:2], scale=w.ln_x0[:, 0:1]).then_inc(s.ctxT_act, 1)
                for lane, b, n in lanes:
                    act.wait_ge(s.kv_ready, n)
                    nc.scalar.activation(t.ksq[:, lane, :, :], banks(lane, 0, KT)[:, :, 0:D], ACT.Square)
                    nc.scalar.copy(t.v[:, lane, :, :, 0:XD], banks(lane, 0, KT)[:, :, D:2 * D].rearrange("p t (h d) -> p t h d", d=XD)).then_inc(s.kv_act, 1)
                for lane, b, n in lanes:
                    act.wait_ge(s.kqT_ready, n)
                    nc.scalar.copy(t.kT[:, lane, :, :], banks(lane, 0, DC)).then_inc(s.kT, 1)
                for lane, b, n in lanes:
                    act.wait_ge(s.rowmax, n)
                    for h in range(XH):
                        last = nc.scalar.activation(t.probs[0:S, lane, h, :], bank(lane, h)[0:S, 0:KEYS], ACT.Exp, bias=t.rowmax[:, lane, h:h + 1])
                    last.then_inc(s.probs, 1)
                for lane, b, n in lanes:
                    act.wait_ge(s.turned_ready, n)
                    nc.scalar.copy(t.probsT[:, lane, 0:2, :], banks(lane, 0, 2)[:, :, 0:XH * S]).then_inc(s.probsT_act, 1)
                for lane, b, n in lanes:
                    act.wait_ge(s.headsT_ready, n)
                    nc.scalar.copy(t.headsT[:, lane, :, :], bank(lane, 1)[:, 0:DC * S].rearrange("p (c s) -> p c s", s=S)).then_inc(s.headsT, 1)

        @block.vector
        def _(dve):
            dve.wait_ge(g.loaded.cross, g.total.cross)
            dve.wait_ge(s.ones, 3)
            nc.vector.tensor_scalar(bias[:, 0:CTX], w.mask[:, :], 1.0, -MASKED, ALU.subtract, ALU.mult).then_inc(s.bias, 1)
            nc.vector.memset(bias[:, NT * P:KEYS], 0.0).then_inc(s.bias, 1)
            nc.vector.scalar_tensor_tensor(t.gain[:, :], w.qn_g[:, :], XD ** -0.5, w.kn_g[:, :], ALU.mult, ALU.mult).then_inc(s.gain, 1)
            dve.wait_ge(s.gain, 1)
            with dve.Fori(0, PAIRS) as pair:
                lanes = lanes_of(dve, pair)
                norm_stats(nc, dve, m1, lanes, lambda lane, b: g.x[:, b, :])
                for lane, b, n in lanes:
                    dve.wait_ge(raw_loaded[lane], dve.snap(pair * 32 + 32))
                    for j in range(NT):
                        last = nc.vector.bn_stats(t.cstats[:, lane, j, :], t.raw[:, lane, j, :])
                    last.then_inc(s.cstats, 1)
                for lane, b, n in lanes:
                    norm_apply(nc, dve, m1, lane, n, t.y[:, lane, :], g.x[:, b, :], s.y)
                dve.wait_ge(s.y, lanes[-1][2])
                norm_stats(nc, dve, m2, lanes, lambda lane, b: t.y[:, lane, :])
                dve.wait_ge(s.cstats, lanes[-1][2])
                nc.vector.memset(t.chold[:, :], 0.0)
                for lane, b, n in lanes:
                    for j in range(NT):
                        last = nc.vector.bn_aggr(t.cmeanvar[:, lane, j, :], t.cstats[:, lane, j, :])
                    last.then_inc(s.cmeanvar, 1)
                for lane, b, n in lanes:
                    norm_apply(nc, dve, m2, lane, n, t.yy[:, lane, :], t.y[:, lane, :], s.yy)
                for lane, b, n in lanes:
                    dve.wait_ge(s.crstd, n)
                    for j in range(NT):
                        last = nc.vector.tensor_scalar(t.cn[:, lane, j, :], t.raw[:, lane, j, :], t.cmeanvar[:, lane, j, 0:1], t.crstd[:, lane, j:j + 1],
                                                       ALU.subtract, ALU.mult)
                    last.then_inc(s.cn, 1)
                for lane, b, n in lanes:
                    dve.wait_ge(s.qsq, n)
                    nc.vector.reduce_sum(t.qsum[:, lane, :], t.qsq[:, lane, :].rearrange("s (h d) -> s h d", d=XD), AX.X).then_inc(s.qsum, 1)
                for lane, b, n in lanes:
                    dve.wait_ge(s.qsum, n)
                    nc.vector.tensor_scalar(t.qclip[:, lane, :], t.qsum[:, lane, :], 1.0 / XD, 1e-16, ALU.mult, ALU.max).then_inc(s.qclip, 1)
                for lane, b, n in lanes:
                    dve.wait_ge(s.ctxT_ready, n)
                    nc.vector.tensor_scalar(t.ctxT1[:, lane, :], bank(lane, 2)[0:CD - P, 0:NT * P], w.ln_x1[:, 0:1], w.ln_x1[:, 1:2],
                                            ALU.mult, ALU.add).then_inc(s.ctxT_dve, 1)
                for lane, b, n in lanes:
                    dve.wait_ge(s.qroot, n)
                    nc.vector.tensor_tensor(t.qn[:, lane, :].rearrange("s (h d) -> s h d", d=XD), bank(lane, 3)[0:S, 0:D].rearrange("s (h d) -> s h d", d=XD),
                                            t.qroot[:, lane, :].unsqueeze(2).broadcast_to([S, XH, XD]), ALU.mult).then_inc(s.qn, 1)
                for lane, b, n in lanes:
                    dve.wait_ge(s.kv_act, n)
                    nc.vector.reduce_sum(t.ksum[:, lane, :], t.ksq[:, lane, :, :].rearrange("p t (h d) -> p (t h) d", d=XD), AX.X).then_inc(s.ksum, 1)
                for lane, b, n in lanes:
                    dve.wait_ge(s.ksum, n)
                    nc.vector.tensor_scalar(t.kclip[:, lane, :], t.ksum[:, lane, :], 1.0 / XD, 1e-16, ALU.mult, ALU.max).then_inc(s.kclip, 1)
                for lane, b, n in lanes:
                    dve.wait_ge(s.kroot, n)
                    nc.vector.tensor_tensor(t.kn[:, lane, :, :].rearrange("p t (h d) -> p t h d", d=XD),
                                            banks(lane, 0, KT)[:, :, 0:D].rearrange("p t (h d) -> p t h d", d=XD),
                                            t.kroot[:, lane, :].rearrange("p (t h) -> p t h", h=XH).unsqueeze(3).broadcast_to([P, KT, XH, XD]),
                                            ALU.mult).then_inc(s.kn, 1)
                for lane, b, n in lanes:
                    dve.wait_ge(s.kqT_ready, n)
                    nc.vector.tensor_scalar(t.qT[:, lane, :, :], bank(lane, 2)[:, 0:DC * S].rearrange("p (c s) -> p c s", s=S), t.gain[:, :], None,
                                            ALU.mult).then_inc(s.qT, 1)
                for lane, b, n in lanes:
                    dve.wait_ge(s.scores_ready, n)
                    nc.vector.reduce_max(t.rowmax[:, lane, :], banks(lane, 0, XH)[0:S, :, 0:KEYS], AX.X, negate=True).then_inc(s.rowmax, 1)
                for lane, b, n in lanes:
                    dve.wait_ge(s.turned_ready, n)
                    nc.vector.tensor_copy(t.probsT[:, lane, 2, :], bank(lane, 2)[:, 0:XH * S])
                    nc.vector.tensor_copy(t.probsT[0:S, lane, 3, :], bank(lane, 3)[0:S, 0:XH * S]).then_inc(s.probsT_dve, 1)
                for lane, b, n in lanes:
                    dve.wait_ge(s.heads_ready, n)
                    o = bank(lane, 0)[0:S, 0:XH * (XD + 1)].rearrange("s (h d) -> s h d", d=XD + 1)
                    nc.vector.reciprocal(t.rowsum[:, lane, :].unsqueeze(2), o[:, :, XD:XD + 1]).then_inc(s.rowsum, 1)
                for lane, b, n in lanes:
                    dve.wait_ge(s.rowsum, n)
                    o = bank(lane, 0)[0:S, 0:XH * (XD + 1)].rearrange("s (h d) -> s h d", d=XD + 1)
                    nc.vector.tensor_tensor(t.heads[:, lane, :].rearrange("s (h d) -> s h d", d=XD), o[:, :, 0:XD],
                                            t.rowsum[:, lane, :].unsqueeze(2).broadcast_to([S, XH, XD]), ALU.mult).then_inc(s.heads, 1)
                for lane, b, n in lanes:
                    dve.wait_ge(s.proj_ready, n)
                    nc.vector.tensor_tensor(g.x[:, b, :], g.x[:, b, :], bank(lane, 2)[0:S, 0:D], ALU.add)



TWO_PI_HI = float(np.float32(6.28125))
TWO_PI_LO = float(2 * np.pi - 6.28125)
PI_BELOW = float(np.nextafter(np.float32(np.pi), np.float32(0)))
NQ = 8


ROTATED = NH // RG
SETS = 2
GROUPS = [(lane, part) for part in (1, 0) for lane in range(LANES)]
VROWS = 32


def rotation_phase(nc, g, w):
    STEPS = len(GROUPS) * RG
    with ExitStack() as ctx:
        s = semaphores(nc, ctx, "rot", "filled folded_ready folded turns whole_i whole near angle size cosine sine k_bias y yT_ready yT mean_ready mean "
                       "k_norms_ready k_norms kT_ready kmin spread_in spread_ready ends q_norms_ready span inverse ratios ratio heads headsT_ready headsT "
                       "proj_ready added")
        each = lambda name, count: [ctx.enter_context(nc.semaphore(f"rot_{name}{k}")) for k in range(count)]
        qk_ready, q_kept, k_kept, v_ready, v_kept = (each(n, LANES) for n in ("qk_ready", "q_kept", "k_kept", "v_ready", "v_kept"))
        h_ready, h_done = each("tanh_in_ready", STEPS), each("tanh", STEPS)
        vectors_ready, turned, mixed_ready, squares = (each(n, len(GROUPS)) for n in ("vectors_ready", "turned", "mixed_ready", "squares"))
        t = buffers(nc, ctx, "rot", y=[S, LANES, D], yT=[P, LANES, DC, S], q=[P, SETS, LANES, 2, QT * S], v=[S, LANES, D],
                    h=[P, 2, DC, QT * S], w2=[P, DC, VROWS], b2=[P, 1], k_bias=[P, 2, DC], cos=[P, PAIRS, ROTATED], sin=[P, PAIRS, ROTATED],
                    turns=[P, 4, ROTATED], near=[P, 4, ROTATED], angle=[P, 4, ROTATED], size=[P, 4, ROTATED],
                    by_cos=[P, LANES, 2, QT * S], by_sin=[P, LANES, 2, QT * S], squares=[VROWS, LANES, 2, QT * S],
                    k_norms=[S, LANES, NH], k_ends=[NH, 2 * LANES], spread=[NH, 2 * LANES, NH], ends=[S, 2, LANES * NH], span=[S, 2, LANES * NH],
                    inverse=[S, 2, LANES * NH], ratios=[S, 2, LANES * NH], ratio=[S, LANES, NH], mean=[S, LANES, D], heads=[S, LANES, D],
                    headsT=[P, LANES, DC, S])
        whole = ctx.enter_context(nc.sbuf_tensor("rot_whole", [P, 4, ROTATED], I32))
        m1 = norm_of(nc, ctx, "rot_ln")
        tanh_in = lambda k, m: g.psum[:, k % 2 * DC + m, 0:QT * S]
        vec = lambda group: g.psum[:, 4 + group % 2, :]
        make, side = g.psum[:, 6, :], g.psum[:, 7, :]
        by_lane = lambda ps: ps[0:S, :].rearrange("s (l d) -> s l d", l=LANES)
        by_chunk = lambda ps: ps[:, 0:LANES * DC * S].rearrange("p (l c s) -> p l c s", l=LANES, c=DC)
        block = ctx.enter_context(nc.Block())

        def pair_of(eng, pair):
            fixed = isinstance(pair, int)
            at = (lambda e: e) if fixed else eng.snap
            return pair, at(pair + 1), [(lane, at(pair * LANES + lane), at(pair * LANES + lane + 1)) for lane in range(LANES)]

        def pairs(eng, run):
            with eng.Fori(0, PAIRS // SETS - 1) as two:
                some = [(k % SETS, *pair_of(eng, eng.snap(two * SETS + k))) for k in range(SETS + 1)]
                for k in range(SETS):
                    run(some[k], some[k + 1])
            ends = [(k % SETS, *pair_of(eng, PAIRS - SETS + k)) for k in range(SETS)]
            run(ends[0], ends[1])
            run(ends[1], None)

        FIRST = (0, *pair_of(None, 0))

        @block.gpsimd
        def _(pool):
            nc.gpsimd.memset(t.cos[:, :, :], 1.0).then_inc(s.filled, 1)
            nc.gpsimd.memset(t.sin[:, :, :], 0.0).then_inc(s.filled, 1)
            with pool.Fori(0, PAIRS) as pair:
                for lane, b, n in lanes_of(pool, pair):
                    norm_root(nc, pool, g, m1, lane, n)

        @block.tensor
        def _(pe):
            pe.wait_ge(g.loaded.rot, g.total.rot)
            for c in range(DC):
                nc.tensor.matmul(make[:, c * VROWS:(c + 1) * VROWS], w.w2T[:, c * P:(c + 1) * P], w.hadamard[:, 0:VROWS], start=True, stop=True)
            nc.tensor.matmul(side[:, 0:1], w.hadamard[:, :], w.b2[:, :], start=True, stop=True).then_inc(s.folded_ready, 1)
            pe.wait_ge(s.folded, 1)

            def make_rows(pr):
                pe.wait_ge(s.y, pr[3][-1][2])
                for lane in range(LANES):
                    last = turn(nc, g, make[:, lane * DC * S:], t.y[:, lane, :], DC)
                last.then_inc(s.yT_ready, 1)

            def make_qk(pr, lane):
                if lane == 0:
                    pe.wait_ge(s.yT, pr[2])
                else:
                    pe.wait_ge(q_kept[lane - 1], pr[2])
                    pe.wait_ge(k_kept[lane - 1], pr[2])
                for m in range(2 * DC):
                    for c in range(DC):
                        last = nc.tensor.matmul(make[:, m * S:(m + 1) * S], w.qkv[:, c, m * P:(m + 1) * P], t.yT[:, lane, c, :], start=(c == 0), stop=(c == DC - 1))
                last.then_inc(qk_ready[lane], 1)

            def make_v(pr, lane):
                if lane == 0:
                    pe.wait_ge(q_kept[LANES - 1], pr[2])
                    pe.wait_ge(k_kept[LANES - 1], pr[2])
                else:
                    pe.wait_ge(v_kept[lane - 1], pr[2])
                for c in range(DC):
                    nc.tensor.matmul(make[0:S, 0:D], t.yT[:, lane, c, :], w.qkv[:, c, 2 * D:3 * D], start=(c == 0), stop=False)
                nc.tensor.matmul(make[0:S, 0:D], g.ones[0:1, 0:S], w.v_b[:, :], start=False, stop=True).then_inc(v_ready[lane], 1)

            def mean(pr):
                pe.wait_ge(v_kept[LANES - 1], pr[2])
                last = nc.tensor.matmul(make[0:S, :], w.uniform[:, :], t.v[:, :, :].rearrange("s l d -> s (l d)"), start=True, stop=True)
                last.then_inc(s.mean_ready, 1)

            def first_layer(pr, k):
                group, r = k // RG, k % RG
                lane, part = GROUPS[group]
                if r == 0:
                    pe.wait_ge((k_kept if part else q_kept)[lane], pr[2])
                rows = slice(ROWS * r, ROWS * (r + 1))
                for m in range(DC):
                    last = nc.tensor.matmul(tanh_in(k, m), w.w1[rows, m * P:(m + 1) * P], t.q[rows, pr[0], lane, part, :], start=True, stop=True)
                last.then_inc(h_ready[k], 1)

            def last_layer(pr, k):
                group, r = k // RG, k % RG
                if r == 0 and group >= 2:
                    pe.wait_ge(turned[group - 2], pr[2])
                pe.wait_ge(h_done[k], pr[2])
                for m in range(DC):
                    last = nc.tensor.matmul(vec(group)[VROWS * r:VROWS * (r + 1), 0:QT * S], t.w2[:, m, :], t.h[:, k % 2, m, :], start=(m == 0), stop=(m == DC - 1))
                if r == RG - 1:
                    last.then_inc(vectors_ready[group], 1)

            def mix(pr, group, bank):
                lane, part = GROUPS[group]
                if lane == 0:
                    pe.wait_ge(turned[group], pr[2])
                    pe.wait_ge(turned[group + 1], pr[2])
                nc.tensor.matmul(bank[0:VROWS, 0:QT * S], w.real[:, :], t.by_cos[:, lane, part, :], start=True, stop=False)
                nc.tensor.matmul(bank[0:VROWS, 0:QT * S], w.imag[:, :], t.by_sin[:, 1 - lane, part, :], start=False, stop=True).then_inc(mixed_ready[group], 1)

            def norms(pr, part, ready):
                for lane in range(LANES):
                    pe.wait_ge(squares[GROUPS.index((lane, part))], pr[2])
                for lane in range(LANES):
                    for j in range(ROTATED):
                        at = (lane * ROTATED + j) * RG
                        last = nc.tensor.matmul(side[0:S, at:at + RG], t.squares[:, lane, part, j * S:(j + 1) * S], w.sum8[:, :], start=True, stop=True)
                last.then_inc(ready, 1)

            def run(pr, after):
                n = pr[2]
                for k in range(STEPS):
                    if 0 < k < STEPS - 1:
                        first_layer(pr, k + 1)
                    elif k == STEPS - 1 and after:
                        first_layer(after, 0)
                    if k == 0:
                        mean(pr)
                    elif k == 2 and after:
                        pe.wait_ge(s.mean, n)
                        make_rows(after)
                    elif k == 4 and after:
                        make_qk(after, 0)
                    elif k == 11:
                        norms(pr, 1, s.k_norms_ready)
                    elif k == 12:
                        pe.wait_ge(s.k_norms, n)
                        for lane in range(LANES):
                            last = nc.tensor.transpose(side[0:NH, lane * S:(lane + 1) * S], t.k_norms[:, lane, :], g.ident[0:S, 0:S])
                        last.then_inc(s.kT_ready, 1)
                    last_layer(pr, k)
                    if k == 8:
                        mix(pr, 0, side)
                    elif k == 9:
                        pe.wait_ge(squares[0], n)
                        mix(pr, 1, side)
                    elif k == 13:
                        pe.wait_ge(s.spread_in, n)
                        nc.tensor.matmul(side[0:S, 0:2 * LANES * NH], g.ones[0:NH, 0:S], t.spread[:, :, :].rearrange("h a b -> h (a b)"),
                                         start=True, stop=True).then_inc(s.spread_ready, 1)
                if after:
                    make_qk(after, 1)
                mix(pr, 2, vec(2))
                mix(pr, 3, vec(3))
                if after:
                    make_v(after, 0)
                pe.wait_ge(s.ends, n)
                norms(pr, 0, s.q_norms_ready)
                if after:
                    first_layer(after, 1)
                pe.wait_ge(s.heads, n)
                for lane in range(LANES):
                    last = turn(nc, g, vec(0)[:, lane * DC * S:], t.heads[:, lane, :], DC)
                last.then_inc(s.headsT_ready, 1)
                if after:
                    make_v(after, 1)
                pe.wait_ge(s.headsT, n)
                for lane in range(LANES):
                    rows = by_lane(vec(1))[:, lane, :]
                    for c in range(DC):
                        nc.tensor.matmul(rows, t.headsT[:, lane, c, :], w.proj[:, c, :], start=(c == 0), stop=False)
                    last = nc.tensor.matmul(rows, g.ones[0:1, 0:S], w.proj_b[:, :], start=False, stop=True)
                last.then_inc(s.proj_ready, 1)
                if after:
                    pe.wait_ge(s.added, n)

            make_rows(FIRST)
            for lane in range(LANES):
                make_qk(FIRST, lane)
            for lane in range(LANES):
                make_v(FIRST, lane)
            for k in range(2):
                first_layer(FIRST, k)
            pairs(pe, run)

        @block.scalar
        def _(act):
            act.wait_ge(s.filled, 2)
            act.wait_ge(s.angle, 1)
            nc.scalar.activation(t.sin[:, 0:NQ // 2, :], t.angle[:, :, :], ACT.Sin).then_inc(s.sine, 1)
            act.wait_ge(s.size, 2)
            nc.scalar.activation(t.cos[:, 0:NQ // 2, :], t.size[:, :, :], ACT.Sin).then_inc(s.cosine, 1)
            act.wait_ge(s.k_bias, 1)

            def keep_rows(pr):
                act.wait_ge(s.yT_ready, pr[2])
                nc.scalar.copy(t.yT[:, :, :, :], by_chunk(make)).then_inc(s.yT, 1)

            def keep_k(pr, lane):
                act.wait_ge(q_kept[lane], pr[2])
                for e in range(2):
                    for c in range(DC):
                        at = (e * DC + c) * S
                        last = nc.scalar.activation(t.q[:, pr[0], lane, 1, at:at + S], make[:, (DC + c) * S:(DC + c + 1) * S], ACT.Identity,
                                                    bias=t.k_bias[:, e, c:c + 1], scale=w.half[:, e:e + 1])
                last.then_inc(k_kept[lane], 1)

            def keep_v(pr, lane):
                act.wait_ge(v_ready[lane], pr[2])
                nc.scalar.copy(t.v[:, lane, :], make[0:S, 0:D]).then_inc(v_kept[lane], 1)

            def tanh(pr, k):
                act.wait_ge(h_ready[k], pr[2])
                for m in range(DC):
                    last = nc.scalar.activation(t.h[:, k % 2, m, :], tanh_in(k, m), ACT.Tanh, bias=w.b1[:, m:m + 1])
                last.then_inc(h_done[k], 1)

            def square(pr, group, bank):
                lane, part = GROUPS[group]
                act.wait_ge(mixed_ready[group], pr[2])
                nc.scalar.activation(t.squares[:, lane, part, :], bank[0:VROWS, 0:QT * S], ACT.Square).then_inc(squares[group], 1)

            def run(pr, after):
                n = pr[2]
                for k in range(STEPS):
                    if 0 < k < STEPS - 1:
                        tanh(pr, k + 1)
                    elif k == STEPS - 1 and after:
                        tanh(after, 0)
                    if k == 0:
                        act.wait_ge(s.mean_ready, n)
                        nc.scalar.copy(t.mean[:, :, :], by_lane(make)).then_inc(s.mean, 1)
                    elif k == 2 and after:
                        keep_rows(after)
                    elif k == 4 and after:
                        keep_k(after, 0)
                    elif k == 8:
                        square(pr, 0, side)
                    elif k == 9:
                        square(pr, 1, side)
                if after:
                    keep_k(after, 1)
                square(pr, 2, vec(2))
                square(pr, 3, vec(3))
                if after:
                    keep_v(after, 0)
                    tanh(after, 1)
                act.wait_ge(s.headsT_ready, n)
                nc.scalar.copy(t.headsT[:, :, :, :], by_chunk(vec(0))).then_inc(s.headsT, 1)
                if after:
                    keep_v(after, 1)

            keep_rows(FIRST)
            for lane in range(LANES):
                keep_k(FIRST, lane)
            for lane in range(LANES):
                keep_v(FIRST, lane)
            for k in range(2):
                tanh(FIRST, k)
            pairs(act, run)

        @block.vector
        def _(dve):
            dve.wait_ge(g.loaded.rot, g.total.rot)
            nc.vector.tensor_scalar(t.turns[:, :, :], w.rot[:, :, :], 0.25 / np.pi, None, ALU.mult).then_inc(s.turns, 1)
            dve.wait_ge(s.turns, 1)
            nc.vector.tensor_copy(whole[:, :, :], t.turns[:, :, :]).then_inc(s.whole_i, 1)
            dve.wait_ge(s.whole_i, 1)
            nc.vector.tensor_copy(t.turns[:, :, :], whole[:, :, :]).then_inc(s.whole, 1)
            nc.vector.tensor_scalar(t.near[:, :, :], w.rot[:, :, :], 0.5, None, ALU.mult).then_inc(s.whole, 1)
            dve.wait_ge(s.whole, 2)
            nc.vector.scalar_tensor_tensor(t.near[:, :, :], t.turns[:, :, :], -TWO_PI_HI, t.near[:, :, :], ALU.mult, ALU.add).then_inc(s.near, 1)
            dve.wait_ge(s.near, 1)
            nc.vector.scalar_tensor_tensor(t.near[:, :, :], t.turns[:, :, :], -TWO_PI_LO, t.near[:, :, :], ALU.mult, ALU.add).then_inc(s.near, 1)
            dve.wait_ge(s.near, 2)
            nc.vector.tensor_scalar(t.angle[:, :, :], t.near[:, :, :], PI_BELOW, -PI_BELOW, ALU.min, ALU.max).then_inc(s.angle, 1)
            dve.wait_ge(s.angle, 1)
            nc.vector.scalar_tensor_tensor(t.size[:, :, :], t.angle[:, :, :], -1.0, t.angle[:, :, :], ALU.mult, ALU.max).then_inc(s.size, 1)
            dve.wait_ge(s.size, 1)
            nc.vector.tensor_scalar(t.size[:, :, :], t.size[:, :, :], -1.0, float(np.pi / 2), ALU.mult, ALU.add).then_inc(s.size, 1)
            for e in range(2):
                last = nc.vector.tensor_scalar(t.k_bias[:, e, :], w.qk_b[:, DC:2 * DC], w.half[:, e:e + 1], None, ALU.mult)
            last.then_inc(s.k_bias, 1)
            dve.wait_ge(s.folded_ready, 1)
            nc.vector.tensor_copy(t.w2[:, :, :], make[:, 0:DC * VROWS].rearrange("p (c v) -> p c v", v=VROWS))
            nc.vector.tensor_copy(t.b2[:, :], side[:, 0:1]).then_inc(s.folded, 1)
            dve.wait_ge(s.folded, 1)
            dve.wait_ge(s.sine, 1)
            dve.wait_ge(s.cosine, 1)

            def stats(pr):
                norm_stats(nc, dve, m1, pr[3], lambda lane, b: g.x[:, b, :])

            def apply(pr):
                for lane, b, n in pr[3]:
                    norm_apply(nc, dve, m1, lane, n, t.y[:, lane, :], g.x[:, b, :], s.y)

            def keep_q(pr, lane):
                dve.wait_ge(qk_ready[lane], pr[2])
                for e in range(2):
                    for c in range(DC):
                        at = (e * DC + c) * S
                        last = nc.vector.tensor_scalar(t.q[:, pr[0], lane, 0, at:at + S], make[:, c * S:(c + 1) * S], w.qk_b[:, c:c + 1],
                                                       w.half[:, e:e + 1], ALU.add, ALU.mult)
                last.then_inc(q_kept[lane], 1)

            def turn_by(pr, group):
                lane, part = GROUPS[group]
                rows = vec(group)[:, 0:QT * S].rearrange("p (j s) -> p j s", s=S)
                dve.wait_ge(vectors_ready[group], pr[2])
                for table, out in ((t.cos, t.by_cos), (t.sin, t.by_sin)):
                    last = nc.vector.scalar_tensor_tensor(out[:, lane, part, :].rearrange("p (j s) -> p j s", s=S), rows, t.b2[:, :],
                                                          table[:, pr[1], :].unsqueeze(2).broadcast_to([P, ROTATED, S]), ALU.add, ALU.mult)
                last.then_inc(turned[group], 1)

            def run(pr, after):
                n = pr[2]
                if after:
                    stats(after)
                    apply(after)
                for k in range(STEPS):
                    if k == 4 and after:
                        keep_q(after, 0)
                    elif k == 11:
                        dve.wait_ge(s.k_norms_ready, n)
                        nc.vector.tensor_copy(t.k_norms[:, :, :].rearrange("s l h -> s (l h)"), side[0:S, 0:LANES * NH]).then_inc(s.k_norms, 1)
                    if k % RG == RG - 1:
                        turn_by(pr, k // RG)
                    if k == 12:
                        dve.wait_ge(s.kT_ready, n)
                        kT = side[0:NH, 0:LANES * S].rearrange("h (l s) -> h l s", s=S)
                        nc.vector.reduce_max(t.k_ends[:, 0:LANES], kT, AX.X)
                        nc.vector.tensor_reduce(t.k_ends[:, LANES:2 * LANES], kT, AX.X, ALU.min).then_inc(s.kmin, 1)
                        dve.wait_ge(s.kmin, n)
                        nc.vector.tensor_tensor(t.spread[:, :, :], g.ident[0:NH, 0:NH].unsqueeze(1).broadcast_to([NH, 2 * LANES, NH]),
                                                t.k_ends[:, :].unsqueeze(2).broadcast_to([NH, 2 * LANES, NH]), ALU.mult).then_inc(s.spread_in, 1)
                    elif k == 13:
                        dve.wait_ge(s.spread_ready, n)
                        nc.vector.tensor_copy(t.ends[:, :, :].rearrange("s k h -> s (k h)"), side[0:S, 0:2 * LANES * NH]).then_inc(s.ends, 1)
                if after:
                    keep_q(after, 1)
                dve.wait_ge(s.q_norms_ready, n)
                nc.vector.tensor_tensor(t.span[:, :, :], side[0:S, 0:LANES * NH].unsqueeze(1).broadcast_to([S, 2, LANES * NH]), t.ends[:, :, :],
                                        ALU.mult).then_inc(s.span, 1)
                dve.wait_ge(s.span, n)
                nc.vector.reciprocal(t.inverse[:, :, :], t.span[:, :, :]).then_inc(s.inverse, 1)
                dve.wait_ge(s.inverse, n)
                nc.vector.tensor_tensor(t.ratios[:, :, :], t.span[:, :, :], t.inverse[:, :, :], ALU.mult).then_inc(s.ratios, 1)
                dve.wait_ge(s.ratios, n)
                for lane in range(LANES):
                    least, most = (t.ratios[:, k, lane * NH:(lane + 1) * NH].rearrange("s (e c r) -> s e c r", e=2, c=DC) for k in range(2))
                    last = nc.vector.tensor_tensor(t.ratio[:, lane, :].rearrange("s (c r e) -> s e c r", c=DC, e=2), least, most, ALU.mult)
                last.then_inc(s.ratio, 1)
                dve.wait_ge(s.ratio, n)
                dve.wait_ge(s.mean, n)
                nc.vector.tensor_tensor(t.heads[:, :, :].rearrange("s l (h d) -> s (l h) d", d=HD), t.mean[:, :, :].rearrange("s l (h d) -> s (l h) d", d=HD),
                                        t.ratio[:, :, :].rearrange("s l h -> s (l h)").unsqueeze(2).broadcast_to([S, LANES * NH, HD]), ALU.mult).then_inc(s.heads, 1)
                dve.wait_ge(s.proj_ready, n)
                for lane, b, nb in pr[3]:
                    last = nc.vector.tensor_tensor(g.x[:, b, :], g.x[:, b, :], by_lane(vec(1))[:, lane, :], ALU.add)
                last.then_inc(s.added, 1)

            stats(FIRST)
            apply(FIRST)
            for lane in range(LANES):
                keep_q(FIRST, lane)
            pairs(dve, run)



WIDE_TILES = [(0, 121), (121, 120), (241, 120)]
ITEM = 2
ITEMS = WH // ITEM
KM = WM
MADE = [("k", 0), ("k", 1), ("k", 2), ("k", 3), ("y", 0), ("k", 4), ("k", 5), ("k", 6), ("k", 7), ("q", 0), ("q", 1)] + [
    ("v", 2 * j + half) for j in range(len(WIDE_TILES)) for half in range(2)]
NEXT_LAST = len(MADE) - 1
BETWEEN = 2 * (ITEMS - 2)
BY_ACT = lambda u: u % 2 == 0


def wide_cross_phase(nc, g, w, ctxT_in):
    TMAX = WIDE_TILES[0][1]
    with ExitStack() as ctx:
        s = semaphores(nc, ctx, "wide", "ones bias turned_zero any_key any_inverse any y headsT_ready headsT_act headsT_dve proj_ready added")
        made = [ctx.enter_context(nc.semaphore(f"wide_made_{k}{i}")) for k, i in MADE]
        kept = [ctx.enter_context(nc.semaphore(f"wide_kept_{k}{i}")) for k, i in MADE]
        a = [semaphores(nc, ctx, f"wide{i}", "scores_ready rowmax probs turned_ready probsT_act probsT_dve heads_ready rowsum heads") for i in range(ITEMS)]
        ctx_loaded = [ctx.enter_context(nc.semaphore(f"wide_ctx_loaded{lane}")) for lane in range(LANES)]
        t = buffers(nc, ctx, "wide", y=[S, LANES, D], yT=[P, LANES, DC, S], c0=[P, LANES, CTX], c1=[CD - P, LANES, CTX], kT=[P, LANES, WM, CTX],
                    v=[TMAX, LANES, NT, WH, WD + 1], qT=[P, LANES, WM, S], rowmax=[S, 2, ITEM], probs=[S, 2, ITEM, CTX],
                    probsT=[TMAX, 2, ITEM, NT * S], rowsum=[S, ITEM], heads=[S, LANES, WI], headsT=[P, LANES, WM, S], any_key=[S, 1], any_inverse=[S, 1], any=[S, 1])
        bias = ctx.enter_context(nc.sbuf_tensor("wide_bias", [S, CTX], BF16))
        m1 = norm_of(nc, ctx, "wide_ln")
        scores = lambda i: g.psum[0:S, i % 2 * ITEM:(i % 2 + 1) * ITEM, 0:CTX]
        turned, out_bank, make_bank = lambda j: g.psum[:, 4 + j, :], g.psum[:, 6, :], g.psum[:, 7, :]
        item_out = out_bank[0:S, 0:ITEM * (WD + 1)].rearrange("s (h d) -> s h d", d=WD + 1)
        four = lambda ps: ps[:, 0:4 * S].rearrange("p (c s) -> p c s", s=S)
        block = ctx.enter_context(nc.Block())

        def batches(eng, run):
            with eng.Fori(0, PAIRS - 1) as pair:
                here = [(lane, b, n, eng.snap(pair + 1)) for lane, b, n in lanes_of(eng, pair)]
                after = (0, eng.snap(pair * LANES + LANES), eng.snap(pair * LANES + LANES + 1), eng.snap(pair + 2))
                run(here[0], here[1])
                run(here[1], after)
            run((0, B - 2, B - 1, PAIRS), (1, B - 1, B, PAIRS))
            run((1, B - 1, B, PAIRS), None)

        FIRST = (0, 0, 1, 1)

        def load_ctx(sp, lane, b):
            sp.dma_start(t.c0[:, lane, :], ctxT_in[0:P, b, :]).then_inc(ctx_loaded[lane], 16)
            sp.dma_start(t.c1[:, lane, :], ctxT_in[P:CD, b, :]).then_inc(ctx_loaded[lane], 16)

        @block.sync
        def _(sp):
            for lane in range(LANES):
                load_ctx(sp, lane, lane)
            with sp.Fori(1, PAIRS) as pair:
                for lane, b, n in lanes_of(sp, pair):
                    sp.wait_ge(made[NEXT_LAST], sp.snap(b - 1))
                    load_ctx(sp, lane, b)

        @block.gpsimd
        def _(pool):
            nc.gpsimd.memset(t.v[:, :, :, :, WD:WD + 1], 1.0).then_inc(s.ones, 1)
            with pool.Fori(0, PAIRS) as pair:
                for lane, b, n in lanes_of(pool, pair):
                    norm_root(nc, pool, g, m1, lane, n)

        @block.tensor
        def _(pe):
            pe.wait_ge(g.loaded.wide, g.total.wide)
            pe.wait_ge(s.ones, 1)
            pe.wait_ge(s.bias, 1)
            pe.wait_ge(s.turned_zero, 1)

            def make(batch, u):
                lane, b, n, pairs = batch
                kind, i = MADE[u]
                if u == 0:
                    pe.wait_ge(ctx_loaded[lane], pe.snap(pairs * 32))
                    if b is not FIRST[1]:
                        pe.wait_ge(kept[NEXT_LAST], pe.snap(n - 1))
                else:
                    pe.wait_ge(kept[u - 1], n)
                if kind == "y":
                    pe.wait_ge(s.y, n)
                    last = turn(nc, g, make_bank, t.y[:, lane, :], DC)
                elif kind == "k":
                    nc.tensor.matmul(make_bank[:, 0:CTX], w.k0[:, i * P:(i + 1) * P], t.c0[:, lane, :], start=True, stop=False)
                    last = nc.tensor.matmul(make_bank[:, 0:CTX], w.k1[:, i * P:(i + 1) * P], t.c1[:, lane, :], start=False, stop=True)
                elif kind == "q":
                    for m in range(4 * i, 4 * i + 4):
                        for c in range(DC):
                            last = nc.tensor.matmul(make_bank[:, m % 4 * S:(m % 4 + 1) * S], w.q[:, c, m * P:(m + 1) * P], t.yT[:, lane, c, :],
                                                    start=(c == 0), stop=(c == DC - 1))
                else:
                    (k0, kw), cols = WIDE_TILES[i // 2], slice(i % 2 * BANK, (i % 2 + 1) * BANK)
                    nc.tensor.matmul(make_bank[0:kw, :], t.c0[:, lane, k0:k0 + kw], w.v0[:, cols], start=True, stop=False)
                    last = nc.tensor.matmul(make_bank[0:kw, :], t.c1[:, lane, k0:k0 + kw], w.v1[:, cols], start=False, stop=True)
                last.then_inc(made[u], 1)

            def score(batch, i):
                lane, b, n, pairs = batch
                if i == 0:
                    pe.wait_ge(kept[MADE.index(("q", 1))], n)
                    pe.wait_ge(kept[MADE.index(("q", 0))], n)
                for j in range(ITEM):
                    nc.tensor.matmul(scores(i)[:, j, :], g.ident_b[0:S, 0:S], bias[:, :], start=True, stop=False)
                for j in range(ITEM):
                    h = i * ITEM + j
                    rows = slice(WD * (h % 2), WD * (h % 2 + 1))
                    last = nc.tensor.matmul(scores(i)[:, j, :], t.qT[rows, lane, h // 2, :], t.kT[rows, lane, h // 2, :], start=False, stop=True)
                last.then_inc(a[i].scores_ready, 1)

            def heads_out(batch, i):
                lane, b, n, pairs = batch
                pe.wait_ge(a[i].probsT_act, n)
                pe.wait_ge(a[i].probsT_dve, n)
                if i == 0:
                    pe.wait_ge(kept[NEXT_LAST], n)
                    pe.wait_ge(kept[NEXT_LAST - 1], n)
                else:
                    pe.wait_ge(a[i - 1].heads, n)
                for j in range(ITEM):
                    for k, (k0, kw) in enumerate(WIDE_TILES):
                        last = nc.tensor.matmul(item_out[:, j, :], t.probsT[0:kw, i % 2, j, k * S:(k + 1) * S], t.v[0:kw, lane, k, i * ITEM + j, :],
                                                start=(k == 0), stop=(k == NT - 1))
                last.then_inc(a[i].heads_ready, 1)

            def run(batch, after):
                lane, b, n, pairs = batch
                for i in range(ITEMS):
                    end = i == ITEMS - 1
                    if not end:
                        score(batch, i + 1)
                    elif after:
                        score(after, 0)
                    if after and 2 * i < BETWEEN:
                        make(after, 2 * i)
                    elif after and end:
                        make(after, BETWEEN)
                    pe.wait_ge(a[i].probs, n)
                    if i > 0:
                        pe.wait_ge(a[i - 1].probsT_act, n)
                        pe.wait_ge(a[i - 1].probsT_dve, n)
                    for j in range(ITEM):
                        for k, (k0, kw) in enumerate(WIDE_TILES):
                            last = nc.tensor.transpose(turned(j)[0:kw, k * S:(k + 1) * S], t.probs[:, i % 2, j, k0:k0 + kw], g.ident[0:S, 0:S])
                    last.then_inc(a[i].turned_ready, 1)
                    if i > 0:
                        heads_out(batch, i - 1)
                    if after and 2 * i < BETWEEN:
                        make(after, 2 * i + 1)
                    elif after and end:
                        make(after, BETWEEN + 1)
                heads_out(batch, ITEMS - 1)
                if after:
                    make(after, BETWEEN + 2)
                pe.wait_ge(a[ITEMS - 1].heads, n)
                for m in range(WM):
                    last = nc.tensor.transpose(turned(m // 4)[:, m % 4 * S:(m % 4 + 1) * S], t.heads[:, lane, m * P:(m + 1) * P], g.ident[0:S, 0:S])
                last.then_inc(s.headsT_ready, 1)
                if after:
                    make(after, BETWEEN + 3)
                pe.wait_ge(s.headsT_act, n)
                pe.wait_ge(s.headsT_dve, n)
                for m in range(WM):
                    nc.tensor.matmul(out_bank[0:S, 0:D], t.headsT[:, lane, m, :], w.proj[:, m, :], start=(m == 0), stop=False)
                nc.tensor.matmul(out_bank[0:S, 0:D], g.ones[0:1, 0:S], w.proj_b[:, :], start=False, stop=True).then_inc(s.proj_ready, 1)
                if after:
                    make(after, BETWEEN + 4)
                    pe.wait_ge(s.added, n)

            for u in range(len(MADE)):
                make(FIRST, u)
            score(FIRST, 0)
            batches(pe, run)

        def keep(eng, copy, scaled, batch, u):
            lane, b, n, pairs = batch
            kind, i = MADE[u]
            eng.wait_ge(made[u], n)
            if kind == "y":
                for c in range(DC):
                    last = nc.scalar.activation(t.yT[:, lane, c, :], make_bank[:, c * S:(c + 1) * S], ACT.Identity,
                                                bias=w.ln[:, DC + c:DC + c + 1], scale=w.ln[:, c:c + 1])
            elif kind == "k":
                last = copy(t.kT[:, lane, i, :], make_bank[:, 0:CTX])
            elif kind == "q":
                last = scaled(t.qT[:, lane, 4 * i:4 * i + 4, :], four(make_bank), WD ** -0.5)
            else:
                kw, heads = WIDE_TILES[i // 2][1], slice(i % 2 * WH // 2, (i % 2 + 1) * WH // 2)
                last = copy(t.v[0:kw, lane, i // 2, heads, 0:WD], make_bank[0:kw, :].rearrange("k (h d) -> k h d", d=WD))
            last.then_inc(kept[u], 1)

        @block.scalar
        def _(act):
            act.wait_ge(g.loaded.wide, g.total.wide)
            act.wait_ge(s.ones, 1)

            def keep_by_act(batch, u):
                if batch and BY_ACT(u):
                    keep(act, nc.scalar.copy, nc.scalar.mul, batch, u)

            def weigh(batch, i):
                act.wait_ge(a[i].rowmax, batch[2])
                for j in range(ITEM):
                    last = nc.scalar.activation(t.probs[:, i % 2, j, :], scores(i)[:, j, :], ACT.Exp, bias=t.rowmax[:, i % 2, j:j + 1])
                last.then_inc(a[i].probs, 1)

            def run(batch, after):
                lane, b, n, pairs = batch
                for i in range(ITEMS):
                    end = i == ITEMS - 1
                    if not end:
                        weigh(batch, i + 1)
                    elif after:
                        weigh(after, 0)
                    if 2 * i < BETWEEN:
                        keep_by_act(after, 2 * i)
                    elif end:
                        keep_by_act(after, BETWEEN)
                    act.wait_ge(a[i].turned_ready, n)
                    nc.scalar.copy(t.probsT[:, i % 2, 0, :], turned(0)[0:TMAX, 0:NT * S]).then_inc(a[i].probsT_act, 1)
                    if 2 * i < BETWEEN:
                        keep_by_act(after, 2 * i + 1)
                    elif end:
                        keep_by_act(after, BETWEEN + 1)
                keep_by_act(after, BETWEEN + 2)
                act.wait_ge(s.headsT_ready, n)
                nc.scalar.copy(t.headsT[:, lane, 0:4, :], four(turned(0))).then_inc(s.headsT_act, 1)
                keep_by_act(after, BETWEEN + 3)
                keep_by_act(after, BETWEEN + 4)

            for u in range(len(MADE)):
                keep_by_act(FIRST, u)
            weigh(FIRST, 0)
            batches(act, run)

        @block.vector
        def _(dve):
            dve.wait_ge(g.loaded.wide, g.total.wide)
            nc.vector.tensor_scalar(bias[:, :], w.mask[:, :], 1.0, -MASKED, ALU.subtract, ALU.mult).then_inc(s.bias, 1)
            nc.vector.memset(g.psum[:, 4:6, :], 0.0).then_inc(s.turned_zero, 1)
            nc.vector.reduce_max(t.any_key[:, :], w.mask[:, :], AX.X).then_inc(s.any_key, 1)
            dve.wait_ge(s.any_key, 1)
            nc.vector.reciprocal(t.any_inverse[:, :], t.any_key[:, :]).then_inc(s.any_inverse, 1)
            dve.wait_ge(s.any_inverse, 1)
            nc.vector.tensor_tensor(t.any[:, :], t.any_key[:, :], t.any_inverse[:, :], ALU.mult).then_inc(s.any, 1)
            dve.wait_ge(s.any, 1)
            dve.wait_ge(s.ones, 1)

            def keep_by_dve(batch, u):
                if batch and not BY_ACT(u):
                    keep(dve, nc.vector.tensor_copy, lambda out, rows, by: nc.vector.tensor_scalar(out, rows, by, None, ALU.mult), batch, u)

            def stats(batch):
                norm_stats(nc, dve, m1, [batch[0:3]], lambda lane, b: g.x[:, b, :])

            def apply(batch):
                lane, b, n, pairs = batch
                norm_apply(nc, dve, m1, lane, n, t.y[:, lane, :], g.x[:, b, :], s.y)

            def peak(batch, i):
                dve.wait_ge(a[i].scores_ready, batch[2])
                nc.vector.reduce_max(t.rowmax[:, i % 2, :], scores(i), AX.X, negate=True).then_inc(a[i].rowmax, 1)

            def divide(batch, i):
                lane, b, n, pairs = batch
                dve.wait_ge(a[i].heads_ready, n)
                nc.vector.reciprocal(t.rowsum[:, :].unsqueeze(2), item_out[:, :, WD:WD + 1]).then_inc(a[i].rowsum, 1)
                dve.wait_ge(a[i].rowsum, n)
                nc.vector.tensor_tensor(t.heads[:, lane, i * ITEM * WD:(i + 1) * ITEM * WD].rearrange("s (h d) -> s h d", d=WD), item_out[:, :, 0:WD],
                                        t.rowsum[:, :].unsqueeze(2).broadcast_to([S, ITEM, WD]), ALU.mult).then_inc(a[i].heads, 1)

            def run(batch, after):
                lane, b, n, pairs = batch
                if after:
                    stats(after)
                for i in range(ITEMS):
                    end = i == ITEMS - 1
                    if not end:
                        peak(batch, i + 1)
                    elif after:
                        peak(after, 0)
                    if i == 1 and after:
                        apply(after)
                    if 2 * i < BETWEEN:
                        keep_by_dve(after, 2 * i)
                    elif end:
                        keep_by_dve(after, BETWEEN)
                    dve.wait_ge(a[i].turned_ready, n)
                    nc.vector.tensor_copy(t.probsT[:, i % 2, 1, :], turned(1)[0:TMAX, 0:NT * S]).then_inc(a[i].probsT_dve, 1)
                    if i > 0:
                        divide(batch, i - 1)
                    if 2 * i < BETWEEN:
                        keep_by_dve(after, 2 * i + 1)
                    elif end:
                        keep_by_dve(after, BETWEEN + 1)
                divide(batch, ITEMS - 1)
                keep_by_dve(after, BETWEEN + 2)
                dve.wait_ge(s.headsT_ready, n)
                nc.vector.tensor_copy(t.headsT[:, lane, 4:8, :], four(turned(1))).then_inc(s.headsT_dve, 1)
                keep_by_dve(after, BETWEEN + 3)
                dve.wait_ge(s.proj_ready, n)
                nc.vector.scalar_tensor_tensor(g.x[:, b, :], out_bank[0:S, 0:D], t.any[:, :], g.x[:, b, :], ALU.mult, ALU.add).then_inc(s.added, 1)
                keep_by_dve(after, BETWEEN + 4)

            stats(FIRST)
            apply(FIRST)
            for u in range(len(MADE)):
                keep_by_dve(FIRST, u)
            peak(FIRST, 0)
            batches(dve, run)



EXPERTS = NE + 1
RING = 3
UNIT = 4
UT = UNIT * S
UNITS = B // UNIT


def gate_phase(nc, g, w, f):
    with ExitStack() as ctx:
        z = semaphores(nc, ctx, "gate", "ones y yT_ready yT kept gates_ready gates gmax gexp cmp ties behind rank chosen gsum grec coef coefT_ready coefT")
        u = buffers(nc, ctx, "gate", y=[S, LANES, D], yT=[P, LANES, DC, S], gates=[S, LANES, NE], gmax=[S, LANES, 1], gexp=[S, LANES, NE],
                    above=[S, LANES, NE, NE], equal=[S, LANES, NE, NE], rank=[S, LANES, NE], chosen=[S, LANES, NE], gsum=[S, LANES, 1],
                    grec=[S, LANES, 1], coef=[S, LANES, EXPERTS])
        m1 = norm_of(nc, ctx, "gate_ln")
        bank = lambda lane, k: g.psum[:, lane * BANKS + k, :]
        block = ctx.enter_context(nc.Block())

        @block.gpsimd
        def _(pool):
            nc.gpsimd.memset(u.coef[:, :, 0:1], 1.0).then_inc(z.ones, 1)
            nc.gpsimd.memset(f.sum[:, :, :], 0.0)
            with pool.Fori(0, PAIRS) as pair:
                lanes = lanes_of(pool, pair)
                for lane, b, n in lanes:
                    norm_root(nc, pool, g, m1, lane, n)
                for lane, b, n in lanes:
                    pool.wait_ge(z.yT, n)
                    nc.gpsimd.tensor_copy(f.yT[:, :, bass.ds(b * S, S)], u.yT[:, lane, :, :]).then_inc(z.kept, 1)

        @block.tensor
        def _(pe):
            pe.wait_ge(g.loaded.moe, g.total.moe)
            with pe.Fori(0, PAIRS) as pair:
                lanes = lanes_of(pe, pair)
                for lane, b, n in lanes:
                    pe.wait_ge(z.y, n)
                    turn(nc, g, bank(lane, 0), u.y[:, lane, :], DC).then_inc(z.yT_ready, 1)
                for lane, b, n in lanes:
                    pe.wait_ge(z.yT, n)
                    for c in range(DC):
                        last = nc.tensor.matmul(bank(lane, 1)[0:S, 0:NE], u.yT[:, lane, c, :], w.gate[:, c, :], start=(c == 0), stop=(c == DC - 1))
                    last.then_inc(z.gates_ready, 1)
                for lane, b, n in lanes:
                    pe.wait_ge(z.coef, n)
                    pe.wait_ge(z.kept, n)
                    nc.tensor.transpose(bank(lane, 2)[0:EXPERTS, 0:S], u.coef[:, lane, :], g.ident[0:S, 0:S]).then_inc(z.coefT_ready, 1)

        @block.scalar
        def _(act):
            with act.Fori(0, PAIRS) as pair:
                lanes = lanes_of(act, pair)
                for lane, b, n in lanes:
                    act.wait_ge(z.yT_ready, n)
                    nc.scalar.copy(u.yT[:, lane, :, :], bank(lane, 0)[:, 0:DC * S].rearrange("p (c s) -> p c s", s=S)).then_inc(z.yT, 1)
                for lane, b, n in lanes:
                    act.wait_ge(z.gmax, n)
                    nc.scalar.activation(u.gexp[:, lane, :], u.gates[:, lane, :], ACT.Exp, bias=u.gmax[:, lane, :]).then_inc(z.gexp, 1)
                for lane, b, n in lanes:
                    act.wait_ge(z.coefT_ready, n)
                    nc.scalar.copy(f.coefT[:, bass.ds(b * S, S)], bank(lane, 2)[0:EXPERTS, 0:S]).then_inc(z.coefT, 1)

        @block.vector
        def _(dve):
            dve.wait_ge(z.ones, 1)
            with dve.Fori(0, PAIRS) as pair:
                lanes = lanes_of(dve, pair)
                norm_stats(nc, dve, m1, lanes, lambda lane, b: g.x[:, b, :])
                for lane, b, n in lanes:
                    norm_apply(nc, dve, m1, lane, n, u.y[:, lane, :], g.x[:, b, :], z.y)
                for lane, b, n in lanes:
                    dve.wait_ge(z.gates_ready, n)
                    nc.vector.tensor_copy(u.gates[:, lane, :], bank(lane, 1)[0:S, 0:NE]).then_inc(z.gates, 1)
                for lane, b, n in lanes:
                    dve.wait_ge(z.gates, n)
                    nc.vector.reduce_max(u.gmax[:, lane, :], u.gates[:, lane, :], AX.X, negate=True).then_inc(z.gmax, 1)
                top_two(nc, dve, g, lanes, u, z, u.gates)
                for lane, b, n in lanes:
                    dve.wait_ge(z.rank, n)
                    dve.wait_ge(z.gexp, n)
                    nc.vector.scalar_tensor_tensor(u.chosen[:, lane, :], u.rank[:, lane, :], 2.0, u.gexp[:, lane, :], ALU.is_lt, ALU.mult).then_inc(z.chosen, 1)
                for lane, b, n in lanes:
                    dve.wait_ge(z.chosen, n)
                    nc.vector.reduce_sum(u.gsum[:, lane, :], u.chosen[:, lane, :], AX.X).then_inc(z.gsum, 1)
                for lane, b, n in lanes:
                    dve.wait_ge(z.gsum, n)
                    nc.vector.reciprocal(u.grec[:, lane, :], u.gsum[:, lane, :]).then_inc(z.grec, 1)
                for lane, b, n in lanes:
                    dve.wait_ge(z.grec, n)
                    nc.vector.tensor_scalar(u.coef[:, lane, 1:EXPERTS], u.chosen[:, lane, :], u.grec[:, lane, :], None, ALU.mult).then_inc(z.coef, 1)


def experts_phase(nc, g, w, f, w1_in, w2_in):
    with ExitStack() as ctx:
        s = semaphores(nc, ctx, "moe", "row gate gate_ready hidden_ready hidden out_ready0 out_ready1 scaled0 scaled1 added0 added1")
        w_loaded = [ctx.enter_context(nc.semaphore(f"moe_w_loaded{k}")) for k in range(RING)]
        t = buffers(nc, ctx, "moe", w1=[P, RING, DC, HID], w2=[P, RING, HM, D], row=[EXPERTS, LANES, UT], hidden=[P, LANES, HM, UT],
                    scaled=[P, LANES, DC, UT], gate=[P, LANES, UT])
        HB = 4
        out_ready, scaled, added = (s.out_ready0, s.out_ready1), (s.scaled0, s.scaled1), (s.added0, s.added1)
        block = ctx.enter_context(nc.Block())
        UPAIRS = UNITS // LANES

        def units(eng, turn_, k, pair):
            base = turn_ * (RING * UNITS) + pair * LANES
            return [(lane, eng.snap(pair * LANES + lane), eng.snap(base + (k * UNITS + lane))) for lane in range(LANES)]

        @block.sync
        def _(sp):
            def load(k, e):
                sp.dma_start(t.w1[:, k, :, :], w1_in[e]).then_inc(w_loaded[k], 16)
                sp.dma_start(t.w2[:, k, :, :], w2_in[e]).then_inc(w_loaded[k], 16)

            for k in range(RING):
                load(k, k)
            with sp.Fori(1, EXPERTS // RING) as turn_:
                for k in range(RING):
                    sp.wait_ge(s.out_ready1, sp.snap((turn_ - 1) * (RING * UNITS) + (k + 1) * UNITS))
                    load(k, sp.snap(turn_ * RING + k))

        @block.tensor
        def _(pe):
            with pe.Fori(0, EXPERTS // RING) as turn_:
                for k in range(RING):
                    with pe.Fori(0, UPAIRS) as pair:
                        todo = units(pe, turn_, k, pair)
                        pe.wait_ge(w_loaded[k], pe.snap(turn_ * 32 + 32))
                        for lane, unit, n in todo:
                            for m in range(HM):
                                if m >= HB or lane > 0:
                                    pe.wait_ge(s.hidden, pe.snap(n * HM + (m - HB + 1)))
                                for c in range(DC):
                                    last = nc.tensor.matmul(g.psum[:, m % HB, 0:UT], t.w1[:, k, c, m * P:(m + 1) * P],
                                                            f.yT[:, c, bass.ds(unit * UT, UT)], start=(c == 0), stop=(c == DC - 1))
                                last.then_inc(s.hidden_ready, 1)
                            pe.wait_ge(s.row, pe.snap(n + 1))
                            nc.tensor.matmul(g.psum[:, 6 + lane, 0:UT], g.ones[0:EXPERTS, :], t.row[:, lane, :], start=True, stop=True).then_inc(s.gate_ready, 1)
                        for lane, unit, n in todo:
                            pe.wait_ge(s.hidden, pe.snap(n * HM + HM))
                            for c in range(DC):
                                if lane > 0:
                                    pe.wait_ge(scaled[c], n)
                                for m in range(HM):
                                    last = nc.tensor.matmul(g.psum[:, 4 + c, 0:UT], t.w2[:, k, m, c * P:(c + 1) * P], t.hidden[:, lane, m, :],
                                                            start=(m == 0), stop=(m == HM - 1))
                                last.then_inc(out_ready[c], 1)

        @block.scalar
        def _(act):
            with act.Fori(0, EXPERTS // RING) as turn_:
                for k in range(RING):
                    with act.Fori(0, UPAIRS) as pair:
                        for lane, unit, n in units(act, turn_, k, pair):
                            for m in range(HM):
                                act.wait_ge(s.hidden_ready, act.snap(n * HM + (m + 1)))
                                nc.scalar.activation(t.hidden[:, lane, m, :], g.psum[:, m % HB, 0:UT], ACT.Silu).then_inc(s.hidden, 1)

        @block.gpsimd
        def _(pool):
            with pool.Fori(0, EXPERTS // RING) as turn_:
                for k in range(RING):
                    with pool.Fori(0, UPAIRS) as pair:
                        for lane, unit, n in units(pool, turn_, k, pair):
                            for c in range(DC):
                                pool.wait_ge(scaled[c], pool.snap(n + 1))
                                part = f.sum[:, c, bass.ds(unit * UT, UT)]
                                nc.gpsimd.tensor_tensor(part, part, t.scaled[:, lane, c, :], ALU.add).then_inc(added[c], 1)

        @block.vector
        def _(dve):
            with dve.Fori(0, EXPERTS // RING) as turn_:
                for k in range(RING):
                    with dve.Fori(0, UPAIRS) as pair:
                        todo = units(dve, turn_, k, pair)
                        for lane, unit, n in todo:
                            nc.vector.tensor_scalar(t.row[:, lane, :], f.coefT[:, bass.ds(unit * UT, UT)], g.ident[0:EXPERTS, turn_ * RING + k].unsqueeze(1), None,
                                                    ALU.mult).then_inc(s.row, 1)
                        for lane, unit, n in todo:
                            dve.wait_ge(s.gate_ready, dve.snap(n + 1))
                            nc.vector.tensor_copy(t.gate[:, lane, :], g.psum[:, 6 + lane, 0:UT]).then_inc(s.gate, 1)
                            dve.wait_ge(s.gate, dve.snap(n + 1))
                            for c in range(DC):
                                dve.wait_ge(out_ready[c], dve.snap(n + 1))
                                nc.vector.tensor_tensor(t.scaled[:, lane, c, :], g.psum[:, 4 + c, 0:UT], t.gate[:, lane, :], ALU.mult).then_inc(scaled[c], 1)
                        dve.wait_ge(added[DC - 1], dve.snap(todo[-1][2] + 1))


def finish_phase(nc, g, f, out):
    with ExitStack() as ctx:
        s = semaphores(nc, ctx, "finish", "part turned_ready rows")
        stored = [ctx.enter_context(nc.semaphore(f"finish_stored{lane}")) for lane in range(LANES)]
        t = buffers(nc, ctx, "finish", part=[P, LANES, DC, S])
        bank = lambda lane, k: g.psum[:, lane * BANKS + k, :]
        block = ctx.enter_context(nc.Block())

        @block.gpsimd
        def _(pool):
            for b in range(LANES):
                nc.gpsimd.tensor_copy(t.part[:, b, :, :], f.sum[:, :, b * S:(b + 1) * S]).then_inc(s.part, 1)
            with pool.Fori(1, PAIRS) as pair:
                for lane, b, n in lanes_of(pool, pair):
                    pool.wait_ge(s.rows, pool.snap(b - 1))
                    nc.gpsimd.tensor_copy(t.part[:, lane, :, :], f.sum[:, :, bass.ds(b * S, S)]).then_inc(s.part, 1)

        @block.tensor
        def _(pe):
            with pe.Fori(0, PAIRS) as pair:
                for lane, b, n in lanes_of(pe, pair):
                    pe.wait_ge(s.part, n)
                    for c in range(DC):
                        last = nc.tensor.transpose(bank(lane, 0)[0:S, c * P:(c + 1) * P], t.part[:, lane, c, :], g.ident[:, :])
                    last.then_inc(s.turned_ready, 1)

        @block.vector
        def _(dve):
            with dve.Fori(0, PAIRS) as pair:
                for lane, b, n in lanes_of(dve, pair):
                    dve.wait_ge(s.turned_ready, n)
                    nc.vector.tensor_tensor(g.x[:, b, :], g.x[:, b, :], bank(lane, 0)[0:S, 0:D], ALU.add).then_inc(s.rows, 1)

        @block.sync
        def _(sp):
            with sp.Fori(0, PAIRS) as pair:
                for lane, b, n in lanes_of(sp, pair):
                    sp.wait_ge(s.rows, n)
                    sp.dma_start(out[b], g.x[:, b, :]).then_inc(stored[lane], 16)
            for lane in range(LANES):
                sp.wait_ge(stored[lane], 16 * PAIRS)


def clear_semaphores(nc):
    with nc.Block() as block:
        @block.gpsimd
        def _(pool):
            nc.gpsimd.sem_clear(range(min(nc.free_semaphores), max(nc.free_semaphores) + 1))


def decoder(nc, i, out):
    with ExitStack() as ctx:
        sb = lambda n, shape, dt=F32: ctx.enter_context(nc.sbuf_tensor(n, shape, dt))
        g = Fields(x=sb("x", [S, B, D]), ident=sb("ident", [P, P]), ident_b=sb("ident_b", [P, P], BF16),
                            causal=sb("causal", [S, QT * S], BF16), half_scaled=sb("half_scaled", [P, 2]), ones=sb("ones", [NH, P]),
                            before=sb("before", [S, NE, NE]), eps=sb("eps", [P, 1]), neg_half=sb("neg_half", [P, 32]))
        g.psum = ctx.enter_context(nc.psum_tensor("banks", [P, 8, BANK], F32))
        sets = "first cross mix rot wide moe"
        g.loaded = Fields(**{n: ctx.enter_context(nc.semaphore("loaded_" + n)) for n in sets.split() + ["filled"]})
        g.total = Fields(**{n: 0 for n in sets.split()})
        g.loads = []

        def load(which, dst, src):
            g.loads.append((g.loaded[which], dst, src))
            g.total[which] += 16

        def weight(stack, which, name, shape, dt=F32):
            dst = stack.enter_context(nc.sbuf_tensor("w_" + name, shape, dt))
            load(which, dst[tuple(slice(None) for _ in shape)], i[name])
            return dst

        with ExitStack() as late, ExitStack() as early:
            moe_w = Fields(gate=sb("w_moe_gate", [P, DC, NE]))
            load("moe", moe_w.gate[:, :, :], i["moe_gate"])
            wide_w = Fields(mask=weight(late, "wide", "wide_mask", [S, CTX], U8), **{n: weight(late, "wide", "wide_" + n, shape) for n, shape in dict(
                q=[P, DC, WI], k0=[P, WI], k1=[CD - P, WI], v0=[P, WI], v1=[CD - P, WI], proj=[P, WM, D], proj_b=[1, D], ln=[P, 2 * DC]).items()})
            wide_loads, g.loads = g.loads, []
            load("first", g.x[:, 0:2, :], i["x"][0:2].rearrange("b s d -> s b d"))
            for n in ("ident", "ident_b", "causal", "half_scaled", "ones", "before"):
                t = g[n]
                load("first", t[tuple(slice(None) for _ in t.shape)], i[n].bitcast(t.dtype))
            self_w = Fields(qkv=weight(early, "first", "self_qkv", [P, DC, 3 * D]), proj=weight(early, "first", "self_proj", [P, DC, D]))
            load("first", g.x[:, 2:B, :], i["x"][2:B].rearrange("b s d -> s b d"))
            cross_w = Fields(**{n: weight(early, "cross", "cross_" + n, shape) for n, shape in dict(
                q=[P, DC, D], kv0=[P, 2 * D], kv1=[CD - P, 2 * D], lkv=[P, DC, 2 * D], proj=[P, DC, D], proj_b=[1, D], ln_l=[P, 2 * DC],
                ln_x0=[P, 2], ln_x1=[CD - P, 2], qn_g=[P, 1], kn_g=[P, 1]).items()}, mask=weight(early, "cross", "cross_mask", [B, CTX], U8))
            mix_w = Fields(**{n: weight(early, "mix", "mix_" + n, shape) for n, shape in dict(
                qkv=[P, DC, 3 * D], in_b=[P, 3 * DC], proj=[P, DC, D], proj_b=[1, D], gate=[P, DC, NE], gate_b=[1, NE], expert=[P, DC, NE * D],
                expert_b=[NE, D], ln1_w=[S, D], ln1_b=[S, D], ln2_w=[S, D], ln2_b=[S, D], cos=[S, D], sin=[S, D]).items()})
            rot_w = Fields(**{n: weight(early, "rot", "rot_" + n, shape) for n, shape in dict(
                qkv=[P, DC, 3 * D], qk_b=[P, 2 * DC], v_b=[1, D], proj=[P, DC, D], proj_b=[1, D], w1=[P, D], b1=[P, DC], w2T=[2 * NQ, D],
                b2=[2 * NQ, 1], hadamard=[2 * NQ, RG * VROWS], rot=[P, 4, ROTATED], half=[P, 2], uniform=[S, S],
                real=[P, VROWS], imag=[P, VROWS], sum8=[VROWS, RG]).items()})
            g.loads += wide_loads
            causal_phase(nc, g, self_w, False)
            clear_semaphores(nc)
            normed_cross_phase(nc, g, cross_w, i["ctx"])
            clear_semaphores(nc)
            causal_phase(nc, g, mix_w, True)
            clear_semaphores(nc)
            rotation_phase(nc, g, rot_w)
            early.close()
            clear_semaphores(nc)
            wide_cross_phase(nc, g, wide_w, i["ctxT"])
            late.close()
            f = Fields(yT=sb("moe_yT", [P, DC, B * S]), coefT=sb("moe_coefT", [EXPERTS, B * S]), sum=sb("moe_sum", [P, DC, B * S]))
            clear_semaphores(nc)
            gate_phase(nc, g, moe_w, f)
            clear_semaphores(nc)
            experts_phase(nc, g, moe_w, f, i["moe_w1"], i["moe_w2"])
            clear_semaphores(nc)
            finish_phase(nc, g, f, out)


def program(nc, arrays, out_shape):
    import concourse.mybir as mybir
    ins = {n: nc.dram_tensor(f"in_{n}", a.shape, mybir.dt.from_np(a.dtype), kind="ExternalInput").ap() for n, a in arrays.items()}
    out = nc.dram_tensor("out", out_shape, F32, kind="ExternalOutput").ap()
    decoder(nc, ins, out)



def constants():
    f = np.float32
    short = lambda v: (v.astype(f).view(np.uint32) >> 16).astype(np.uint16)
    i = np.arange(S)
    inv = (1.0 / f(10000.0) ** (np.arange(0, HD, 2, dtype=f) / f(HD))).astype(f)
    ang = (i.astype(f)[:, None] * inv[None, :]).astype(f)
    cos, sin = np.cos(ang).astype(f), np.sin(ang).astype(f)
    half = (np.arange(P)[:, None] // HD % 2 == np.arange(2)[None, :]).astype(f)
    e = np.arange(NE)
    row, of = np.arange(P)[:, None], np.arange(VROWS)[None, :]
    part_of = lambda part: ((row // VROWS == of // NQ) & (row % VROWS == part * NQ + of % NQ)).astype(f)
    return dict(
        ident=np.eye(P, dtype=f), ident_b=short(np.eye(P, dtype=f)),
        causal=short(np.tile(np.where(i[None, :] > i[:, None], f(MASKED), f(0)), (1, QT))),
        half_scaled=half * f(HD ** -0.5), rot_half=half, rot_real=part_of(0), rot_imag=part_of(1),
        rot_sum8=(np.arange(VROWS)[:, None] // NQ == np.arange(RG)[None, :]).astype(f), rot_uniform=np.full((S, S), 1.0 / S, f), ones=np.ones((NH, P), f),
        before=np.broadcast_to((e[None, :] < e[:, None]).astype(f), (S, NE, NE)).copy(),
        mix_cos=np.tile(np.repeat(cos, 2, axis=1), (1, NH)), mix_sin=np.tile(np.stack([-sin, sin], -1).reshape(S, HD), (1, NH)))


def two_blocks(m):
    out = np.zeros((2 * NQ, RG, VROWS), m.dtype)
    for part in range(2):
        out[part * NQ:(part + 1) * NQ, :, part * NQ:(part + 1) * NQ] = m[:, None, :]
    return out.reshape(2 * NQ, RG * VROWS)


def kernel(**inputs):
    import concourse.bacc as bacc
    from concourse.bass_utils import run_bass_kernel_spmd

    a = {n: np.asarray(v) for n, v in inputs.items()}
    rows = lambda m: np.ascontiguousarray(m.reshape(m.shape[0] // P, P, m.shape[1]).transpose(1, 0, 2))
    cols = lambda v: np.ascontiguousarray(v.reshape(-1, P).T)
    wide = lambda v: np.ascontiguousarray(np.broadcast_to(v, (S, v.shape[-1])))
    arrays = dict(constants(), x=a["x"],
        self_qkv=rows(a["L0_attn_w_qkv"]), self_proj=rows(a["L0_attn_w_proj"]),
        mix_qkv=rows(a["L0_ffn_in_proj_w"].T), mix_in_b=cols(a["L0_ffn_in_proj_b"]), mix_proj=rows(a["L0_ffn_out_proj_w"].T),
        mix_proj_b=a["L0_ffn_out_proj_b"].reshape(1, D), mix_gate=rows(a["L0_ffn_gate_w"].T), mix_gate_b=a["L0_ffn_gate_b"].reshape(1, NE),
        mix_expert=rows(a["L0_ffn_expert_w"].transpose(2, 0, 1).reshape(D, NE * D)), mix_expert_b=a["L0_ffn_expert_b"],
        mix_ln1_w=wide(a["L0_ffn_ln1_w"]), mix_ln1_b=wide(a["L0_ffn_ln1_b"]), mix_ln2_w=wide(a["L0_ffn_ln2_w"]), mix_ln2_b=wide(a["L0_ffn_ln2_b"]),
        ctx=a["ctx_768"], cross_mask=a["mask_BxS2_bk0"],
        cross_q=rows(a["L0_xattn_Wq"].T), cross_kv0=np.ascontiguousarray(a["L0_xattn_Wkv"].T[0:P]), cross_kv1=np.ascontiguousarray(a["L0_xattn_Wkv"].T[P:CD]),
        cross_lkv=rows(a["L0_xattn_Wlkv"].T), cross_proj=rows(a["L0_xattn_Wo"].T), cross_proj_b=a["L0_xattn_bo"].reshape(1, D),
        cross_ln_l=np.concatenate([cols(a["L0_xattn_ln_l_g"]), cols(a["L0_xattn_ln_l_b"])], 1),
        cross_ln_x0=np.stack([a["L0_xattn_ln_x_g"][0:P], a["L0_xattn_ln_x_b"][0:P]], 1), cross_ln_x1=np.stack([a["L0_xattn_ln_x_g"][P:], a["L0_xattn_ln_x_b"][P:]], 1),
        cross_qn_g=np.tile(a["L0_xattn_qn_g"], P // XD).reshape(P, 1), cross_kn_g=np.tile(a["L0_xattn_kn_g"], P // XD).reshape(P, 1),
        rot_qkv=rows(np.concatenate([a["L1_attn_wq"], a["L1_attn_wk"], a["L1_attn_wv"]], 1)),
        rot_qk_b=np.concatenate([cols(a["L1_attn_bq"]), cols(a["L1_attn_bk"])], 1), rot_v_b=a["L1_attn_bv"].reshape(1, D),
        rot_proj=rows(a["L1_attn_wo"]), rot_proj_b=a["L1_attn_bo"].reshape(1, D), rot_w1=np.tile(a["L1_attn_w1"], (P // HD, 1)),
        rot_b1=cols(a["L1_attn_b1"]), rot_w2T=a["L1_attn_w2"].T,
        rot_b2=a["L1_attn_b2"].reshape(2 * NQ, 1), rot_hadamard=two_blocks(a["L1_attn_hadamard"]),
        rot_rot=np.repeat(a["L1_attn_rot"][:, :NQ // 2, 0][[[head_at(r, e, c) for e in range(2) for c in range(DC)] for r in range(RG)]].transpose(0, 2, 1), ROWS, axis=0),
        ctxT=np.ascontiguousarray(a["ctx_768"].transpose(2, 0, 1)), wide_mask=a["mask_1x1xSxS2_bk0"].reshape(S, CTX),
        wide_q=rows(a["L1_xattn_Wq"]), wide_k0=a["L1_xattn_Wkv"][0:P, 0:WI], wide_k1=a["L1_xattn_Wkv"][P:CD, 0:WI],
        wide_v0=a["L1_xattn_Wkv"][0:P, WI:], wide_v1=a["L1_xattn_Wkv"][P:CD, WI:], wide_proj=rows(a["L1_xattn_Wo"]),
        wide_proj_b=a["L1_xattn_bo"].reshape(1, D), wide_ln=np.concatenate([cols(a["L1_xattn_ln_gamma"]), cols(a["L1_xattn_ln_beta"])], 1),
        moe_gate=rows(a["L1_ffn_gate_w"].T),
        moe_w1=np.stack([rows(m.T) for m in [a["L1_ffn_shared_w1"], *a["L1_ffn_experts_w1"]]]),
        moe_w2=np.stack([rows(m.T) for m in [a["L1_ffn_shared_w2"], *a["L1_ffn_experts_w2"]]]),
    )
    arrays = {n: np.ascontiguousarray(v) for n, v in arrays.items()}
    nc = bacc.Bacc("TRN2", target_bir_lowering=False, num_devices=1)
    program(nc, arrays, (B, S, D))
    r = run_bass_kernel_spmd(nc, [{f"in_{n}": v for n, v in arrays.items()}], core_ids=[0])
    return r.results[0]["out"]
```

```python
from contextlib import ExitStack

import numpy as np

import concourse.bass as bass
from concourse import mybir

ALU = mybir.AluOpType
ACT = mybir.ActivationFunctionType
AX = mybir.AxisListType
F32 = mybir.dt.float32
BF16 = mybir.dt.bfloat16
U8 = mybir.dt.uint8
I32 = mybir.dt.int32

B, S, D = 32, 100, 256
P = 128
DC = D // P
CTX, CD = 361, 192
NH, HD = 16, 16
ROWS = 32
RG = P // ROWS
XH, XD = 4, 64
WH, WD = 16, 64
WI = WH * WD
WM = WI // P
NE = 8
HID = 4 * D
HM = HID // P
LANES = 2
PAIRS = B // LANES
BANK = 512
MASKED = -1e30
CTX_TILES = [(0, P), (P, P), (2 * P, CTX - 2 * P)]
NT = len(CTX_TILES)
CTX_CHUNKS = [(0, P), (P, CD - P)]
QT = NH // RG


class Fields(dict):

    def __getattr__(self, name):
        return self[name]


def head_at(r, e, c):
    return 2 * RG * c + 2 * r + e


def semaphores(nc, ctx, phase, names):
    return Fields(**{n: ctx.enter_context(nc.semaphore(f"{phase}_{n}")) for n in names.split()})


def buffers(nc, ctx, phase, **shapes):
    return Fields(**{n: ctx.enter_context(nc.sbuf_tensor(f"{phase}_{n}", s, F32)) for n, s in shapes.items()})


def lanes_of(eng, pair):
    return [(lane, eng.snap(pair * LANES + lane), eng.snap(pair * LANES + lane + 1)) for lane in range(LANES)]



def norm_of(nc, ctx, name):
    m = buffers(nc, ctx, name, stats=[S, LANES, 6], meanvar=[S, LANES, 2], vareps=[S, LANES, 1], rstd=[S, LANES, 1], hold=[S, 1])
    m.done = semaphores(nc, ctx, name, "stats meanvar vareps rstd")
    return m


def norm_stats(nc, dve, m, lanes, rows):
    for lane, b, n in lanes:
        nc.vector.bn_stats(m.stats[:, lane, :], rows(lane, b)).then_inc(m.done.stats, 1)
    dve.wait_ge(m.done.stats, lanes[-1][2])
    nc.vector.memset(m.hold[:, :], 0.0)
    for lane, b, n in lanes:
        nc.vector.bn_aggr(m.meanvar[:, lane, :], m.stats[:, lane, :]).then_inc(m.done.meanvar, 1)


def norm_root(nc, pool, g, m, lane, n):
    pool.wait_ge(m.done.meanvar, n)
    nc.gpsimd.tensor_tensor(m.vareps[:, lane, :], m.meanvar[:, lane, 1:2], g.eps[0:S, :], ALU.add).then_inc(m.done.vareps, 1)
    pool.wait_ge(m.done.vareps, n)
    nc.gpsimd.tensor_tensor(m.rstd[:, lane, :], m.vareps[:, lane, :], g.neg_half[0:S, 0:1], ALU.pow).then_inc(m.done.rstd, 1)


def norm_apply(nc, dve, m, lane, n, out, rows, done):
    dve.wait_ge(m.done.rstd, n)
    nc.vector.tensor_scalar(out, rows, m.meanvar[:, lane, 0:1], m.rstd[:, lane, :], ALU.subtract, ALU.mult).then_inc(done, 1)


def turn(nc, g, out, rows, chunks):
    for c in range(chunks):
        last = nc.tensor.transpose(out[:, c * S:(c + 1) * S], rows[:, c * P:(c + 1) * P], g.ident[0:S, 0:S])
    return last



WARM = 4


def causal_phase(nc, g, w, mixture):
    name = "mix" if mixture else "self"
    ROWS_AT, QK_AT = 1, 2
    TWO = 2 * D
    with ExitStack() as ctx:
        s = semaphores(nc, ctx, name, "ones y yT_ready yT qk_ready q k v_ready v heads_ready rowsum heads headsT_ready headsT proj_ready added")
        a = [semaphores(nc, ctx, f"{name}{r}", "scores_ready rowmax shifted probs turned_ready probsT") for r in range(RG)]
        t = buffers(nc, ctx, name, y=[S, LANES, D], yT=[P, 2 * DC, S], q=[P, LANES, DC, P // HD, S], k=[P, LANES, DC, S],
                    v=[S, LANES, NH, HD + 1], rowmax=[S, 2, QT], probs=[S, 2, QT * S], probsT=[S, 2, QT * S],
                    rowsum=[S, NH], heads=[S, D], headsT=[P, DC, S])
        m1 = norm_of(nc, ctx, name + "_ln")
        if mixture:
            z = semaphores(nc, ctx, name, "rope_parts rope x1_scaled x1 x1T_ready x1T gates_ready gmax gexp gsum grec gates cmp ties behind rank coef "
                           "coefT_ready coefT bias_ready sum0 normed out_scaled out_shifted out stored")
            z.experts_ready = [ctx.enter_context(nc.semaphore(f"{name}_experts_ready{k}")) for k in range(NE // 2)]
            z.added = [ctx.enter_context(nc.semaphore(f"{name}_added{e}")) for e in range(NE)]
            u = buffers(nc, ctx, name + "_m", rope=[S, D], rope_a=[S, D], rope_b=[S, D], after=[S, D], x1=[S, D], x1T=[P, LANES, DC, S],
                        gmax=[S, 1, 1], gexp=[S, 1, NE], gsum=[S, 1, 1], grec=[S, 1, 1], gates=[S, 1, NE], above=[S, 1, NE, NE],
                        equal=[S, 1, NE, NE], rank=[S, 1, NE], coef=[S, LANES, NE], coefT=[NE, S], sum=[S, LANES, D])
            m2, m3 = norm_of(nc, ctx, name + "_ln1"), norm_of(nc, ctx, name + "_ln2")
        bank = lambda k: g.psum[:, k, :]
        scores = lambda r: g.psum[0:S, r % 2, 0:QT * S]
        turned, out_bank, make, side = bank(2), bank(3), bank(4), bank(7)
        heads_out = out_bank[0:S, 0:NH * (HD + 1)].rearrange("s (h d) -> s h d", d=HD + 1)
        chunks = lambda ps, k: ps[:, 0:k * S].rearrange("p (c s) -> p c s", s=S)
        by_head = lambda rows: rows.rearrange("s (j k) -> s j k", k=S)
        block = ctx.enter_context(nc.Block())

        def batches(eng, run):
            run(None, None, (0, 0, 1), (1, 1, 2))
            run(None, (0, 0, 1), (1, 1, 2), (0, 2, 3))
            with eng.Fori(0, PAIRS - 2) as pair:
                some = [(k % LANES, eng.snap(pair * LANES + k) if k else eng.snap(pair * LANES), eng.snap(pair * LANES + (k + 1))) for k in range(LANES + 3)]
                for k in range(2, LANES + 2):
                    run(some[k - 2], some[k - 1], some[k], some[k + 1])
            run((0, B - 4, B - 3), (1, B - 3, B - 2), (0, B - 2, B - 1), (1, B - 1, B))
            run((1, B - 3, B - 2), (0, B - 2, B - 1), (1, B - 1, B), None)

        FIRST, LAST_BUT_ONE, LAST = (0, 0, 1), (0, B - 2, B - 1), (1, B - 1, B)

        @block.sync
        def _(sp):
            if not mixture:
                for sem, dst, src in g.loads:
                    sp.dma_start(dst, src).then_inc(sem, 16)
                sp.wait_ge(g.loaded.filled, 3)
                with sp.Fori(0, FILLS) as k:
                    part = g.slots[bass.ds(sp.snap(k * (P * FILL)), P * FILL), :].rearrange("(p r) d -> p (r d)", p=P)
                    sp.dma_start(part, g.zeros[:, :]).then_inc(g.loaded.cleared, 16)

        @block.gpsimd
        def _(pool):
            if not mixture:
                nc.gpsimd.memset(g.eps[:, :], 1e-5).then_inc(g.loaded.filled, 1)
                nc.gpsimd.memset(g.neg_half[:, :], -0.5).then_inc(g.loaded.filled, 1)
                nc.gpsimd.memset(g.zeros[:, :], 0.0).then_inc(g.loaded.filled, 1)
            pool.wait_ge(g.loaded.filled, 3)
            nc.gpsimd.memset(t.v[:, :, :, HD:HD + 1], 1.0).then_inc(s.ones, 1)
            if mixture:
                pool.wait_ge(g.loaded.mix, g.total.mix)
                pool.wait_ge(g.loaded.cleared, 16 * FILLS)

            def rope(batch):
                lane, b, n = batch
                pool.wait_ge(s.y, n)
                y2 = t.y[:, lane, :].rearrange("s (f two) -> s f two", two=2)
                b2 = u.rope_b[:, :].rearrange("s (f two) -> s f two", two=2)
                sin2 = w.sin[:, :].rearrange("s (f two) -> s f two", two=2)
                nc.gpsimd.tensor_tensor(u.rope_a[:, :], t.y[:, lane, :], w.cos[:, :], ALU.mult)
                nc.gpsimd.tensor_tensor(b2[:, :, 0], y2[:, :, 1], sin2[:, :, 0], ALU.mult)
                nc.gpsimd.tensor_tensor(b2[:, :, 1], y2[:, :, 0], sin2[:, :, 1], ALU.mult).then_inc(z.rope_parts, 1)
                pool.wait_ge(z.rope_parts, n)
                nc.gpsimd.tensor_tensor(u.rope[:, :], u.rope_a[:, :], u.rope_b[:, :], ALU.add).then_inc(z.rope, 1)

            def first_norm(batch):
                lane, b, n = batch
                pool.wait_ge(z.normed, n)
                nc.gpsimd.tensor_tensor(u.after[:, :], u.after[:, :], w.ln1_w[:, :], ALU.mult).then_inc(z.x1_scaled, 1)
                pool.wait_ge(z.x1_scaled, n)
                nc.gpsimd.tensor_tensor(u.x1[:, :], u.after[:, :], w.ln1_b[:, :], ALU.add).then_inc(z.x1, 1)

            def add_rows(batch):
                lane, b, n = batch
                norm_root(nc, pool, g, m3, lane, n)
                pool.wait_ge(z.out, n)
                nc.gpsimd.tensor_tensor(u.sum[:, lane, :], u.sum[:, lane, :], w.ln2_w[:, :], ALU.mult).then_inc(z.out_scaled, 1)
                pool.wait_ge(z.out_scaled, n)
                nc.gpsimd.tensor_tensor(u.sum[:, lane, :], u.sum[:, lane, :], w.ln2_b[:, :], ALU.add).then_inc(z.out_shifted, 1)
                pool.wait_ge(z.out_shifted, n)
                nc.gpsimd.tensor_tensor(g.x[:, b, :], g.x[:, b, :], u.sum[:, lane, :], ALU.add).then_inc(z.stored, 1)

            def run(older, before, batch, after):
                if after:
                    norm_root(nc, pool, g, m1, after[0], after[2])
                if mixture:
                    if after:
                        rope(after)
                    if older:
                        add_rows(older)
                    norm_root(nc, pool, g, m2, batch[0], batch[2])
                    first_norm(batch)

            norm_root(nc, pool, g, m1, 0, 1)
            if mixture:
                rope(FIRST)
            batches(pool, run)
            if mixture:
                add_rows(LAST_BUT_ONE)
                add_rows(LAST)

        @block.tensor
        def _(pe):
            pe.wait_ge(g.loaded.first, g.total.first)
            pe.wait_ge(s.ones, 1)
            if mixture:
                pe.wait_ge(g.loaded.mix, g.total.mix)
            src = DC if mixture else 0

            def make_rows(batch):
                lane, b, n = batch
                pe.wait_ge(s.y, n)
                if b is not FIRST[1]:
                    pe.wait_ge(s.v, pe.snap(n - 1))
                last = turn(nc, g, make, t.y[:, lane, :], DC)
                if mixture:
                    pe.wait_ge(z.rope, n)
                    last = turn(nc, g, make[:, DC * S:], u.rope[:, :], DC)
                last.then_inc(s.yT_ready, 1)

            def make_qk(batch):
                lane, b, n = batch
                pe.wait_ge(s.yT, n)
                for m in range(2 * DC):
                    for c in range(DC):
                        last = nc.tensor.matmul(make[:, m * S:(m + 1) * S], w.qkv[:, c, m * P:(m + 1) * P], t.yT[:, src + c, :],
                                                start=(c == 0), stop=(c == DC - 1))
                last.then_inc(s.qk_ready, 1)

            def make_v(batch):
                lane, b, n = batch
                pe.wait_ge(s.k, n)
                for c in range(DC):
                    last = nc.tensor.matmul(make[0:S, 0:D], t.yT[:, c, :], w.qkv[:, c, 2 * D:3 * D], start=(c == 0), stop=(c == DC - 1))
                last.then_inc(s.v_ready, 1)

            def score(batch, r):
                lane, b, n = batch
                if r == 0:
                    pe.wait_ge(s.k, n)
                nc.tensor.matmul(scores(r), g.ident_b[0:S, 0:S], g.causal[:, :], start=True, stop=False)
                for e in range(2):
                    for c in range(DC):
                        at = (e * DC + c) * S
                        last = nc.tensor.matmul(scores(r)[:, at:at + S], t.q[:, lane, c, 2 * r + e, :], t.k[:, lane, c, :],
                                                start=False, stop=(e == 1 and c == DC - 1))
                last.then_inc(a[r].scores_ready, 1)

            def turn_probs(batch, r):
                lane, b, n = batch
                pe.wait_ge(a[r].probs, n)
                if r > 0:
                    pe.wait_ge(a[r - 1].probsT, n)
                for j in range(QT):
                    last = nc.tensor.transpose(turned[0:S, j * S:(j + 1) * S], t.probs[:, r % 2, j * S:(j + 1) * S], g.ident[0:S, 0:S])
                last.then_inc(a[r].turned_ready, 1)

            def by_v(before, batch, r):
                lane, b, n = batch
                pe.wait_ge(a[r].probsT, n)
                if r == 0:
                    pe.wait_ge(s.v, n)
                    if before:
                        pe.wait_ge(s.added, before[2])
                for e in range(2):
                    for c in range(DC):
                        h, at = head_at(r, e, c), (e * DC + c) * S
                        last = nc.tensor.matmul(heads_out[:, h, :], t.probsT[:, r % 2, at:at + S], t.v[:, lane, h, :], start=True, stop=True)
                if r == RG - 1:
                    last.then_inc(s.heads_ready, 1)

            def turn_x1(batch):
                pe.wait_ge(z.x1, batch[2])
                turn(nc, g, side, u.x1[:, :], DC).then_inc(z.x1T_ready, 1)

            def gate(batch):
                pe.wait_ge(z.x1T, batch[2])
                for c in range(DC):
                    nc.tensor.matmul(side[0:S, 0:NE], u.x1T[:, batch[0], c, :], w.gate[:, c, :], start=(c == 0), stop=False)
                nc.tensor.matmul(side[0:S, 0:NE], g.ones[0:1, 0:S], w.gate_b[:, :], start=False, stop=True).then_inc(z.gates_ready, 1)

            def turn_coef(batch):
                pe.wait_ge(z.coef, batch[2])
                nc.tensor.transpose(side[0:NE, 0:S], u.coef[:, batch[0], :], g.ident[0:S, 0:S]).then_inc(z.coefT_ready, 1)

            def biases(batch):
                pe.wait_ge(z.coefT, batch[2])
                nc.tensor.matmul(side[0:S, 0:D], u.coefT[:, :], w.expert_b[:, :], start=True, stop=True).then_inc(z.bias_ready, 1)

            def experts(batch, k):
                if k >= 2:
                    pe.wait_ge(z.added[2 * k - 3], batch[2])
                for c in range(DC):
                    last = nc.tensor.matmul(bank(5 + k % 2)[0:S, :], u.x1T[:, batch[0], c, :], w.expert[:, c, k * TWO:(k + 1) * TWO],
                                            start=(c == 0), stop=(c == DC - 1))
                last.then_inc(z.experts_ready[k], 1)

            def run(older, before, batch, after):
                lane, b, n = batch
                mix = before if mixture else None
                for r in range(RG):
                    if r < RG - 1:
                        score(batch, r + 1)
                    if mixture and older:
                        experts(older, r)
                    if mix and r == 1:
                        turn_x1(mix)
                    if mix and r == 2:
                        gate(mix)
                    if after and r == ROWS_AT:
                        make_rows(after)
                    if after and r == QK_AT:
                        make_qk(after)
                    turn_probs(batch, r)
                    if r > 0:
                        by_v(before, batch, r - 1)
                if after:
                    make_v(after)
                by_v(before, batch, RG - 1)
                if after:
                    score(after, 0)
                pe.wait_ge(s.heads, n)
                turn(nc, g, turned, t.heads[:, :], DC).then_inc(s.headsT_ready, 1)
                pe.wait_ge(s.headsT, n)
                for c in range(DC):
                    last = nc.tensor.matmul(out_bank[0:S, 0:D], t.headsT[:, c, :], w.proj[:, c, :], start=(c == 0), stop=(not mixture and c == DC - 1))
                if mixture:
                    last = nc.tensor.matmul(out_bank[0:S, 0:D], g.ones[0:1, 0:S], w.proj_b[:, :], start=False, stop=True)
                last.then_inc(s.proj_ready, 1)
                if mix:
                    turn_coef(mix)
                    biases(mix)

            make_rows(FIRST)
            make_qk(FIRST)
            for k in range(WARM):
                nc.tensor.matmul(side, w.qkv[:, 0, 0:P], w.qkv[:, 0, 0:BANK], start=True, stop=True)
            make_v(FIRST)
            score(FIRST, 0)
            batches(pe, run)
            if mixture:
                turn_x1(LAST)
                gate(LAST)
                for k in range(NE // 2):
                    experts(LAST_BUT_ONE, k)
                turn_coef(LAST)
                biases(LAST)
                pe.wait_ge(z.added[NE - 1], B - 1)
                for k in range(NE // 2):
                    experts(LAST, k)

        @block.scalar
        def _(act):
            act.wait_ge(g.loaded.first, g.total.first)
            if mixture:
                act.wait_ge(g.loaded.mix, g.total.mix)

            def keep_rows(batch):
                act.wait_ge(s.yT_ready, batch[2])
                k = 2 * DC if mixture else DC
                nc.scalar.copy(t.yT[:, 0:k, :], chunks(make, k)).then_inc(s.yT, 1)

            def keep_k(batch):
                lane, b, n = batch
                act.wait_ge(s.q, n)
                rows = make[:, DC * S:2 * DC * S]
                if mixture:
                    for c in range(DC):
                        last = nc.scalar.activation(t.k[:, lane, c, :], rows[:, c * S:(c + 1) * S], ACT.Identity, bias=w.in_b[:, DC + c:DC + c + 1])
                else:
                    last = nc.scalar.copy(t.k[:, lane, :, :], chunks(rows, DC))
                last.then_inc(s.k, 1)

            def keep_v(batch):
                lane, b, n = batch
                act.wait_ge(s.v_ready, n)
                nc.scalar.copy(t.v[:, lane, :, 0:HD], make[0:S, 0:D].rearrange("s (h d) -> s h d", d=HD)).then_inc(s.v, 1)

            def weigh(batch, r):
                act.wait_ge(a[r].shifted, batch[2])
                nc.scalar.activation(t.probs[:, r % 2, :], t.probs[:, r % 2, :], ACT.Exp).then_inc(a[r].probs, 1)

            def keep_x1(batch):
                act.wait_ge(z.x1T_ready, batch[2])
                nc.scalar.copy(u.x1T[:, batch[0], :, :], chunks(side, DC)).then_inc(z.x1T, 1)

            def weigh_gates(batch):
                act.wait_ge(z.gmax, batch[2])
                nc.scalar.activation(u.gexp[:, 0, :], side[0:S, 0:NE], ACT.Exp, bias=u.gmax[:, 0, :]).then_inc(z.gexp, 1)

            def keep_coef(batch):
                act.wait_ge(z.coefT_ready, batch[2])
                nc.scalar.copy(u.coefT[:, :], side[0:NE, 0:S]).then_inc(z.coefT, 1)

            def run(older, before, batch, after):
                lane, b, n = batch
                mix = before if mixture else None
                for r in range(RG):
                    if mix and r == 1:
                        keep_x1(mix)
                    if after and r == ROWS_AT:
                        keep_rows(after)
                    act.wait_ge(a[r].turned_ready, n)
                    nc.scalar.copy(t.probsT[:, r % 2, :], turned[0:S, 0:QT * S]).then_inc(a[r].probsT, 1)
                    if r < RG - 1:
                        weigh(batch, r + 1)
                    if mix and r == 2:
                        weigh_gates(mix)
                    if after and r == QK_AT:
                        keep_k(after)
                if after:
                    keep_v(after)
                act.wait_ge(s.headsT_ready, n)
                if mixture:
                    for c in range(DC):
                        last = nc.scalar.activation(t.headsT[:, c, :], turned[:, c * S:(c + 1) * S], ACT.Identity, bias=w.in_b[:, 2 * DC + c:2 * DC + c + 1])
                else:
                    last = nc.scalar.copy(t.headsT[:, :, :], chunks(turned, DC))
                last.then_inc(s.headsT, 1)
                if mix:
                    keep_coef(mix)
                if after:
                    weigh(after, 0)

            keep_rows(FIRST)
            keep_k(FIRST)
            keep_v(FIRST)
            weigh(FIRST, 0)
            batches(act, run)
            if mixture:
                keep_x1(LAST)
                weigh_gates(LAST)
                keep_coef(LAST)

        @block.vector
        def _(dve):
            dve.wait_ge(g.loaded.first, g.total.first)
            if mixture:
                dve.wait_ge(g.loaded.mix, g.total.mix)

            def stats(batch):
                norm_stats(nc, dve, m1, [batch], lambda lane, b: g.x[:, b, :])

            def apply(batch):
                lane, b, n = batch
                norm_apply(nc, dve, m1, lane, n, t.y[:, lane, :], g.x[:, b, :], s.y)

            def keep_q(batch):
                lane, b, n = batch
                dve.wait_ge(s.qk_ready, n)
                for c in range(DC):
                    rows = make[:, c * S:(c + 1) * S].unsqueeze(1).broadcast_to([P, P // HD, S])
                    own = g.own_scaled[:, :].unsqueeze(2).broadcast_to([P, P // HD, S])
                    if mixture:
                        last = nc.vector.scalar_tensor_tensor(t.q[:, lane, c, :, :], rows, w.in_b[:, c:c + 1], own, ALU.add, ALU.mult)
                    else:
                        last = nc.vector.tensor_tensor(t.q[:, lane, c, :, :], rows, own, ALU.mult)
                last.then_inc(s.q, 1)

            def shift(batch, r):
                lane, b, n = batch
                dve.wait_ge(a[r].scores_ready, n)
                nc.vector.reduce_max(t.rowmax[:, r % 2, :], by_head(scores(r)), AX.X).then_inc(a[r].rowmax, 1)
                dve.wait_ge(a[r].rowmax, n)
                nc.vector.tensor_tensor(by_head(t.probs[:, r % 2, :]), by_head(scores(r)), t.rowmax[:, r % 2, :].unsqueeze(2).broadcast_to([S, QT, S]),
                                        ALU.subtract).then_inc(a[r].shifted, 1)

            def divide(batch):
                lane, b, n = batch
                dve.wait_ge(s.heads_ready, n)
                nc.vector.reciprocal(t.rowsum[:, :].unsqueeze(2), heads_out[:, :, HD:HD + 1]).then_inc(s.rowsum, 1)
                dve.wait_ge(s.rowsum, n)
                nc.vector.tensor_tensor(t.heads[:, :].rearrange("s (h d) -> s h d", d=HD), heads_out[:, :, 0:HD],
                                        t.rowsum[:, :].unsqueeze(2).broadcast_to([S, NH, HD]), ALU.mult).then_inc(s.heads, 1)

            def first_norm(batch):
                lane, b, n = batch
                norm_apply(nc, dve, m2, lane, n, u.after[:, :], u.after[:, :], z.normed)

            def peak_gates(batch):
                dve.wait_ge(z.gates_ready, batch[2])
                nc.vector.reduce_max(u.gmax[:, 0, :], side[0:S, 0:NE], AX.X, negate=True).then_inc(z.gmax, 1)

            def choose(batch):
                n = batch[2]
                dve.wait_ge(z.gexp, n)
                nc.vector.reduce_sum(u.gsum[:, 0, :], u.gexp[:, 0, :], AX.X).then_inc(z.gsum, 1)
                dve.wait_ge(z.gsum, n)
                nc.vector.reciprocal(u.grec[:, 0, :], u.gsum[:, 0, :]).then_inc(z.grec, 1)
                dve.wait_ge(z.grec, n)
                nc.vector.tensor_scalar(u.gates[:, 0, :], u.gexp[:, 0, :], u.grec[:, 0, :], None, ALU.mult).then_inc(z.gates, 1)
                top_two(nc, dve, g, [(0, batch[1], n)], u, z, u.gates)
                dve.wait_ge(z.rank, n)
                nc.vector.scalar_tensor_tensor(u.coef[:, batch[0], :], u.rank[:, 0, :], 2.0, u.gates[:, 0, :], ALU.is_lt, ALU.mult).then_inc(z.coef, 1)

            def add_biases(batch):
                dve.wait_ge(z.bias_ready, batch[2])
                nc.vector.tensor_tensor(u.sum[:, batch[0], :], u.x1[:, :], side[0:S, 0:D], ALU.add).then_inc(z.sum0, 1)

            def add_experts(batch, k):
                lane, b, n = batch
                dve.wait_ge(z.experts_ready[k], n)
                for e in (2 * k, 2 * k + 1):
                    dve.wait_ge(z.added[e - 1] if e else z.sum0, n)
                    nc.vector.scalar_tensor_tensor(u.sum[:, lane, :], bank(5 + k % 2)[0:S, e % 2 * D:(e % 2 + 1) * D], u.coef[:, lane, e:e + 1],
                                                   u.sum[:, lane, :], ALU.mult, ALU.add).then_inc(z.added[e], 1)

            def second_stats(batch):
                dve.wait_ge(z.added[NE - 1], batch[2])
                norm_stats(nc, dve, m3, [batch], lambda lane, b: u.sum[:, lane, :])

            def second_norm(batch):
                lane, b, n = batch
                norm_apply(nc, dve, m3, lane, n, u.sum[:, lane, :], u.sum[:, lane, :], z.out)

            def run(older, before, batch, after):
                lane, b, n = batch
                mix = before if mixture else None
                if after:
                    stats(after)
                for r in range(RG):
                    if r < RG - 1:
                        shift(batch, r + 1)
                    if after and r == 0:
                        apply(after)
                    if mix and r == 2:
                        peak_gates(mix)
                    if after and r == QK_AT:
                        keep_q(after)
                    if mixture and older:
                        add_experts(older, r)
                if mixture and older:
                    second_stats(older)
                divide(batch)
                if mix:
                    choose(mix)
                if mixture and older:
                    second_norm(older)
                if after:
                    shift(after, 0)
                elif mix:
                    dve.wait_ge(z.stored, before[2] - 2)
                dve.wait_ge(s.proj_ready, n)
                if mixture:
                    nc.vector.tensor_tensor(u.after[:, :], t.y[:, lane, :], out_bank[0:S, 0:D], ALU.add).then_inc(s.added, 1)
                    dve.wait_ge(s.added, n)
                    norm_stats(nc, dve, m2, [batch], lambda lane, b: u.after[:, :])
                    if before:
                        add_biases(before)
                    first_norm(batch)
                else:
                    nc.vector.tensor_tensor(g.x[:, b, :], g.x[:, b, :], out_bank[0:S, 0:D], ALU.add).then_inc(s.added, 1)

            stats(FIRST)
            apply(FIRST)
            keep_q(FIRST)
            shift(FIRST, 0)
            batches(dve, run)
            if mixture:
                peak_gates(LAST)
                for k in range(NE // 2):
                    add_experts(LAST_BUT_ONE, k)
                second_stats(LAST_BUT_ONE)
                choose(LAST)
                second_norm(LAST_BUT_ONE)
                dve.wait_ge(z.stored, B - 2)
                add_biases(LAST)
                for k in range(NE // 2):
                    add_experts(LAST, k)
                second_stats(LAST)
                second_norm(LAST)


def top_two(nc, dve, g, lanes, u, z, gates):
    for lane, b, n in lanes:
        dve.wait_ge(z.gates, n)
        mine = gates[:, lane, :].unsqueeze(2).broadcast_to([S, NE, NE])
        other = gates[:, lane, :].unsqueeze(1).broadcast_to([S, NE, NE])
        nc.vector.tensor_tensor(u.above[:, lane, :, :], other, mine, ALU.is_gt)
        nc.vector.tensor_tensor(u.equal[:, lane, :, :], other, mine, ALU.is_equal).then_inc(z.cmp, 1)
    for lane, b, n in lanes:
        dve.wait_ge(z.cmp, n)
        nc.vector.tensor_tensor(u.equal[:, lane, :, :], u.equal[:, lane, :, :], g.before[:, :, :], ALU.mult).then_inc(z.ties, 1)
    for lane, b, n in lanes:
        dve.wait_ge(z.ties, n)
        nc.vector.tensor_tensor(u.above[:, lane, :, :], u.above[:, lane, :, :], u.equal[:, lane, :, :], ALU.add).then_inc(z.behind, 1)
    for lane, b, n in lanes:
        dve.wait_ge(z.behind, n)
        nc.vector.reduce_sum(u.rank[:, lane, :], u.above[:, lane, :, :], AX.X).then_inc(z.rank, 1)



def normed_cross_phase(nc, g, w, ctx_in):
    KT = NT + 1
    KEYS = NT * P + S
    HALVES = 2
    HT = KT // HALVES
    width = [P] * NT + [S]
    with ExitStack() as ctx:
        s = semaphores(nc, ctx, "cross", "zeroed ones bias turned_zero gain y yy yT_ready lT cstats cmeanvar cvareps crstd cn ctxT_ready ctxT_act ctxT_dve "
                       "q_ready qsq qsum qclip qroot qn qT_ready qT kT_ready kT pick heads_ready rowsum heads headsT_ready headsT proj_ready added")
        a = [semaphores(nc, ctx, f"cross{h}", "scores_ready rowmax probs turned_ready probsT") for h in range(XH)]
        each = lambda name, count: [ctx.enter_context(nc.semaphore(f"cross_{name}{k}")) for k in range(count)]
        kv_ready, kv_kept = each("kv_ready", KT), each("kv_kept", KT)
        ksq, ksum, kclip, kroot, kn = (each(n, HALVES) for n in ("ksq", "ksum", "kclip", "kroot", "kn"))
        raw_loaded = each("ctx_loaded", LANES)
        t = buffers(nc, ctx, "cross", y=[S, D], yy=[S, D], lT=[P, DC, P], raw=[P, LANES, NT, CD], cn=[P, NT, CD],
                    cstats=[P, NT, 6], cmeanvar=[P, NT, 2], cvareps=[P, NT], crstd=[P, NT], chold=[P, 1],
                    ctxT0=[P, NT * P], ctxT1=[CD - P, NT * P], qsq=[S, D], qsum=[S, XH], qclip=[S, XH], qroot=[S, XH], qn=[S, D],
                    k=[P, KT, D], ksq=[P, KT, D], ksum=[P, KT * XH], kclip=[P, KT * XH], kroot=[P, KT * XH],
                    v=[P, LANES, KT, XH, XD + 1], kT=[P, DC, KT * P], qT=[P, DC, S],
                    rowmax=[S, 2], probs=[S, 2, KEYS], probsT=[P, 2, KT * S], rowsum=[S, XH], heads=[S, D], headsT=[P, DC, S], gain=[P, 1])
        bias = ctx.enter_context(nc.sbuf_tensor("cross_bias", [B, KEYS], BF16))
        pick = ctx.enter_context(nc.sbuf_tensor("cross_pick", [B, LANES, S], BF16))
        m1, m2 = norm_of(nc, ctx, "cross_ln"), norm_of(nc, ctx, "cross_ln_l")
        bank = lambda k: g.psum[:, k, :]
        scores = lambda h: g.psum[0:S, h % 2, 0:KEYS]
        turned, out_bank = bank(2), bank(3)
        kv_bank = lambda j: bank(4 + j % 2)
        q_bank, row_bank = bank(6), bank(7)
        heads_out = out_bank[0:S, 0:XH * (XD + 1)].rearrange("s (h d) -> s h d", d=XD + 1)
        chunks = lambda ps: ps[:, 0:DC * S].rearrange("p (c s) -> p c s", s=S)
        by_head = lambda rows: rows.rearrange("s (h d) -> s h d", d=XD)
        block = ctx.enter_context(nc.Block())

        def batches(eng, run):
            with eng.Fori(0, PAIRS - 1) as pair:
                some = [(k % LANES, eng.snap(pair * LANES + k) if k else eng.snap(pair * LANES), eng.snap(pair * LANES + (k + 1)), eng.snap(pair + (1 + k // LANES)))
                        for k in range(2 * LANES)]
                for k in range(LANES):
                    run(some[k], some[k + 1], some[k + 2])
            run((0, B - 2, B - 1, PAIRS), (1, B - 1, B, PAIRS), None)
            run((1, B - 1, B, PAIRS), None, None)

        FIRST, SECOND = (0, 0, 1, 1), (1, 1, 2, 1)

        def load_ctx(sp, lane, b):
            whole = (NT - 1) * P
            sp.dma_start(t.raw[:, lane, 0:NT - 1, :], ctx_in[b, 0:whole, :].rearrange("(t p) d -> p t d", p=P)).then_inc(raw_loaded[lane], 16)
            sp.dma_start(t.raw[0:CTX - whole, lane, NT - 1, :], ctx_in[b, whole:CTX, :]).then_inc(raw_loaded[lane], 16)

        @block.sync
        def _(sp):
            sp.wait_ge(s.zeroed, 1)
            for lane in range(LANES):
                load_ctx(sp, lane, lane)
            with sp.Fori(1, PAIRS) as pair:
                for lane, b, n in lanes_of(sp, pair):
                    sp.wait_ge(s.cn, sp.snap(b - 1))
                    load_ctx(sp, lane, b)

        @block.gpsimd
        def _(pool):
            nc.gpsimd.memset(t.raw[:, :, NT - 1, :], 0.0).then_inc(s.zeroed, 1)
            nc.gpsimd.memset(t.lT[:, :, :], 0.0).then_inc(s.ones, 1)
            nc.gpsimd.memset(t.v[:, :, :, :, XD:XD + 1], 1.0).then_inc(s.ones, 1)
            nc.gpsimd.memset(bias[:, :], MASKED).then_inc(s.ones, 1)

            def choose_mask(batch):
                lane, b, n, pairs = batch
                nc.gpsimd.tensor_copy(pick[:, lane, :], g.ident_b[0:B, b].unsqueeze(1).broadcast_to([B, S])).then_inc(s.pick, 1)

            def root_q(batch):
                pool.wait_ge(s.qclip, batch[2])
                nc.gpsimd.tensor_tensor(t.qroot[:, :], t.qclip[:, :], g.neg_half[0:S, 0:XH], ALU.pow).then_inc(s.qroot, 1)

            def root_k(batch, half):
                at = slice(half * HT * XH, (half + 1) * HT * XH)
                pool.wait_ge(kclip[half], batch[2])
                nc.gpsimd.tensor_tensor(t.kroot[:, at], t.kclip[:, at], g.neg_half[:, at], ALU.pow).then_inc(kroot[half], 1)

            def root_rows(batch, m):
                norm_root(nc, pool, g, m, 0, batch[2])

            def root_ctx(batch):
                pool.wait_ge(s.cmeanvar, batch[2])
                nc.gpsimd.tensor_tensor(t.cvareps[:, :], t.cmeanvar[:, :, 1], g.eps[:, :].broadcast_to([P, NT]), ALU.add).then_inc(s.cvareps, 1)
                pool.wait_ge(s.cvareps, batch[2])
                nc.gpsimd.tensor_tensor(t.crstd[:, :], t.cvareps[:, :], g.neg_half[:, 0:NT], ALU.pow).then_inc(s.crstd, 1)

            def run(batch, after, third):
                if after:
                    root_q(after)
                    choose_mask(after)
                if third:
                    root_rows(third, m1)
                    root_rows(third, m2)
                if after:
                    root_k(after, 0)
                if third:
                    root_ctx(third)
                if after:
                    root_k(after, 1)

            for batch in (FIRST, SECOND):
                root_rows(batch, m1)
                root_rows(batch, m2)
                root_ctx(batch)
                if batch is FIRST:
                    root_q(batch)
                    choose_mask(batch)
                    for half in range(HALVES):
                        root_k(batch, half)
            batches(pool, run)

        @block.tensor
        def _(pe):
            pe.wait_ge(g.loaded.cross, g.total.cross)
            pe.wait_ge(s.ones, 3)
            pe.wait_ge(s.bias, 2)
            pe.wait_ge(s.turned_zero, 1)

            def turn_rows(batch):
                pe.wait_ge(s.yy, batch[2])
                turn(nc, g, row_bank, t.yy[:, :], DC).then_inc(s.yT_ready, 1)

            def turn_ctx(batch, last_made):
                pe.wait_ge(s.cn, batch[2])
                if last_made:
                    for j in (KT - 2, KT - 1):
                        pe.wait_ge(kv_kept[j], last_made[2])
                for k, (c0, cw) in enumerate(CTX_CHUNKS):
                    for j in range(NT):
                        last = nc.tensor.transpose(bank(4 + k)[0:cw, j * P:(j + 1) * P], t.cn[:, j, c0:c0 + cw], g.ident[:, :])
                last.then_inc(s.ctxT_ready, 1)

            def make_q(batch):
                pe.wait_ge(s.lT, batch[2])
                for c in range(DC):
                    last = nc.tensor.matmul(q_bank[0:S, 0:D], t.lT[:, c, 0:S], w.q[:, c, :], start=(c == 0), stop=(c == DC - 1))
                last.then_inc(s.q_ready, 1)

            def make_kv(batch, j):
                n = batch[2]
                if j == 0:
                    pe.wait_ge(s.ctxT_act, n)
                    pe.wait_ge(s.ctxT_dve, n)
                elif j >= 2:
                    pe.wait_ge(kv_kept[j - 2], n)
                if j < NT:
                    nc.tensor.matmul(kv_bank(j), t.ctxT0[:, j * P:(j + 1) * P], w.kv0[:, :], start=True, stop=False)
                    last = nc.tensor.matmul(kv_bank(j), t.ctxT1[:, j * P:(j + 1) * P], w.kv1[:, :], start=False, stop=True)
                else:
                    for c in range(DC):
                        last = nc.tensor.matmul(kv_bank(j), t.lT[:, c, :], w.lkv[:, c, :], start=(c == 0), stop=(c == DC - 1))
                last.then_inc(kv_ready[j], 1)

            def turn_q(batch):
                pe.wait_ge(s.qn, batch[2])
                turn(nc, g, q_bank, t.qn[:, :], DC).then_inc(s.qT_ready, 1)

            def turn_k(batch, third):
                n = batch[2]
                if third:
                    pe.wait_ge(s.lT, third[2])
                pe.wait_ge(s.qT, n)
                for half in range(HALVES):
                    pe.wait_ge(kn[half], n)
                for c in range(DC):
                    for j in range(KT):
                        last = nc.tensor.transpose(bank(6 + c)[:, j * P:(j + 1) * P], t.k[:, j, c * P:(c + 1) * P], g.ident[:, :])
                last.then_inc(s.kT_ready, 1)

            def score(batch, h):
                lane, b, n, pairs = batch
                if h == 0:
                    pe.wait_ge(s.kT, n)
                    pe.wait_ge(s.pick, n)
                rows = slice(XD * (h % 2), XD * (h % 2 + 1))
                nc.tensor.matmul(scores(h), pick[:, lane, :], bias[:, :], start=True, stop=False)
                nc.tensor.matmul(scores(h), t.qT[rows, h // 2, :], t.kT[rows, h // 2, 0:KEYS], start=False, stop=True).then_inc(a[h].scores_ready, 1)

            def turn_probs(batch, h):
                n = batch[2]
                pe.wait_ge(a[h].probs, n)
                if h > 0:
                    pe.wait_ge(a[h - 1].probsT, n)
                for j in range(KT):
                    last = nc.tensor.transpose(turned[0:width[j], j * S:(j + 1) * S], t.probs[:, h % 2, j * P:j * P + width[j]], g.ident[0:S, 0:S])
                last.then_inc(a[h].turned_ready, 1)

            def by_v(batch, h):
                lane, b, n, pairs = batch
                pe.wait_ge(a[h].probsT, n)
                for j in range(KT):
                    last = nc.tensor.matmul(heads_out[:, h, :], t.probsT[0:width[j], h % 2, j * S:(j + 1) * S], t.v[0:width[j], lane, j, h, :],
                                            start=(j == 0), stop=(j == KT - 1))
                if h == XH - 1:
                    last.then_inc(s.heads_ready, 1)

            def run(batch, after, third):
                n = batch[2]
                for h in range(XH):
                    if h < XH - 1:
                        score(batch, h + 1)
                    if after and h == 0:
                        make_q(after)
                    if after:
                        make_kv(after, h)
                    turn_probs(batch, h)
                    if h > 0:
                        by_v(batch, h - 1)
                if after:
                    turn_q(after)
                if third:
                    turn_rows(third)
                by_v(batch, XH - 1)
                if third:
                    turn_ctx(third, after)
                pe.wait_ge(s.heads, n)
                turn(nc, g, turned, t.heads[:, :], DC).then_inc(s.headsT_ready, 1)
                pe.wait_ge(s.headsT, n)
                for c in range(DC):
                    nc.tensor.matmul(out_bank[0:S, 0:D], t.headsT[:, c, :], w.proj[:, c, :], start=(c == 0), stop=False)
                nc.tensor.matmul(out_bank[0:S, 0:D], g.ones[0:1, 0:S], w.proj_b[:, :], start=False, stop=True).then_inc(s.proj_ready, 1)
                if after:
                    turn_k(after, third)
                    score(after, 0)
                    pe.wait_ge(s.added, n)

            turn_rows(FIRST)
            turn_ctx(FIRST, None)
            make_q(FIRST)
            for j in range(KT):
                make_kv(FIRST, j)
            turn_q(FIRST)
            turn_k(FIRST, None)
            pe.wait_ge(s.kT, 1)
            turn_rows(SECOND)
            turn_ctx(SECOND, FIRST)
            score(FIRST, 0)
            batches(pe, run)

        @block.scalar
        def _(act):
            act.wait_ge(g.loaded.cross, g.total.cross)
            act.wait_ge(s.ones, 3)

            def keep_rows(batch):
                act.wait_ge(s.yT_ready, batch[2])
                for c in range(DC):
                    last = nc.scalar.activation(t.lT[:, c, 0:S], row_bank[:, c * S:(c + 1) * S], ACT.Identity,
                                                bias=w.ln_l[:, DC + c:DC + c + 1], scale=w.ln_l[:, c:c + 1])
                last.then_inc(s.lT, 1)

            def keep_ctx(batch):
                act.wait_ge(s.ctxT_ready, batch[2])
                nc.scalar.activation(t.ctxT0[:, :], bank(4)[:, 0:NT * P], ACT.Identity,
                                     bias=w.ln_x0[:, 1:2], scale=w.ln_x0[:, 0:1]).then_inc(s.ctxT_act, 1)

            def square_q(batch):
                act.wait_ge(s.q_ready, batch[2])
                nc.scalar.activation(t.qsq[:, :], q_bank[0:S, 0:D], ACT.Square).then_inc(s.qsq, 1)

            def keep_kv(batch, j):
                lane, b, n, pairs = batch
                act.wait_ge(kv_ready[j], n)
                nc.scalar.copy(t.k[:, j, :], kv_bank(j)[:, 0:D])
                nc.scalar.copy(t.v[:, lane, j, :, 0:XD], by_head(kv_bank(j)[:, D:2 * D])).then_inc(kv_kept[j], 1)

            def square_k(batch, half):
                tiles = slice(half * HT, (half + 1) * HT)
                act.wait_ge(kv_kept[(half + 1) * HT - 1], batch[2])
                nc.scalar.activation(t.ksq[:, tiles, :], t.k[:, tiles, :], ACT.Square).then_inc(ksq[half], 1)

            def keep_k(batch):
                act.wait_ge(s.kT_ready, batch[2])
                nc.scalar.copy(t.kT[:, :, :], g.psum[:, 6:8, :]).then_inc(s.kT, 1)

            def weigh(batch, h):
                act.wait_ge(a[h].rowmax, batch[2])
                nc.scalar.activation(t.probs[:, h % 2, :], scores(h), ACT.Exp, bias=t.rowmax[:, h % 2:h % 2 + 1]).then_inc(a[h].probs, 1)

            def run(batch, after, third):
                n = batch[2]
                for h in range(XH):
                    if after and h == 0:
                        square_q(after)
                    if h < XH - 1:
                        weigh(batch, h + 1)
                    if after:
                        keep_kv(after, h)
                    act.wait_ge(a[h].turned_ready, n)
                    nc.scalar.copy(t.probsT[:, h % 2, :], turned[:, 0:KT * S]).then_inc(a[h].probsT, 1)
                    if after and h % HT == HT - 1:
                        square_k(after, h // HT)
                if third:
                    keep_rows(third)
                    keep_ctx(third)
                act.wait_ge(s.headsT_ready, n)
                nc.scalar.copy(t.headsT[:, :, :], chunks(turned)).then_inc(s.headsT, 1)
                if after:
                    keep_k(after)
                    weigh(after, 0)

            keep_rows(FIRST)
            keep_ctx(FIRST)
            square_q(FIRST)
            for j in range(KT):
                keep_kv(FIRST, j)
            for half in range(HALVES):
                square_k(FIRST, half)
            keep_k(FIRST)
            keep_rows(SECOND)
            keep_ctx(SECOND)
            weigh(FIRST, 0)
            batches(act, run)

        @block.vector
        def _(dve):
            dve.wait_ge(g.loaded.cross, g.total.cross)
            dve.wait_ge(s.ones, 3)
            nc.vector.tensor_scalar(bias[:, 0:CTX], w.mask[:, :], 1.0, -MASKED, ALU.subtract, ALU.mult).then_inc(s.bias, 1)
            nc.vector.memset(bias[:, NT * P:KEYS], 0.0).then_inc(s.bias, 1)
            nc.vector.memset(turned, 0.0).then_inc(s.turned_zero, 1)
            nc.vector.scalar_tensor_tensor(t.gain[:, :], w.qn_g[:, :], XD ** -0.5, w.kn_g[:, :], ALU.mult, ALU.mult).then_inc(s.gain, 1)
            dve.wait_ge(s.gain, 1)

            def row_stats(batch):
                norm_stats(nc, dve, m1, [(0, batch[1], batch[2])], lambda lane, b: g.x[:, b, :])

            def row_norm(batch):
                lane, b, n, pairs = batch
                norm_apply(nc, dve, m1, 0, n, t.y[:, :], g.x[:, b, :], s.y)
                dve.wait_ge(s.y, n)
                norm_stats(nc, dve, m2, [(0, b, n)], lambda lane, b: t.y[:, :])

            def second_norm(batch):
                norm_apply(nc, dve, m2, 0, batch[2], t.yy[:, :], t.y[:, :], s.yy)

            def ctx_stats(batch):
                lane, b, n, pairs = batch
                dve.wait_ge(raw_loaded[lane], dve.snap(pairs * 32))
                for j in range(NT):
                    last = nc.vector.bn_stats(t.cstats[:, j, :], t.raw[:, lane, j, :])
                last.then_inc(s.cstats, 1)
                dve.wait_ge(s.cstats, n)
                nc.vector.memset(t.chold[:, :], 0.0)
                for j in range(NT):
                    last = nc.vector.bn_aggr(t.cmeanvar[:, j, :], t.cstats[:, j, :])
                last.then_inc(s.cmeanvar, 1)

            def ctx_norm(batch):
                lane, b, n, pairs = batch
                dve.wait_ge(s.crstd, n)
                for j in range(NT):
                    last = nc.vector.tensor_scalar(t.cn[:, j, :], t.raw[:, lane, j, :], t.cmeanvar[:, j, 0:1], t.crstd[:, j:j + 1], ALU.subtract, ALU.mult)
                last.then_inc(s.cn, 1)

            def keep_ctx(batch):
                dve.wait_ge(s.ctxT_ready, batch[2])
                nc.vector.tensor_scalar(t.ctxT1[:, :], bank(5)[0:CD - P, 0:NT * P], w.ln_x1[:, 0:1], w.ln_x1[:, 1:2], ALU.mult, ALU.add).then_inc(s.ctxT_dve, 1)

            def mean_q(batch):
                n = batch[2]
                dve.wait_ge(s.qsq, n)
                nc.vector.reduce_sum(t.qsum[:, :], by_head(t.qsq[:, :]), AX.X).then_inc(s.qsum, 1)
                dve.wait_ge(s.qsum, n)
                nc.vector.tensor_scalar(t.qclip[:, :], t.qsum[:, :], 1.0 / XD, 1e-16, ALU.mult, ALU.max).then_inc(s.qclip, 1)

            def norm_q(batch):
                dve.wait_ge(s.qroot, batch[2])
                nc.vector.tensor_tensor(by_head(t.qn[:, :]), by_head(q_bank[0:S, 0:D]), t.qroot[:, :].unsqueeze(2).broadcast_to([S, XH, XD]),
                                        ALU.mult).then_inc(s.qn, 1)

            def keep_q(batch):
                dve.wait_ge(s.qT_ready, batch[2])
                nc.vector.tensor_scalar(t.qT[:, :, :], chunks(q_bank), t.gain[:, :], None, ALU.mult).then_inc(s.qT, 1)

            def mean_k(batch, half):
                n, at, tiles = batch[2], slice(half * HT * XH, (half + 1) * HT * XH), slice(half * HT, (half + 1) * HT)
                dve.wait_ge(ksq[half], n)
                nc.vector.reduce_sum(t.ksum[:, at], t.ksq[:, tiles, :].rearrange("p t (h d) -> p (t h) d", d=XD), AX.X).then_inc(ksum[half], 1)
                dve.wait_ge(ksum[half], n)
                nc.vector.tensor_scalar(t.kclip[:, at], t.ksum[:, at], 1.0 / XD, 1e-16, ALU.mult, ALU.max).then_inc(kclip[half], 1)

            def norm_k(batch, half):
                at, rows = slice(half * HT * XH, (half + 1) * HT * XH), t.k[:, half * HT:(half + 1) * HT, :].rearrange("p t (h d) -> p (t h) d", d=XD)
                dve.wait_ge(kroot[half], batch[2])
                nc.vector.tensor_tensor(rows, rows, t.kroot[:, at].unsqueeze(2).broadcast_to([P, HT * XH, XD]), ALU.mult).then_inc(kn[half], 1)

            def peak(batch, h):
                dve.wait_ge(a[h].scores_ready, batch[2])
                nc.vector.reduce_max(t.rowmax[:, h % 2:h % 2 + 1], scores(h), AX.X, negate=True).then_inc(a[h].rowmax, 1)

            def run(batch, after, third):
                lane, b, n, pairs = batch
                for h in range(XH):
                    if h < XH - 1:
                        peak(batch, h + 1)
                    if after and h == 0:
                        mean_q(after)
                    if third and h == 0:
                        row_stats(third)
                    if after and h == 1:
                        norm_q(after)
                    if third and h == 1:
                        row_norm(third)
                    if after and h == 2:
                        mean_k(after, 0)
                    if third and h == 2:
                        ctx_stats(third)
                        second_norm(third)
                    if after and h == 3:
                        norm_k(after, 0)
                    if third and h == 3:
                        ctx_norm(third)
                if after:
                    keep_q(after)
                    mean_k(after, 1)
                dve.wait_ge(s.heads_ready, n)
                nc.vector.reciprocal(t.rowsum[:, :].unsqueeze(2), heads_out[:, :, XD:XD + 1]).then_inc(s.rowsum, 1)
                dve.wait_ge(s.rowsum, n)
                nc.vector.tensor_tensor(by_head(t.heads[:, :]), heads_out[:, :, 0:XD], t.rowsum[:, :].unsqueeze(2).broadcast_to([S, XH, XD]),
                                        ALU.mult).then_inc(s.heads, 1)
                if after:
                    norm_k(after, 1)
                if third:
                    keep_ctx(third)
                dve.wait_ge(s.proj_ready, n)
                nc.vector.tensor_tensor(g.x[:, b, :], g.x[:, b, :], out_bank[0:S, 0:D], ALU.add).then_inc(s.added, 1)
                if after:
                    peak(after, 0)

            for batch in (FIRST, SECOND):
                row_stats(batch)
                row_norm(batch)
                ctx_stats(batch)
                second_norm(batch)
                ctx_norm(batch)
                if batch is SECOND:
                    keep_ctx(batch)
                    break
                keep_ctx(batch)
                mean_q(batch)
                norm_q(batch)
                for half in range(HALVES):
                    mean_k(batch, half)
                    norm_k(batch, half)
                keep_q(batch)
            peak(FIRST, 0)
            batches(dve, run)



TWO_PI_HI = float(np.float32(6.28125))
TWO_PI_LO = float(2 * np.pi - 6.28125)
PI_BELOW = float(np.nextafter(np.float32(np.pi), np.float32(0)))
NQ = 8


ROTATED = NH // RG
SETS = 2
GROUPS = [(lane, part) for part in (1, 0) for lane in range(LANES)]
VROWS = 32


def rotation_phase(nc, g, w):
    STEPS = len(GROUPS) * RG
    with ExitStack() as ctx:
        s = semaphores(nc, ctx, "rot", "filled folded_ready folded turns whole_i whole near angle size cosine sine k_bias y yT_ready yT mean_ready mean "
                       "k_norms_ready k_norms kT_ready kmin spread_in spread_ready ends q_norms_ready span inverse ratios ratio heads headsT_ready headsT "
                       "proj_ready added")
        each = lambda name, count: [ctx.enter_context(nc.semaphore(f"rot_{name}{k}")) for k in range(count)]
        qk_ready, q_kept, k_kept, v_ready, v_kept = (each(n, LANES) for n in ("qk_ready", "q_kept", "k_kept", "v_ready", "v_kept"))
        h_ready, h_done = each("tanh_in_ready", STEPS), each("tanh", STEPS)
        vectors_ready, turned, mixed_ready, squares = (each(n, len(GROUPS)) for n in ("vectors_ready", "turned", "mixed_ready", "squares"))
        t = buffers(nc, ctx, "rot", y=[S, LANES, D], yT=[P, LANES, DC, S], q=[P, SETS, LANES, 2, QT * S], v=[S, LANES, D],
                    h=[P, 2, DC, QT * S], w1=[P, RG, D], w2=[P, DC, VROWS], b2=[P, 1], k_bias=[P, 2, DC], cos=[P, PAIRS, ROTATED], sin=[P, PAIRS, ROTATED],
                    turns=[P, 4, ROTATED], near=[P, 4, ROTATED], angle=[P, 4, ROTATED], size=[P, 4, ROTATED],
                    by_cos=[P, LANES, 2, QT * S], by_sin=[P, LANES, 2, QT * S], squares=[VROWS, LANES, 2, QT * S],
                    k_norms=[S, LANES, NH], k_ends=[NH, 2 * LANES], spread=[NH, 2 * LANES, NH], ends=[S, 2, LANES * NH], span=[S, 2, LANES * NH],
                    inverse=[S, 2, LANES * NH], ratios=[S, 2, LANES * NH], ratio=[S, LANES, NH], mean=[S, LANES, D], heads=[S, LANES, D],
                    headsT=[P, LANES, DC, S])
        whole = ctx.enter_context(nc.sbuf_tensor("rot_whole", [P, 4, ROTATED], I32))
        m1 = norm_of(nc, ctx, "rot_ln")
        tanh_in = lambda k, m: g.psum[:, k % 2 * DC + m, 0:QT * S]
        vec = lambda group: g.psum[:, 4 + group % 2, :]
        make, side = g.psum[:, 6, :], g.psum[:, 7, :]
        by_lane = lambda ps: ps[0:S, :].rearrange("s (l d) -> s l d", l=LANES)
        by_chunk = lambda ps: ps[:, 0:LANES * DC * S].rearrange("p (l c s) -> p l c s", l=LANES, c=DC)
        block = ctx.enter_context(nc.Block())

        def pair_of(eng, pair):
            fixed = isinstance(pair, int)
            at = (lambda e: e) if fixed else eng.snap
            return pair, at(pair + 1), [(lane, at(pair * LANES + lane), at(pair * LANES + lane + 1)) for lane in range(LANES)]

        def pairs(eng, run):
            with eng.Fori(0, PAIRS // SETS - 1) as two:
                some = [(k % SETS, *pair_of(eng, eng.snap(two * SETS + k))) for k in range(SETS + 1)]
                for k in range(SETS):
                    run(some[k], some[k + 1])
            ends = [(k % SETS, *pair_of(eng, PAIRS - SETS + k)) for k in range(SETS)]
            run(ends[0], ends[1])
            run(ends[1], None)

        FIRST = (0, *pair_of(None, 0))

        @block.gpsimd
        def _(pool):
            nc.gpsimd.memset(t.cos[:, :, :], 1.0).then_inc(s.filled, 1)
            nc.gpsimd.memset(t.sin[:, :, :], 0.0).then_inc(s.filled, 1)
            nc.gpsimd.memset(t.w1[:, :, :], 0.0).then_inc(s.filled, 1)
            with pool.Fori(0, PAIRS) as pair:
                for lane, b, n in lanes_of(pool, pair):
                    norm_root(nc, pool, g, m1, lane, n)

        @block.tensor
        def _(pe):
            pe.wait_ge(g.loaded.rot, g.total.rot)
            for c in range(DC):
                nc.tensor.matmul(make[:, c * VROWS:(c + 1) * VROWS], w.w2T[:, c * P:(c + 1) * P], w.hadamard[:, 0:VROWS], start=True, stop=True)
            nc.tensor.matmul(side[:, 0:1], w.hadamard[:, :], w.b2[:, :], start=True, stop=True).then_inc(s.folded_ready, 1)
            pe.wait_ge(s.folded, 1)

            def make_rows(pr):
                pe.wait_ge(s.y, pr[3][-1][2])
                for lane in range(LANES):
                    last = turn(nc, g, make[:, lane * DC * S:], t.y[:, lane, :], DC)
                last.then_inc(s.yT_ready, 1)

            def make_qk(pr, lane):
                if lane == 0:
                    pe.wait_ge(s.yT, pr[2])
                else:
                    pe.wait_ge(q_kept[lane - 1], pr[2])
                    pe.wait_ge(k_kept[lane - 1], pr[2])
                for m in range(2 * DC):
                    for c in range(DC):
                        last = nc.tensor.matmul(make[:, m * S:(m + 1) * S], w.qkv[:, c, m * P:(m + 1) * P], t.yT[:, lane, c, :], start=(c == 0), stop=(c == DC - 1))
                last.then_inc(qk_ready[lane], 1)

            def make_v(pr, lane):
                if lane == 0:
                    pe.wait_ge(q_kept[LANES - 1], pr[2])
                    pe.wait_ge(k_kept[LANES - 1], pr[2])
                else:
                    pe.wait_ge(v_kept[lane - 1], pr[2])
                for c in range(DC):
                    nc.tensor.matmul(make[0:S, 0:D], t.yT[:, lane, c, :], w.qkv[:, c, 2 * D:3 * D], start=(c == 0), stop=False)
                nc.tensor.matmul(make[0:S, 0:D], g.ones[0:1, 0:S], w.v_b[:, :], start=False, stop=True).then_inc(v_ready[lane], 1)

            def mean(pr):
                pe.wait_ge(v_kept[LANES - 1], pr[2])
                last = nc.tensor.matmul(make[0:S, :], w.uniform[:, :], t.v[:, :, :].rearrange("s l d -> s (l d)"), start=True, stop=True)
                last.then_inc(s.mean_ready, 1)

            def first_layer(pr, k):
                group, r = k // RG, k % RG
                lane, part = GROUPS[group]
                if r == 0:
                    pe.wait_ge((k_kept if part else q_kept)[lane], pr[2])
                for m in range(DC):
                    last = nc.tensor.matmul(tanh_in(k, m), t.w1[:, r, m * P:(m + 1) * P], t.q[:, pr[0], lane, part, :], start=True, stop=True)
                last.then_inc(h_ready[k], 1)

            def last_layer(pr, k):
                group, r = k // RG, k % RG
                if r == 0 and group >= 2:
                    pe.wait_ge(turned[group - 2], pr[2])
                pe.wait_ge(h_done[k], pr[2])
                for m in range(DC):
                    last = nc.tensor.matmul(vec(group)[VROWS * r:VROWS * (r + 1), 0:QT * S], t.w2[:, m, :], t.h[:, k % 2, m, :], start=(m == 0), stop=(m == DC - 1))
                if r == RG - 1:
                    last.then_inc(vectors_ready[group], 1)

            def mix(pr, group, bank):
                lane, part = GROUPS[group]
                if lane == 0:
                    pe.wait_ge(turned[group], pr[2])
                    pe.wait_ge(turned[group + 1], pr[2])
                nc.tensor.matmul(bank[0:VROWS, 0:QT * S], w.real[:, :], t.by_cos[:, lane, part, :], start=True, stop=False)
                nc.tensor.matmul(bank[0:VROWS, 0:QT * S], w.imag[:, :], t.by_sin[:, 1 - lane, part, :], start=False, stop=True).then_inc(mixed_ready[group], 1)

            def norms(pr, part, ready):
                for lane in range(LANES):
                    pe.wait_ge(squares[GROUPS.index((lane, part))], pr[2])
                for lane in range(LANES):
                    for j in range(ROTATED):
                        at = (lane * ROTATED + j) * RG
                        last = nc.tensor.matmul(side[0:S, at:at + RG], t.squares[:, lane, part, j * S:(j + 1) * S], w.sum8[:, :], start=True, stop=True)
                last.then_inc(ready, 1)

            def run(pr, after):
                n = pr[2]
                for k in range(STEPS):
                    if 0 < k < STEPS - 1:
                        first_layer(pr, k + 1)
                    elif k == STEPS - 1 and after:
                        first_layer(after, 0)
                    if k == 0:
                        mean(pr)
                    elif k == 2 and after:
                        pe.wait_ge(s.mean, n)
                        make_rows(after)
                    elif k == 4 and after:
                        make_qk(after, 0)
                    elif k == 11:
                        norms(pr, 1, s.k_norms_ready)
                    elif k == 12:
                        pe.wait_ge(s.k_norms, n)
                        for lane in range(LANES):
                            last = nc.tensor.transpose(side[0:NH, lane * S:(lane + 1) * S], t.k_norms[:, lane, :], g.ident[0:S, 0:S])
                        last.then_inc(s.kT_ready, 1)
                    last_layer(pr, k)
                    if k == 8:
                        mix(pr, 0, side)
                    elif k == 9:
                        pe.wait_ge(squares[0], n)
                        mix(pr, 1, side)
                    elif k == 13:
                        pe.wait_ge(s.spread_in, n)
                        nc.tensor.matmul(side[0:S, 0:2 * LANES * NH], g.ones[0:NH, 0:S], t.spread[:, :, :].rearrange("h a b -> h (a b)"),
                                         start=True, stop=True).then_inc(s.spread_ready, 1)
                if after:
                    make_qk(after, 1)
                mix(pr, 2, vec(2))
                mix(pr, 3, vec(3))
                if after:
                    make_v(after, 0)
                pe.wait_ge(s.ends, n)
                norms(pr, 0, s.q_norms_ready)
                if after:
                    first_layer(after, 1)
                pe.wait_ge(s.heads, n)
                for lane in range(LANES):
                    last = turn(nc, g, vec(0)[:, lane * DC * S:], t.heads[:, lane, :], DC)
                last.then_inc(s.headsT_ready, 1)
                if after:
                    make_v(after, 1)
                pe.wait_ge(s.headsT, n)
                for lane in range(LANES):
                    rows = by_lane(vec(1))[:, lane, :]
                    for c in range(DC):
                        nc.tensor.matmul(rows, t.headsT[:, lane, c, :], w.proj[:, c, :], start=(c == 0), stop=False)
                    last = nc.tensor.matmul(rows, g.ones[0:1, 0:S], w.proj_b[:, :], start=False, stop=True)
                last.then_inc(s.proj_ready, 1)
                if after:
                    pe.wait_ge(s.added, n)

            make_rows(FIRST)
            for lane in range(LANES):
                make_qk(FIRST, lane)
            for lane in range(LANES):
                make_v(FIRST, lane)
            for k in range(2):
                first_layer(FIRST, k)
            pairs(pe, run)

        @block.scalar
        def _(act):
            act.wait_ge(s.filled, 3)
            act.wait_ge(s.angle, 1)
            nc.scalar.activation(t.sin[:, 0:NQ // 2, :], t.angle[:, :, :], ACT.Sin).then_inc(s.sine, 1)
            act.wait_ge(s.size, 2)
            nc.scalar.activation(t.cos[:, 0:NQ // 2, :], t.size[:, :, :], ACT.Sin).then_inc(s.cosine, 1)
            act.wait_ge(s.k_bias, 1)

            def keep_rows(pr):
                act.wait_ge(s.yT_ready, pr[2])
                nc.scalar.copy(t.yT[:, :, :, :], by_chunk(make)).then_inc(s.yT, 1)

            def keep_k(pr, lane):
                act.wait_ge(q_kept[lane], pr[2])
                for e in range(2):
                    for c in range(DC):
                        at = (e * DC + c) * S
                        last = nc.scalar.activation(t.q[:, pr[0], lane, 1, at:at + S], make[:, (DC + c) * S:(DC + c + 1) * S], ACT.Identity,
                                                    bias=t.k_bias[:, e, c:c + 1], scale=w.half[:, e:e + 1])
                last.then_inc(k_kept[lane], 1)

            def keep_v(pr, lane):
                act.wait_ge(v_ready[lane], pr[2])
                nc.scalar.copy(t.v[:, lane, :], make[0:S, 0:D]).then_inc(v_kept[lane], 1)

            def tanh(pr, k):
                act.wait_ge(h_ready[k], pr[2])
                for m in range(DC):
                    last = nc.scalar.activation(t.h[:, k % 2, m, :], tanh_in(k, m), ACT.Tanh, bias=w.b1[:, m:m + 1])
                last.then_inc(h_done[k], 1)

            def square(pr, group, bank):
                lane, part = GROUPS[group]
                act.wait_ge(mixed_ready[group], pr[2])
                nc.scalar.activation(t.squares[:, lane, part, :], bank[0:VROWS, 0:QT * S], ACT.Square).then_inc(squares[group], 1)

            def run(pr, after):
                n = pr[2]
                for k in range(STEPS):
                    if 0 < k < STEPS - 1:
                        tanh(pr, k + 1)
                    elif k == STEPS - 1 and after:
                        tanh(after, 0)
                    if k == 0:
                        act.wait_ge(s.mean_ready, n)
                        nc.scalar.copy(t.mean[:, :, :], by_lane(make)).then_inc(s.mean, 1)
                    elif k == 2 and after:
                        keep_rows(after)
                    elif k == 4 and after:
                        keep_k(after, 0)
                    elif k == 8:
                        square(pr, 0, side)
                    elif k == 9:
                        square(pr, 1, side)
                if after:
                    keep_k(after, 1)
                square(pr, 2, vec(2))
                square(pr, 3, vec(3))
                if after:
                    keep_v(after, 0)
                    tanh(after, 1)
                act.wait_ge(s.headsT_ready, n)
                nc.scalar.copy(t.headsT[:, :, :, :], by_chunk(vec(0))).then_inc(s.headsT, 1)
                if after:
                    keep_v(after, 1)

            keep_rows(FIRST)
            for lane in range(LANES):
                keep_k(FIRST, lane)
            for lane in range(LANES):
                keep_v(FIRST, lane)
            for k in range(2):
                tanh(FIRST, k)
            pairs(act, run)

        @block.vector
        def _(dve):
            dve.wait_ge(g.loaded.rot, g.total.rot)
            nc.vector.tensor_scalar(t.turns[:, :, :], w.rot[:, :, :], 0.25 / np.pi, None, ALU.mult).then_inc(s.turns, 1)
            dve.wait_ge(s.turns, 1)
            nc.vector.tensor_copy(whole[:, :, :], t.turns[:, :, :]).then_inc(s.whole_i, 1)
            dve.wait_ge(s.whole_i, 1)
            nc.vector.tensor_copy(t.turns[:, :, :], whole[:, :, :]).then_inc(s.whole, 1)
            nc.vector.tensor_scalar(t.near[:, :, :], w.rot[:, :, :], 0.5, None, ALU.mult).then_inc(s.whole, 1)
            dve.wait_ge(s.whole, 2)
            nc.vector.scalar_tensor_tensor(t.near[:, :, :], t.turns[:, :, :], -TWO_PI_HI, t.near[:, :, :], ALU.mult, ALU.add).then_inc(s.near, 1)
            dve.wait_ge(s.near, 1)
            nc.vector.scalar_tensor_tensor(t.near[:, :, :], t.turns[:, :, :], -TWO_PI_LO, t.near[:, :, :], ALU.mult, ALU.add).then_inc(s.near, 1)
            dve.wait_ge(s.near, 2)
            nc.vector.tensor_scalar(t.angle[:, :, :], t.near[:, :, :], PI_BELOW, -PI_BELOW, ALU.min, ALU.max).then_inc(s.angle, 1)
            dve.wait_ge(s.angle, 1)
            nc.vector.scalar_tensor_tensor(t.size[:, :, :], t.angle[:, :, :], -1.0, t.angle[:, :, :], ALU.mult, ALU.max).then_inc(s.size, 1)
            dve.wait_ge(s.size, 1)
            nc.vector.tensor_scalar(t.size[:, :, :], t.size[:, :, :], -1.0, float(np.pi / 2), ALU.mult, ALU.add).then_inc(s.size, 1)
            for e in range(2):
                last = nc.vector.tensor_scalar(t.k_bias[:, e, :], w.qk_b[:, DC:2 * DC], w.half[:, e:e + 1], None, ALU.mult)
            last.then_inc(s.k_bias, 1)
            dve.wait_ge(s.filled, 3)
            for r in range(RG):
                rows = slice(ROWS * r, ROWS * (r + 1))
                nc.vector.tensor_copy(t.w1[rows, r, :], w.w1[rows, :])
            dve.wait_ge(s.folded_ready, 1)
            nc.vector.tensor_copy(t.w2[:, :, :], make[:, 0:DC * VROWS].rearrange("p (c v) -> p c v", v=VROWS))
            nc.vector.tensor_copy(t.b2[:, :], side[:, 0:1]).then_inc(s.folded, 1)
            dve.wait_ge(s.folded, 1)
            dve.wait_ge(s.sine, 1)
            dve.wait_ge(s.cosine, 1)

            def stats(pr):
                norm_stats(nc, dve, m1, pr[3], lambda lane, b: g.x[:, b, :])

            def apply(pr):
                for lane, b, n in pr[3]:
                    norm_apply(nc, dve, m1, lane, n, t.y[:, lane, :], g.x[:, b, :], s.y)

            def keep_q(pr, lane):
                dve.wait_ge(qk_ready[lane], pr[2])
                for e in range(2):
                    for c in range(DC):
                        at = (e * DC + c) * S
                        last = nc.vector.tensor_scalar(t.q[:, pr[0], lane, 0, at:at + S], make[:, c * S:(c + 1) * S], w.qk_b[:, c:c + 1],
                                                       w.half[:, e:e + 1], ALU.add, ALU.mult)
                last.then_inc(q_kept[lane], 1)

            def turn_by(pr, group):
                lane, part = GROUPS[group]
                rows = vec(group)[:, 0:QT * S].rearrange("p (j s) -> p j s", s=S)
                dve.wait_ge(vectors_ready[group], pr[2])
                for table, out in ((t.cos, t.by_cos), (t.sin, t.by_sin)):
                    last = nc.vector.scalar_tensor_tensor(out[:, lane, part, :].rearrange("p (j s) -> p j s", s=S), rows, t.b2[:, :],
                                                          table[:, pr[1], :].unsqueeze(2).broadcast_to([P, ROTATED, S]), ALU.add, ALU.mult)
                last.then_inc(turned[group], 1)

            def run(pr, after):
                n = pr[2]
                if after:
                    stats(after)
                    apply(after)
                for k in range(STEPS):
                    if k == 4 and after:
                        keep_q(after, 0)
                    elif k == 11:
                        dve.wait_ge(s.k_norms_ready, n)
                        nc.vector.tensor_copy(t.k_norms[:, :, :].rearrange("s l h -> s (l h)"), side[0:S, 0:LANES * NH]).then_inc(s.k_norms, 1)
                    if k % RG == RG - 1:
                        turn_by(pr, k // RG)
                    if k == 12:
                        dve.wait_ge(s.kT_ready, n)
                        kT = side[0:NH, 0:LANES * S].rearrange("h (l s) -> h l s", s=S)
                        nc.vector.reduce_max(t.k_ends[:, 0:LANES], kT, AX.X)
                        nc.vector.tensor_reduce(t.k_ends[:, LANES:2 * LANES], kT, AX.X, ALU.min).then_inc(s.kmin, 1)
                        dve.wait_ge(s.kmin, n)
                        nc.vector.tensor_tensor(t.spread[:, :, :], g.ident[0:NH, 0:NH].unsqueeze(1).broadcast_to([NH, 2 * LANES, NH]),
                                                t.k_ends[:, :].unsqueeze(2).broadcast_to([NH, 2 * LANES, NH]), ALU.mult).then_inc(s.spread_in, 1)
                    elif k == 13:
                        dve.wait_ge(s.spread_ready, n)
                        nc.vector.tensor_copy(t.ends[:, :, :].rearrange("s k h -> s (k h)"), side[0:S, 0:2 * LANES * NH]).then_inc(s.ends, 1)
                if after:
                    keep_q(after, 1)
                dve.wait_ge(s.q_norms_ready, n)
                nc.vector.tensor_tensor(t.span[:, :, :], side[0:S, 0:LANES * NH].unsqueeze(1).broadcast_to([S, 2, LANES * NH]), t.ends[:, :, :],
                                        ALU.mult).then_inc(s.span, 1)
                dve.wait_ge(s.span, n)
                nc.vector.reciprocal(t.inverse[:, :, :], t.span[:, :, :]).then_inc(s.inverse, 1)
                dve.wait_ge(s.inverse, n)
                nc.vector.tensor_tensor(t.ratios[:, :, :], t.span[:, :, :], t.inverse[:, :, :], ALU.mult).then_inc(s.ratios, 1)
                dve.wait_ge(s.ratios, n)
                for lane in range(LANES):
                    least, most = (t.ratios[:, k, lane * NH:(lane + 1) * NH].rearrange("s (e c r) -> s e c r", e=2, c=DC) for k in range(2))
                    last = nc.vector.tensor_tensor(t.ratio[:, lane, :].rearrange("s (c r e) -> s e c r", c=DC, e=2), least, most, ALU.mult)
                last.then_inc(s.ratio, 1)
                dve.wait_ge(s.ratio, n)
                dve.wait_ge(s.mean, n)
                nc.vector.tensor_tensor(t.heads[:, :, :].rearrange("s l (h d) -> s (l h) d", d=HD), t.mean[:, :, :].rearrange("s l (h d) -> s (l h) d", d=HD),
                                        t.ratio[:, :, :].rearrange("s l h -> s (l h)").unsqueeze(2).broadcast_to([S, LANES * NH, HD]), ALU.mult).then_inc(s.heads, 1)
                dve.wait_ge(s.proj_ready, n)
                for lane, b, nb in pr[3]:
                    last = nc.vector.tensor_tensor(g.x[:, b, :], g.x[:, b, :], by_lane(vec(1))[:, lane, :], ALU.add)
                last.then_inc(s.added, 1)

            stats(FIRST)
            apply(FIRST)
            for lane in range(LANES):
                keep_q(FIRST, lane)
            pairs(dve, run)



WIDE_TILES = [(0, 121), (121, 120), (241, 120)]
ITEM = 2
ITEMS = WH // ITEM
MADE = [("k", 0), ("k", 1), ("k", 2), ("k", 3), ("y", 0), ("k", 4), ("k", 5), ("k", 6), ("k", 7), ("q", 0), ("q", 1)] + [
    ("v", 2 * j + half) for j in range(len(WIDE_TILES)) for half in range(2)]
NEXT_LAST = len(MADE) - 1
BETWEEN = 2 * (ITEMS - 2)
BY_ACT = lambda u: u % 2 == 0


def wide_cross_phase(nc, g, w, ctxT_in):
    TMAX = WIDE_TILES[0][1]
    with ExitStack() as ctx:
        s = semaphores(nc, ctx, "wide", "ones bias turned_zero any_key any_inverse any y headsT_ready headsT_act headsT_dve proj_ready added")
        made = [ctx.enter_context(nc.semaphore(f"wide_made_{k}{i}")) for k, i in MADE]
        kept = [ctx.enter_context(nc.semaphore(f"wide_kept_{k}{i}")) for k, i in MADE]
        a = [semaphores(nc, ctx, f"wide{i}", "scores_ready rowmax probs turned_ready probsT_act probsT_dve heads_ready rowsum heads") for i in range(ITEMS)]
        ctx_loaded = [ctx.enter_context(nc.semaphore(f"wide_ctx_loaded{lane}")) for lane in range(LANES)]
        t = buffers(nc, ctx, "wide", y=[S, LANES, D], yT=[P, LANES, DC, S], c0=[P, LANES, CTX], c1=[CD - P, LANES, CTX], kT=[P, LANES, WM, CTX],
                    v=[TMAX, LANES, NT, WH, WD + 1], qT=[P, LANES, WM, S], rowmax=[S, 2, ITEM], probs=[S, 2, ITEM, CTX],
                    probsT=[TMAX, 2, ITEM, NT * S], rowsum=[S, ITEM], heads=[S, LANES, WI], headsT=[P, LANES, WM, S], any_key=[S, 1], any_inverse=[S, 1], any=[S, 1])
        bias = ctx.enter_context(nc.sbuf_tensor("wide_bias", [S, CTX], BF16))
        m1 = norm_of(nc, ctx, "wide_ln")
        scores = lambda i: g.psum[0:S, i % 2 * ITEM:(i % 2 + 1) * ITEM, 0:CTX]
        turned, out_bank, make_bank = lambda j: g.psum[:, 4 + j, :], g.psum[:, 6, :], g.psum[:, 7, :]
        item_out = out_bank[0:S, 0:ITEM * (WD + 1)].rearrange("s (h d) -> s h d", d=WD + 1)
        four = lambda ps: ps[:, 0:4 * S].rearrange("p (c s) -> p c s", s=S)
        block = ctx.enter_context(nc.Block())

        def batches(eng, run):
            with eng.Fori(0, PAIRS - 1) as pair:
                here = [(lane, b, n, eng.snap(pair + 1)) for lane, b, n in lanes_of(eng, pair)]
                after = (0, eng.snap(pair * LANES + LANES), eng.snap(pair * LANES + LANES + 1), eng.snap(pair + 2))
                run(here[0], here[1])
                run(here[1], after)
            run((0, B - 2, B - 1, PAIRS), (1, B - 1, B, PAIRS))
            run((1, B - 1, B, PAIRS), None)

        FIRST = (0, 0, 1, 1)

        def load_ctx(sp, lane, b):
            sp.dma_start(t.c0[:, lane, :], ctxT_in[0:P, b, :]).then_inc(ctx_loaded[lane], 16)
            sp.dma_start(t.c1[:, lane, :], ctxT_in[P:CD, b, :]).then_inc(ctx_loaded[lane], 16)

        @block.sync
        def _(sp):
            for lane in range(LANES):
                load_ctx(sp, lane, lane)
            with sp.Fori(1, PAIRS) as pair:
                for lane, b, n in lanes_of(sp, pair):
                    sp.wait_ge(made[NEXT_LAST], sp.snap(b - 1))
                    load_ctx(sp, lane, b)

        @block.gpsimd
        def _(pool):
            nc.gpsimd.memset(t.v[:, :, :, :, WD:WD + 1], 1.0).then_inc(s.ones, 1)
            with pool.Fori(0, PAIRS) as pair:
                for lane, b, n in lanes_of(pool, pair):
                    norm_root(nc, pool, g, m1, lane, n)

        @block.tensor
        def _(pe):
            pe.wait_ge(g.loaded.wide, g.total.wide)
            pe.wait_ge(s.ones, 1)
            pe.wait_ge(s.bias, 1)
            pe.wait_ge(s.turned_zero, 1)

            def make(batch, u):
                lane, b, n, pairs = batch
                kind, i = MADE[u]
                if u == 0:
                    pe.wait_ge(ctx_loaded[lane], pe.snap(pairs * 32))
                    if b is not FIRST[1]:
                        pe.wait_ge(kept[NEXT_LAST], pe.snap(n - 1))
                else:
                    pe.wait_ge(kept[u - 1], n)
                if kind == "y":
                    pe.wait_ge(s.y, n)
                    last = turn(nc, g, make_bank, t.y[:, lane, :], DC)
                elif kind == "k":
                    nc.tensor.matmul(make_bank[:, 0:CTX], w.k0[:, i * P:(i + 1) * P], t.c0[:, lane, :], start=True, stop=False)
                    last = nc.tensor.matmul(make_bank[:, 0:CTX], w.k1[:, i * P:(i + 1) * P], t.c1[:, lane, :], start=False, stop=True)
                elif kind == "q":
                    for m in range(4 * i, 4 * i + 4):
                        for c in range(DC):
                            last = nc.tensor.matmul(make_bank[:, m % 4 * S:(m % 4 + 1) * S], w.q[:, c, m * P:(m + 1) * P], t.yT[:, lane, c, :],
                                                    start=(c == 0), stop=(c == DC - 1))
                else:
                    (k0, kw), cols = WIDE_TILES[i // 2], slice(i % 2 * BANK, (i % 2 + 1) * BANK)
                    nc.tensor.matmul(make_bank[0:kw, :], t.c0[:, lane, k0:k0 + kw], w.v0[:, cols], start=True, stop=False)
                    last = nc.tensor.matmul(make_bank[0:kw, :], t.c1[:, lane, k0:k0 + kw], w.v1[:, cols], start=False, stop=True)
                last.then_inc(made[u], 1)

            def score(batch, i):
                lane, b, n, pairs = batch
                if i == 0:
                    pe.wait_ge(kept[MADE.index(("q", 1))], n)
                    pe.wait_ge(kept[MADE.index(("q", 0))], n)
                for j in range(ITEM):
                    nc.tensor.matmul(scores(i)[:, j, :], g.ident_b[0:S, 0:S], bias[:, :], start=True, stop=False)
                for j in range(ITEM):
                    h = i * ITEM + j
                    rows = slice(WD * (h % 2), WD * (h % 2 + 1))
                    last = nc.tensor.matmul(scores(i)[:, j, :], t.qT[rows, lane, h // 2, :], t.kT[rows, lane, h // 2, :], start=False, stop=True)
                last.then_inc(a[i].scores_ready, 1)

            def heads_out(batch, i):
                lane, b, n, pairs = batch
                pe.wait_ge(a[i].probsT_act, n)
                pe.wait_ge(a[i].probsT_dve, n)
                if i == 0:
                    pe.wait_ge(kept[NEXT_LAST], n)
                    pe.wait_ge(kept[NEXT_LAST - 1], n)
                else:
                    pe.wait_ge(a[i - 1].heads, n)
                for j in range(ITEM):
                    for k, (k0, kw) in enumerate(WIDE_TILES):
                        last = nc.tensor.matmul(item_out[:, j, :], t.probsT[0:kw, i % 2, j, k * S:(k + 1) * S], t.v[0:kw, lane, k, i * ITEM + j, :],
                                                start=(k == 0), stop=(k == NT - 1))
                last.then_inc(a[i].heads_ready, 1)

            def run(batch, after):
                lane, b, n, pairs = batch
                for i in range(ITEMS):
                    end = i == ITEMS - 1
                    if not end:
                        score(batch, i + 1)
                    elif after:
                        score(after, 0)
                    if after and 2 * i < BETWEEN:
                        make(after, 2 * i)
                    elif after and end:
                        make(after, BETWEEN)
                    pe.wait_ge(a[i].probs, n)
                    if i > 0:
                        pe.wait_ge(a[i - 1].probsT_act, n)
                        pe.wait_ge(a[i - 1].probsT_dve, n)
                    for j in range(ITEM):
                        for k, (k0, kw) in enumerate(WIDE_TILES):
                            last = nc.tensor.transpose(turned(j)[0:kw, k * S:(k + 1) * S], t.probs[:, i % 2, j, k0:k0 + kw], g.ident[0:S, 0:S])
                    last.then_inc(a[i].turned_ready, 1)
                    if i > 0:
                        heads_out(batch, i - 1)
                    if after and 2 * i < BETWEEN:
                        make(after, 2 * i + 1)
                    elif after and end:
                        make(after, BETWEEN + 1)
                heads_out(batch, ITEMS - 1)
                if after:
                    make(after, BETWEEN + 2)
                pe.wait_ge(a[ITEMS - 1].heads, n)
                for m in range(WM):
                    last = nc.tensor.transpose(turned(m // 4)[:, m % 4 * S:(m % 4 + 1) * S], t.heads[:, lane, m * P:(m + 1) * P], g.ident[0:S, 0:S])
                last.then_inc(s.headsT_ready, 1)
                if after:
                    make(after, BETWEEN + 3)
                pe.wait_ge(s.headsT_act, n)
                pe.wait_ge(s.headsT_dve, n)
                for m in range(WM):
                    nc.tensor.matmul(out_bank[0:S, 0:D], t.headsT[:, lane, m, :], w.proj[:, m, :], start=(m == 0), stop=False)
                nc.tensor.matmul(out_bank[0:S, 0:D], g.ones[0:1, 0:S], w.proj_b[:, :], start=False, stop=True).then_inc(s.proj_ready, 1)
                if after:
                    make(after, BETWEEN + 4)
                    pe.wait_ge(s.added, n)

            for u in range(len(MADE)):
                make(FIRST, u)
            score(FIRST, 0)
            batches(pe, run)

        def keep(eng, copy, scaled, batch, u):
            lane, b, n, pairs = batch
            kind, i = MADE[u]
            eng.wait_ge(made[u], n)
            if kind == "y":
                for c in range(DC):
                    last = nc.scalar.activation(t.yT[:, lane, c, :], make_bank[:, c * S:(c + 1) * S], ACT.Identity,
                                                bias=w.ln[:, DC + c:DC + c + 1], scale=w.ln[:, c:c + 1])
            elif kind == "k":
                last = copy(t.kT[:, lane, i, :], make_bank[:, 0:CTX])
            elif kind == "q":
                last = scaled(t.qT[:, lane, 4 * i:4 * i + 4, :], four(make_bank), WD ** -0.5)
            else:
                kw, heads = WIDE_TILES[i // 2][1], slice(i % 2 * WH // 2, (i % 2 + 1) * WH // 2)
                last = copy(t.v[0:kw, lane, i // 2, heads, 0:WD], make_bank[0:kw, :].rearrange("k (h d) -> k h d", d=WD))
            last.then_inc(kept[u], 1)

        @block.scalar
        def _(act):
            act.wait_ge(g.loaded.wide, g.total.wide)
            act.wait_ge(s.ones, 1)

            def keep_by_act(batch, u):
                if batch and BY_ACT(u):
                    keep(act, nc.scalar.copy, nc.scalar.mul, batch, u)

            def weigh(batch, i):
                act.wait_ge(a[i].rowmax, batch[2])
                for j in range(ITEM):
                    last = nc.scalar.activation(t.probs[:, i % 2, j, :], scores(i)[:, j, :], ACT.Exp, bias=t.rowmax[:, i % 2, j:j + 1])
                last.then_inc(a[i].probs, 1)

            def run(batch, after):
                lane, b, n, pairs = batch
                for i in range(ITEMS):
                    end = i == ITEMS - 1
                    if not end:
                        weigh(batch, i + 1)
                    elif after:
                        weigh(after, 0)
                    if 2 * i < BETWEEN:
                        keep_by_act(after, 2 * i)
                    elif end:
                        keep_by_act(after, BETWEEN)
                    act.wait_ge(a[i].turned_ready, n)
                    nc.scalar.copy(t.probsT[:, i % 2, 0, :], turned(0)[0:TMAX, 0:NT * S]).then_inc(a[i].probsT_act, 1)
                    if 2 * i < BETWEEN:
                        keep_by_act(after, 2 * i + 1)
                    elif end:
                        keep_by_act(after, BETWEEN + 1)
                keep_by_act(after, BETWEEN + 2)
                act.wait_ge(s.headsT_ready, n)
                nc.scalar.copy(t.headsT[:, lane, 0:4, :], four(turned(0))).then_inc(s.headsT_act, 1)
                keep_by_act(after, BETWEEN + 3)
                keep_by_act(after, BETWEEN + 4)

            for u in range(len(MADE)):
                keep_by_act(FIRST, u)
            weigh(FIRST, 0)
            batches(act, run)

        @block.vector
        def _(dve):
            dve.wait_ge(g.loaded.wide, g.total.wide)
            nc.vector.tensor_scalar(bias[:, :], w.mask[:, :], 1.0, -MASKED, ALU.subtract, ALU.mult).then_inc(s.bias, 1)
            nc.vector.memset(g.psum[:, 4:6, :], 0.0).then_inc(s.turned_zero, 1)
            nc.vector.reduce_max(t.any_key[:, :], w.mask[:, :], AX.X).then_inc(s.any_key, 1)
            dve.wait_ge(s.any_key, 1)
            nc.vector.reciprocal(t.any_inverse[:, :], t.any_key[:, :]).then_inc(s.any_inverse, 1)
            dve.wait_ge(s.any_inverse, 1)
            nc.vector.tensor_tensor(t.any[:, :], t.any_key[:, :], t.any_inverse[:, :], ALU.mult).then_inc(s.any, 1)
            dve.wait_ge(s.any, 1)
            dve.wait_ge(s.ones, 1)

            def keep_by_dve(batch, u):
                if batch and not BY_ACT(u):
                    keep(dve, nc.vector.tensor_copy, lambda out, rows, by: nc.vector.tensor_scalar(out, rows, by, None, ALU.mult), batch, u)

            def stats(batch):
                norm_stats(nc, dve, m1, [batch[0:3]], lambda lane, b: g.x[:, b, :])

            def apply(batch):
                lane, b, n, pairs = batch
                norm_apply(nc, dve, m1, lane, n, t.y[:, lane, :], g.x[:, b, :], s.y)

            def peak(batch, i):
                dve.wait_ge(a[i].scores_ready, batch[2])
                nc.vector.reduce_max(t.rowmax[:, i % 2, :], scores(i), AX.X, negate=True).then_inc(a[i].rowmax, 1)

            def divide(batch, i):
                lane, b, n, pairs = batch
                dve.wait_ge(a[i].heads_ready, n)
                nc.vector.reciprocal(t.rowsum[:, :].unsqueeze(2), item_out[:, :, WD:WD + 1]).then_inc(a[i].rowsum, 1)
                dve.wait_ge(a[i].rowsum, n)
                nc.vector.tensor_tensor(t.heads[:, lane, i * ITEM * WD:(i + 1) * ITEM * WD].rearrange("s (h d) -> s h d", d=WD), item_out[:, :, 0:WD],
                                        t.rowsum[:, :].unsqueeze(2).broadcast_to([S, ITEM, WD]), ALU.mult).then_inc(a[i].heads, 1)

            def run(batch, after):
                lane, b, n, pairs = batch
                if after:
                    stats(after)
                for i in range(ITEMS):
                    end = i == ITEMS - 1
                    if not end:
                        peak(batch, i + 1)
                    elif after:
                        peak(after, 0)
                    if i == 1 and after:
                        apply(after)
                    if 2 * i < BETWEEN:
                        keep_by_dve(after, 2 * i)
                    elif end:
                        keep_by_dve(after, BETWEEN)
                    dve.wait_ge(a[i].turned_ready, n)
                    nc.vector.tensor_copy(t.probsT[:, i % 2, 1, :], turned(1)[0:TMAX, 0:NT * S]).then_inc(a[i].probsT_dve, 1)
                    if i > 0:
                        divide(batch, i - 1)
                    if 2 * i < BETWEEN:
                        keep_by_dve(after, 2 * i + 1)
                    elif end:
                        keep_by_dve(after, BETWEEN + 1)
                divide(batch, ITEMS - 1)
                keep_by_dve(after, BETWEEN + 2)
                dve.wait_ge(s.headsT_ready, n)
                nc.vector.tensor_copy(t.headsT[:, lane, 4:8, :], four(turned(1))).then_inc(s.headsT_dve, 1)
                keep_by_dve(after, BETWEEN + 3)
                dve.wait_ge(s.proj_ready, n)
                nc.vector.scalar_tensor_tensor(g.x[:, b, :], out_bank[0:S, 0:D], t.any[:, :], g.x[:, b, :], ALU.mult, ALU.add).then_inc(s.added, 1)
                keep_by_dve(after, BETWEEN + 4)

            stats(FIRST)
            apply(FIRST)
            for u in range(len(MADE)):
                keep_by_dve(FIRST, u)
            peak(FIRST, 0)
            batches(dve, run)



ROWS_ALL = B * S
TILES = 2 * ROWS_ALL // P + NE
SLOTS = (NE - 1) * ROWS_ALL + TILES * P
FILL = 4
FILLS = -(-SLOTS // (P * FILL))
SLOT_ROWS = FILLS * P * FILL
STEPS_OF_TILES = -(-ROWS_ALL // P)
GATHER = 8


def route_phase(nc, g, w, f, slots, experts_in):
    with ExitStack() as ctx:
        s = semaphores(nc, ctx, "route", "running y yT_ready yT gates_ready gates cmp ties behind rank mask chosen prefix_ready "
                       "placed val sum slot slots picked logits larger below gexp gsum grec hid_ready0 hid_ready1 hid0 hid1 out_ready added totals_ready above tiles "
                       "start_in start end past past_tiles tile_expert tile_start tile_row tile_rows tables")
        scattered = [ctx.enter_context(nc.semaphore(f"route_scattered{lane}")) for lane in range(LANES)]
        u = buffers(nc, ctx, "route", y=[S, LANES, D], yT=[P, DC, S], gates=[S, 1, NE], above=[S, 1, NE, NE],
                    equal=[S, 1, NE, NE], rank=[S, 1, NE], mask=[S, NE], chosen=[S, NE], logits=[S, B, 2], larger=[S, B], below=[S, B, 2], gsum=[S, B], grec=[S, B], running=[S, LANES, NE],
                    placed=[S, NE], val=[S, NE], sum=[S, 1], slot=[S, 2], picked=[S, 2, NE], hidden=[P, LANES, HM, S], totals=[S, NE, STEPS_OF_TILES],
                    tiles=[S, NE], start_in=[S, NE, NE], start=[S, NE], end=[S, NE], past=[S, TILES, NE - 1], past_tiles=[S, TILES, NE - 1],
                    tile_expert=[S, TILES], tile_start=[S, TILES], tile_row=[S, TILES], tile_rows=[S, TILES], hold=[S, LANES])
        slot_i = ctx.enter_context(nc.sbuf_tensor("route_slot_i", [S, LANES, 2], I32))
        m1 = norm_of(nc, ctx, "route_ln")
        bank = lambda k: g.psum[:, k, :]
        hid_bank = lambda lane, half: bank(2 * lane + half)
        HALF = HM // 2
        block = ctx.enter_context(nc.Block())

        def batches(eng, run):
            run(None, (0, 0, 1, 1), (1, 1, 2, 1))
            with eng.Fori(0, PAIRS - 1) as pair:
                some = [(k % LANES, eng.snap(pair * LANES + k) if k else eng.snap(pair * LANES), eng.snap(pair * LANES + (k + 1)), eng.snap(pair + (1 + k // LANES)))
                        for k in range(LANES + 2)]
                for k in range(1, LANES + 1):
                    run(some[k - 1], some[k], some[k + 1])
            run((0, B - 2, B - 1, PAIRS), (1, B - 1, B, PAIRS), None)

        FIRST, LAST = (0, 0, 1, 1), (1, B - 1, B, PAIRS)

        @block.sync
        def _(sp):
            for sem, dst, src in g.loads:
                sp.dma_start(dst, src).then_inc(sem, 16)
            for name in ("w1", "w2"):
                for e in range(NE):
                    sp.dma_start(f[name][:, e, :, :], experts_in[name][e]).then_inc(g.loaded.experts, 16)

        @block.gpsimd
        def _(pool):
            pool.wait_ge(g.loaded.cleared, 16 * FILLS)
            nc.gpsimd.memset(u.running[:, 0, :], 0.0).then_inc(s.running, 1)

            def scatter(batch):
                lane, b, n, pairs = batch
                pool.wait_ge(s.slots, n)
                nc.gpsimd.tensor_tensor(u.hold[:, lane:lane + 1], g.eps[0:S, :], g.eps[0:S, :], ALU.add)
                for k in range(2):
                    nc.gpsimd.indirect_dma_start(slots[:, :], bass.IndirectOffsetOnAxis(ap=slot_i[:, lane, k:k + 1], axis=0), u.y[:, lane, :], None).then_inc(scattered[lane], 16)

            def run(before, batch, after):
                if after:
                    norm_root(nc, pool, g, m1, after[0], after[2])
                scatter(batch)

            norm_root(nc, pool, g, m1, 0, 1)
            batches(pool, run)
            for lane in range(LANES):
                pool.wait_ge(scattered[lane], 2 * 16 * PAIRS)

        @block.tensor
        def _(pe):
            pe.wait_ge(g.loaded.moe, g.total.moe)
            pe.wait_ge(s.running, 1)

            def turn_rows(batch):
                lane, b, n, pairs = batch
                pe.wait_ge(s.y, n)
                turn(nc, g, bank(4), u.y[:, lane, :], DC).then_inc(s.yT_ready, 1)

            def gate(batch):
                pe.wait_ge(s.yT, batch[2])
                for c in range(DC):
                    last = nc.tensor.matmul(bank(5)[0:S, 0:NE], u.yT[:, c, :], w.gate[:, c, :], start=(c == 0), stop=(c == DC - 1))
                last.then_inc(s.gates_ready, 1)

            def shared_hidden(batch):
                for half, ready in enumerate((s.hid_ready0, s.hid_ready1)):
                    for m in range(HALF):
                        for c in range(DC):
                            at = (half * HALF + m) * P
                            last = nc.tensor.matmul(hid_bank(batch[0], half)[:, m * S:(m + 1) * S], w.shared1[:, c, at:at + P], u.yT[:, c, :],
                                                    start=(c == 0), stop=(c == DC - 1))
                    last.then_inc(ready, 1)

            def place(batch):
                pe.wait_ge(s.mask, batch[2])
                nc.tensor.matmul(bank(7)[0:S, 0:NE], w.earlier[:, :], u.mask[:, :], start=True, stop=False)
                nc.tensor.matmul(bank(7)[0:S, 0:NE], w.all[:, :], u.running[:, batch[0], :], start=False, stop=True).then_inc(s.prefix_ready, 1)

            def shared_out(batch):
                lane, b, n, pairs = batch
                pe.wait_ge(s.hid0, n)
                pe.wait_ge(s.hid1, n)
                for m in range(HM):
                    last = nc.tensor.matmul(bank(6)[0:S, 0:D], u.hidden[:, lane, m, :], w.shared2[:, m, :], start=(m == 0), stop=(m == HM - 1))
                last.then_inc(s.out_ready, 1)

            def run(before, batch, after):
                gate(batch)
                shared_hidden(batch)
                place(batch)
                if before:
                    shared_out(before)
                if after:
                    turn_rows(after)

            turn_rows(FIRST)
            batches(pe, run)
            pe.wait_ge(s.added, B - 1)
            shared_out(LAST)
            pe.wait_ge(s.slots, B)
            nc.tensor.matmul(bank(7)[0:S, 0:NE], w.all[:, :], u.running[:, 0, :], start=True, stop=True).then_inc(s.totals_ready, 1)

        @block.scalar
        def _(act):
            def keep_rows(batch):
                act.wait_ge(s.yT_ready, batch[2])
                nc.scalar.copy(u.yT[:, :, :], bank(4)[:, 0:DC * S].rearrange("p (c s) -> p c s", s=S)).then_inc(s.yT, 1)

            def run(before, batch, after):
                lane, b, n, pairs = batch
                for half, (ready, done) in enumerate(((s.hid_ready0, s.hid0), (s.hid_ready1, s.hid1))):
                    act.wait_ge(ready, n)
                    nc.scalar.activation(u.hidden[:, lane, half * HALF:(half + 1) * HALF, :].rearrange("p m s -> p (m s)"), hid_bank(lane, half)[:, 0:HALF * S],
                                         ACT.Silu).then_inc(done, 1)
                if after:
                    keep_rows(after)

            keep_rows(FIRST)
            batches(act, run)
            act.wait_ge(s.below, 1)
            nc.scalar.activation(u.below[:, :, :], u.below[:, :, :], ACT.Exp).then_inc(s.gexp, 1)

        @block.vector
        def _(dve):
            dve.wait_ge(g.loaded.moe, g.total.moe)
            dve.wait_ge(s.running, 1)

            def stats(batch):
                norm_stats(nc, dve, m1, [batch[0:3]], lambda lane, b: g.x[:, b, :])

            def apply(batch):
                lane, b, n, pairs = batch
                norm_apply(nc, dve, m1, lane, n, u.y[:, lane, :], g.x[:, b, :], s.y)

            def choose(batch):
                n = batch[2]
                dve.wait_ge(s.gates_ready, n)
                nc.vector.tensor_copy(u.gates[:, 0, :], bank(5)[0:S, 0:NE]).then_inc(s.gates, 1)
                top_two(nc, dve, g, [(0, batch[1], n)], u, s, u.gates)
                dve.wait_ge(s.rank, n)
                nc.vector.tensor_scalar(u.mask[:, :], u.rank[:, 0, :], 2.0, None, ALU.is_lt).then_inc(s.mask, 1)
                nc.vector.scalar_tensor_tensor(u.chosen[:, :], u.rank[:, 0, :], 2.0, u.gates[:, 0, :], ALU.is_lt, ALU.mult).then_inc(s.chosen, 1)
                dve.wait_ge(s.mask, n)

            def place(batch):
                lane, b, n, pairs = batch
                dve.wait_ge(s.prefix_ready, n)
                nc.vector.tensor_tensor(u.running[:, 1 - lane, :], u.running[:, lane, :], u.mask[:, :], ALU.add)
                nc.vector.tensor_tensor(u.placed[:, :], bank(7)[0:S, 0:NE], w.first_slot[:, :], ALU.add).then_inc(s.placed, 1)
                dve.wait_ge(s.placed, n)
                nc.vector.tensor_tensor(u.val[:, :], u.placed[:, :], u.mask[:, :], ALU.mult).then_inc(s.val, 1)
                dve.wait_ge(s.val, n)
                nc.vector.reduce_max(u.slot[:, 1:2], u.val[:, :], AX.X)
                nc.vector.reduce_sum(u.sum[:, :], u.val[:, :], AX.X).then_inc(s.sum, 1)
                dve.wait_ge(s.sum, n)
                nc.vector.tensor_tensor(u.slot[:, 0:1], u.sum[:, :], u.slot[:, 1:2], ALU.subtract).then_inc(s.slot, 1)
                dve.wait_ge(s.slot, n)
                nc.vector.tensor_copy(f.slot_i[:, b, :], u.slot[:, :])
                nc.vector.tensor_copy(slot_i[:, lane, :], u.slot[:, :]).then_inc(s.slots, 1)
                dve.wait_ge(s.chosen, n)
                for k in range(2):
                    last = nc.vector.scalar_tensor_tensor(u.picked[:, k, :], u.val[:, :], u.slot[:, k:k + 1], u.chosen[:, :], ALU.is_equal, ALU.mult)
                last.then_inc(s.picked, 1)
                dve.wait_ge(s.picked, n)
                nc.vector.reduce_sum(u.logits[:, b, :], u.picked[:, :, :], AX.X).then_inc(s.logits, 1)

            def add(batch):
                lane, b, n, pairs = batch
                dve.wait_ge(s.out_ready, n)
                nc.vector.tensor_tensor(g.x[:, b, :], g.x[:, b, :], bank(6)[0:S, 0:D], ALU.add).then_inc(s.added, 1)

            def run(before, batch, after):
                if after:
                    stats(after)
                choose(batch)
                place(batch)
                if after:
                    if before:
                        dve.wait_ge(scattered[after[0]], dve.snap((after[3] - 1) * 32))
                    apply(after)
                if before:
                    add(before)

            stats(FIRST)
            apply(FIRST)
            batches(dve, run)
            add(LAST)
            dve.wait_ge(s.logits, B)
            nc.vector.reduce_max(u.larger[:, :], u.logits[:, :, :], AX.X).then_inc(s.larger, 1)
            dve.wait_ge(s.larger, 1)
            nc.vector.tensor_tensor(u.below[:, :, :], u.logits[:, :, :], u.larger[:, :].unsqueeze(2).broadcast_to([S, B, 2]), ALU.subtract).then_inc(s.below, 1)
            dve.wait_ge(s.gexp, 1)
            nc.vector.reduce_sum(u.gsum[:, :], u.below[:, :, :], AX.X).then_inc(s.gsum, 1)
            dve.wait_ge(s.gsum, 1)
            nc.vector.reciprocal(u.grec[:, :], u.gsum[:, :]).then_inc(s.grec, 1)
            dve.wait_ge(s.grec, 1)
            nc.vector.tensor_tensor(f.gate[:, :, :], u.below[:, :, :], u.grec[:, :].unsqueeze(2).broadcast_to([S, B, 2]), ALU.mult)
            dve.wait_ge(s.totals_ready, 1)
            nc.vector.tensor_tensor(u.totals[:, :, :], bank(7)[0:S, 0:NE].unsqueeze(2).broadcast_to([S, NE, STEPS_OF_TILES]),
                                    w.tile_starts[:, 0:STEPS_OF_TILES].unsqueeze(1).broadcast_to([S, NE, STEPS_OF_TILES]), ALU.is_gt).then_inc(s.above, 1)
            dve.wait_ge(s.above, 1)
            nc.vector.reduce_sum(u.tiles[:, :], u.totals[:, :, :], AX.X).then_inc(s.tiles, 1)
            dve.wait_ge(s.tiles, 1)
            nc.vector.tensor_tensor(u.start_in[:, :, :], u.tiles[:, :].unsqueeze(1).broadcast_to([S, NE, NE]), g.before[:, :, :], ALU.mult).then_inc(s.start_in, 1)
            dve.wait_ge(s.start_in, 1)
            nc.vector.reduce_sum(u.start[:, :], u.start_in[:, :, :], AX.X).then_inc(s.start, 1)
            dve.wait_ge(s.start, 1)
            nc.vector.tensor_tensor(u.end[:, :], u.start[:, :], u.tiles[:, :], ALU.add).then_inc(s.end, 1)
            dve.wait_ge(s.end, 1)
            shape = [S, TILES, NE - 1]
            nc.vector.tensor_tensor(u.past[:, :, :], w.tile_ids[:, :].unsqueeze(2).broadcast_to(shape), u.end[:, 0:NE - 1].unsqueeze(1).broadcast_to(shape),
                                    ALU.is_ge).then_inc(s.past, 1)
            dve.wait_ge(s.past, 1)
            nc.vector.tensor_tensor(u.past_tiles[:, :, :], u.past[:, :, :], u.tiles[:, 0:NE - 1].unsqueeze(1).broadcast_to(shape), ALU.mult).then_inc(s.past_tiles, 1)
            nc.vector.reduce_sum(u.tile_expert[:, :], u.past[:, :, :], AX.X).then_inc(s.tile_expert, 1)
            dve.wait_ge(s.past_tiles, 1)
            nc.vector.reduce_sum(u.tile_start[:, :], u.past_tiles[:, :, :], AX.X).then_inc(s.tile_start, 1)
            dve.wait_ge(s.tile_start, 1)
            nc.vector.tensor_tensor(u.tile_row[:, :], w.tile_ids[:, :], u.tile_start[:, :], ALU.subtract).then_inc(s.tile_row, 1)
            dve.wait_ge(s.tile_expert, 1)
            nc.vector.tensor_scalar(u.tile_rows[:, :], u.tile_expert[:, :], float(ROWS_ALL), None, ALU.mult).then_inc(s.tile_rows, 1)
            dve.wait_ge(s.tile_row, 1)
            dve.wait_ge(s.tile_rows, 1)
            nc.vector.scalar_tensor_tensor(u.tile_start[:, :], u.tile_row[:, :], float(P), u.tile_rows[:, :], ALU.mult, ALU.add).then_inc(s.tables, 1)
            dve.wait_ge(s.tables, 1)
            nc.vector.tensor_copy(f.tile_slot[:, :], u.tile_start[0:1, :])
            nc.vector.tensor_copy(f.tile_expert[:, :], u.tile_expert[0:1, :]).then_inc(s.tables, 1)


def tiles_phase(nc, g, f, slots):
    with ExitStack() as ctx:
        s = semaphores(nc, ctx, "tiles", "xT_ready xT hid_ready0 hid_ready1 hid0 hid1 hT_ready hT_act hT_dve out_ready out")
        loaded, stored = ([ctx.enter_context(nc.semaphore(f"tiles_{n}{lane}")) for lane in range(LANES)] for n in ("loaded", "stored"))
        t = buffers(nc, ctx, "tiles", rows=[P, LANES, D], xT=[P, LANES, DC, P], hidden=[P, LANES, HID], hT=[P, HM, P], out=[P, LANES, D])
        bank = lambda k: g.psum[:, k, :]
        hid_bank = lambda lane, half: bank(1 + 2 * lane + half)
        TP = TILES // LANES
        HALF = HM // 2
        block = ctx.enter_context(nc.Block())

        def tiles(eng, run):
            fixed = [(k % LANES, k, k + 1, k // LANES + 1) for k in range(TILES)] + [None] * 3
            for k in range(LANES):
                run(*fixed[k:k + 4])
            with eng.Fori(1, TP - 2) as pair:
                some = [(k % LANES, eng.snap(pair * LANES + k) if k else eng.snap(pair * LANES), eng.snap(pair * LANES + (k + 1)), eng.snap(pair + (1 + k // LANES)))
                        for k in range(2 * LANES + 1)]
                for k in range(LANES):
                    run(*some[k:k + 4])
            for k in range(TILES - 2 * LANES, TILES):
                run(*fixed[k:k + 4])

        FIRST, SECOND, THIRD = ((k % LANES, k, k + 1, k // LANES + 1) for k in range(3))

        @block.sync
        def _(sp):
            def slots_of(tile):
                return slots[bass.ds(sp.value_load(f.tile_slot[0:1, bass.ds(tile[1], 1)], min_val=0, max_val=SLOTS - P), P), :]

            def load(tile):
                sp.dma_start(t.rows[:, tile[0], :], slots_of(tile)).then_inc(loaded[tile[0]], 16)

            def run(tile, after, third, fourth):
                if fourth:
                    sp.wait_ge(s.xT_ready, after[2])
                    load(fourth)
                there = slots_of(tile)
                sp.wait_ge(s.out, tile[2])
                sp.dma_start(there, t.out[:, tile[0], :]).then_inc(stored[tile[0]], 16)

            load(FIRST)
            load(SECOND)
            sp.wait_ge(s.xT_ready, 1)
            load(THIRD)
            tiles(sp, run)
            for lane in range(LANES):
                sp.wait_ge(stored[lane], 16 * TP)

        @block.tensor
        def _(pe):
            pe.wait_ge(g.loaded.experts, 2 * NE * 16)

            def expert_of(tile):
                return pe.value_load(f.tile_expert[0:1, bass.ds(tile[1], 1)], min_val=0, max_val=NE - 1)

            def turn_rows(tile):
                lane, k, n, pairs = tile
                pe.wait_ge(loaded[lane], pairs * 16 if isinstance(pairs, int) else pe.snap(pairs * 16))
                if tile is not FIRST:
                    pe.wait_ge(s.xT, n - 1 if isinstance(n, int) else pe.snap(n - 1))
                for c in range(DC):
                    last = nc.tensor.transpose(bank(0)[:, c * P:(c + 1) * P], t.rows[:, lane, c * P:(c + 1) * P], g.ident[:, :])
                last.then_inc(s.xT_ready, 1)

            def first_layer(tile):
                lane, k, n, pairs = tile
                e = expert_of(tile)
                pe.wait_ge(s.xT, n)
                for half, ready in enumerate((s.hid_ready0, s.hid_ready1)):
                    for c in range(DC):
                        last = nc.tensor.matmul(hid_bank(lane, half), t.xT[:, lane, c, :], f.w1[:, e, c, half * BANK:(half + 1) * BANK],
                                                start=(c == 0), stop=(c == DC - 1))
                    last.then_inc(ready, 1)

            def run(tile, after, third, fourth):
                lane, k, n, pairs = tile
                pe.wait_ge(s.hid0, n)
                pe.wait_ge(s.hid1, n)
                for m in range(HM):
                    last = nc.tensor.transpose(bank(5 + m // HALF)[:, m % HALF * P:(m % HALF + 1) * P], t.hidden[:, lane, m * P:(m + 1) * P], g.ident[:, :])
                last.then_inc(s.hT_ready, 1)
                if after:
                    first_layer(after)
                if third:
                    turn_rows(third)
                e = expert_of(tile)
                pe.wait_ge(s.hT_act, n)
                pe.wait_ge(s.hT_dve, n)
                for m in range(HM):
                    last = nc.tensor.matmul(bank(7)[:, 0:D], t.hT[:, m, :], f.w2[:, e, m, :], start=(m == 0), stop=(m == HM - 1))
                last.then_inc(s.out_ready, 1)

            turn_rows(FIRST)
            first_layer(FIRST)
            turn_rows(SECOND)
            tiles(pe, run)

        @block.scalar
        def _(act):
            def silu(tile):
                lane, k, n, pairs = tile
                for half, (ready, done) in enumerate(((s.hid_ready0, s.hid0), (s.hid_ready1, s.hid1))):
                    act.wait_ge(ready, n)
                    nc.scalar.activation(t.hidden[:, lane, half * BANK:(half + 1) * BANK], hid_bank(lane, half), ACT.Silu).then_inc(done, 1)

            def run(tile, after, third, fourth):
                act.wait_ge(s.hT_ready, tile[2])
                nc.scalar.copy(t.hT[:, 0:HALF, :].rearrange("p m s -> p (m s)"), bank(5)).then_inc(s.hT_act, 1)
                if after:
                    silu(after)

            silu(FIRST)
            tiles(act, run)

        @block.vector
        def _(dve):
            def keep_rows(tile):
                dve.wait_ge(s.xT_ready, tile[2])
                nc.vector.tensor_copy(t.xT[:, tile[0], :, :].rearrange("p c s -> p (c s)"), bank(0)[:, 0:DC * P]).then_inc(s.xT, 1)

            def run(tile, after, third, fourth):
                lane, k, n, pairs = tile
                dve.wait_ge(s.hT_ready, n)
                nc.vector.tensor_copy(t.hT[:, HALF:HM, :].rearrange("p m s -> p (m s)"), bank(6)).then_inc(s.hT_dve, 1)
                if third:
                    keep_rows(third)
                if not (isinstance(pairs, int) and pairs == 1):
                    dve.wait_ge(stored[lane], (pairs - 1) * 16 if isinstance(pairs, int) else dve.snap((pairs - 1) * 16))
                dve.wait_ge(s.out_ready, n)
                nc.vector.tensor_copy(t.out[:, lane, :], bank(7)[:, 0:D]).then_inc(s.out, 1)

            keep_rows(FIRST)
            keep_rows(SECOND)
            tiles(dve, run)


def combine_phase(nc, g, f, slots, out):
    with ExitStack() as ctx:
        s = semaphores(nc, ctx, "combine", "slots held half rows")
        gathered, stored = ([ctx.enter_context(nc.semaphore(f"combine_{n}{k}")) for k in range(GATHER)] for n in ("gathered", "stored"))
        t = buffers(nc, ctx, "combine", got=[S, GATHER, 2, D], hold=[S, GATHER])
        slot_i = ctx.enter_context(nc.sbuf_tensor("combine_slot_i", [S, GATHER, 2], I32))
        block = ctx.enter_context(nc.Block())
        ROUNDS = B // GATHER

        @block.gpsimd
        def _(pool):
            with pool.Fori(0, ROUNDS) as turn_:
                for k in range(GATHER):
                    pool.wait_ge(s.slots, pool.snap(turn_ * GATHER + (k + 1)))
                    nc.gpsimd.tensor_tensor(t.hold[:, k:k + 1], g.eps[0:S, :], g.eps[0:S, :], ALU.add).then_inc(s.held, 1)
                    for j in range(2):
                        nc.gpsimd.indirect_dma_start(t.got[:, k, j, :], None, slots[:, :], bass.IndirectOffsetOnAxis(ap=slot_i[:, k, j:j + 1], axis=0)).then_inc(gathered[k], 16)

        @block.vector
        def _(dve):
            def slots_of(k, b):
                nc.vector.tensor_copy(slot_i[:, k, :], f.slot_i[:, b, :]).then_inc(s.slots, 1)

            def add(k, b, n, done):
                dve.wait_ge(gathered[k], done)
                nc.vector.scalar_tensor_tensor(g.x[:, b, :], t.got[:, k, 0, :], f.gate[:, b, 0:1], g.x[:, b, :], ALU.mult, ALU.add).then_inc(s.half, 1)
                dve.wait_ge(s.half, n)
                nc.vector.scalar_tensor_tensor(g.x[:, b, :], t.got[:, k, 1, :], f.gate[:, b, 1:2], g.x[:, b, :], ALU.mult, ALU.add).then_inc(s.rows, 1)

            for k in range(GATHER):
                slots_of(k, k)
            with dve.Fori(0, ROUNDS - 1) as turn_:
                done = dve.snap(turn_ * 32 + 32)
                for k in range(GATHER):
                    b = dve.snap(turn_ * GATHER + k) if k else dve.snap(turn_ * GATHER)
                    add(k, b, dve.snap(turn_ * GATHER + (k + 1)), done)
                    dve.wait_ge(s.held, dve.snap(turn_ * GATHER + (k + 1)))
                    dve.wait_ge(s.rows, dve.snap(turn_ * GATHER + (k + 1)))
                    slots_of(k, dve.snap(turn_ * GATHER + (k + GATHER)))
            for k in range(GATHER):
                add(k, B - GATHER + k, B - GATHER + k + 1, 32 * ROUNDS)

        @block.sync
        def _(sp):
            with sp.Fori(0, ROUNDS) as turn_:
                for k in range(GATHER):
                    sp.wait_ge(s.rows, sp.snap(turn_ * GATHER + (k + 1)))
                    b = sp.snap(turn_ * GATHER + k) if k else sp.snap(turn_ * GATHER)
                    sp.dma_start(out[b], g.x[:, b, :]).then_inc(stored[k], 16)
            for k in range(GATHER):
                sp.wait_ge(stored[k], 16 * ROUNDS)


def clear_semaphores(nc):
    with nc.Block() as block:
        @block.gpsimd
        def _(pool):
            nc.gpsimd.sem_clear(range(min(nc.free_semaphores), max(nc.free_semaphores) + 1))


def decoder(nc, i, out, slots):
    with ExitStack() as ctx:
        sb = lambda n, shape, dt=F32: ctx.enter_context(nc.sbuf_tensor(n, shape, dt))
        g = Fields(x=sb("x", [S, B, D]), ident=sb("ident", [P, P]), ident_b=sb("ident_b", [P, P], BF16),
                            causal=sb("causal", [S, QT * S], BF16), own_scaled=sb("own_scaled", [P, P // HD]), ones=sb("ones", [NH, P]),
                            before=sb("before", [S, NE, NE]), eps=sb("eps", [P, 1]), neg_half=sb("neg_half", [P, 32]))
        g.psum = ctx.enter_context(nc.psum_tensor("banks", [P, 8, BANK], F32))
        sets = "first cross mix rot wide moe experts cleared"
        g.loaded = Fields(**{n: ctx.enter_context(nc.semaphore("loaded_" + n)) for n in sets.split() + ["filled"]})
        g.total = Fields(**{n: 0 for n in sets.split()})
        g.loads = []

        def load(which, dst, src):
            g.loads.append((g.loaded[which], dst, src))
            g.total[which] += 16

        def weight(stack, which, name, shape, dt=F32):
            dst = stack.enter_context(nc.sbuf_tensor("w_" + name, shape, dt))
            load(which, dst[tuple(slice(None) for _ in shape)], i[name])
            return dst

        with ExitStack() as late, ExitStack() as early:
            moe_w = Fields(**{n: weight(ctx, "moe", "moe_" + n, shape) for n, shape in dict(
                gate=[P, DC, NE], earlier=[S, S], all=[S, S], first_slot=[S, NE], tile_starts=[S, STEPS_OF_TILES], tile_ids=[S, TILES]).items()})
            wide_w = Fields(mask=weight(late, "wide", "wide_mask", [S, CTX], U8), **{n: weight(late, "wide", "wide_" + n, shape) for n, shape in dict(
                q=[P, DC, WI], k0=[P, WI], k1=[CD - P, WI], v0=[P, WI], v1=[CD - P, WI], proj=[P, WM, D], proj_b=[1, D], ln=[P, 2 * DC]).items()})
            wide_loads, g.loads = g.loads, []
            load("first", g.x[:, 0:2, :], i["x"][0:2].rearrange("b s d -> s b d"))
            for n in ("ident", "ident_b", "causal", "own_scaled", "ones", "before"):
                t = g[n]
                load("first", t[tuple(slice(None) for _ in t.shape)], i[n].bitcast(t.dtype))
            self_w = Fields(qkv=weight(early, "first", "self_qkv", [P, DC, 3 * D]), proj=weight(early, "first", "self_proj", [P, DC, D]))
            load("first", g.x[:, 2:B, :], i["x"][2:B].rearrange("b s d -> s b d"))
            cross_w = Fields(**{n: weight(early, "cross", "cross_" + n, shape) for n, shape in dict(
                q=[P, DC, D], kv0=[P, 2 * D], kv1=[CD - P, 2 * D], lkv=[P, DC, 2 * D], proj=[P, DC, D], proj_b=[1, D], ln_l=[P, 2 * DC],
                ln_x0=[P, 2], ln_x1=[CD - P, 2], qn_g=[P, 1], kn_g=[P, 1]).items()}, mask=weight(early, "cross", "cross_mask", [B, CTX], U8))
            mix_w = Fields(**{n: weight(early, "mix", "mix_" + n, shape) for n, shape in dict(
                qkv=[P, DC, 3 * D], in_b=[P, 3 * DC], proj=[P, DC, D], proj_b=[1, D], gate=[P, DC, NE], gate_b=[1, NE], expert=[P, DC, NE * D],
                expert_b=[NE, D], ln1_w=[S, D], ln1_b=[S, D], ln2_w=[S, D], ln2_b=[S, D], cos=[S, D], sin=[S, D]).items()})
            rot_w = Fields(**{n: weight(early, "rot", "rot_" + n, shape) for n, shape in dict(
                qkv=[P, DC, 3 * D], qk_b=[P, 2 * DC], v_b=[1, D], proj=[P, DC, D], proj_b=[1, D], w1=[P, D], b1=[P, DC], w2T=[2 * NQ, D],
                b2=[2 * NQ, 1], hadamard=[2 * NQ, RG * VROWS], rot=[P, 4, ROTATED], half=[P, 2], uniform=[S, S],
                real=[P, VROWS], imag=[P, VROWS], sum8=[VROWS, RG]).items()})
            g.loads += wide_loads
            g.zeros = early.enter_context(nc.sbuf_tensor("zeros", [P, FILL * D], F32))
            g.slots = slots
            causal_phase(nc, g, self_w, False)
            clear_semaphores(nc)
            normed_cross_phase(nc, g, cross_w, i["ctx"])
            clear_semaphores(nc)
            causal_phase(nc, g, mix_w, True)
            clear_semaphores(nc)
            rotation_phase(nc, g, rot_w)
            early.close()
            clear_semaphores(nc)
            wide_cross_phase(nc, g, wide_w, i["ctxT"])
            late.close()
            f = Fields(w1=sb("moe_w1", [P, NE, DC, HID]), w2=sb("moe_w2", [P, NE, HM, D]), slot_i=sb("moe_slot_i", [S, B, 2], I32), gate=sb("moe_gate", [S, B, 2]),
                       tile_slot=sb("moe_tile_slot", [1, TILES], I32), tile_expert=sb("moe_tile_expert", [1, TILES], I32))
            clear_semaphores(nc)
            with ExitStack() as shared:
                g.loads = []
                for n, shape in dict(shared1=[P, DC, HID], shared2=[P, HM, D]).items():
                    moe_w[n] = weight(shared, "moe", "moe_" + n, shape)
                route_phase(nc, g, moe_w, f, slots, dict(w1=i["moe_w1"], w2=i["moe_w2"]))
            clear_semaphores(nc)
            tiles_phase(nc, g, f, slots)
            clear_semaphores(nc)
            combine_phase(nc, g, f, slots, out)


def program(nc, arrays, out_shape):
    import concourse.mybir as mybir
    ins = {n: nc.dram_tensor(f"in_{n}", a.shape, mybir.dt.from_np(a.dtype), kind="ExternalInput").ap() for n, a in arrays.items()}
    out = nc.dram_tensor("out", out_shape, F32, kind="ExternalOutput").ap()
    slots = nc.dram_tensor("slots", [SLOT_ROWS, D], F32, kind="Internal").ap()
    decoder(nc, ins, out, slots)



def constants():
    f = np.float32
    short = lambda v: (v.astype(f).view(np.uint32) >> 16).astype(np.uint16)
    i = np.arange(S)
    inv = (1.0 / f(10000.0) ** (np.arange(0, HD, 2, dtype=f) / f(HD))).astype(f)
    ang = (i.astype(f)[:, None] * inv[None, :]).astype(f)
    cos, sin = np.cos(ang).astype(f), np.sin(ang).astype(f)
    half = (np.arange(P)[:, None] // HD % 2 == np.arange(2)[None, :]).astype(f)
    e = np.arange(NE)
    row, of = np.arange(P)[:, None], np.arange(VROWS)[None, :]
    part_of = lambda part: ((row // VROWS == of // NQ) & (row % VROWS == part * NQ + of % NQ)).astype(f)
    return dict(
        ident=np.eye(P, dtype=f), ident_b=short(np.eye(P, dtype=f)),
        causal=short(np.tile(np.where(i[None, :] > i[:, None], f(MASKED), f(0)), (1, QT))),
        own_scaled=(np.arange(P)[:, None] // HD == np.arange(P // HD)[None, :]).astype(f) * f(HD ** -0.5), rot_half=half, rot_real=part_of(0), rot_imag=part_of(1),
        rot_sum8=(np.arange(VROWS)[:, None] // NQ == np.arange(RG)[None, :]).astype(f), rot_uniform=np.full((S, S), 1.0 / S, f), ones=np.ones((NH, P), f),
        before=np.broadcast_to((e[None, :] < e[:, None]).astype(f), (S, NE, NE)).copy(),
        moe_earlier=(i[:, None] < i[None, :]).astype(f), moe_all=np.ones((S, S), f), moe_first_slot=np.tile((np.arange(NE) * ROWS_ALL).astype(f), (S, 1)),
        moe_tile_starts=np.tile((np.arange(STEPS_OF_TILES) * P).astype(f), (S, 1)), moe_tile_ids=np.tile(np.arange(TILES).astype(f), (S, 1)),
        mix_cos=np.tile(np.repeat(cos, 2, axis=1), (1, NH)), mix_sin=np.tile(np.stack([-sin, sin], -1).reshape(S, HD), (1, NH)))


def two_blocks(m):
    out = np.zeros((2 * NQ, RG, VROWS), m.dtype)
    for part in range(2):
        out[part * NQ:(part + 1) * NQ, :, part * NQ:(part + 1) * NQ] = m[:, None, :]
    return out.reshape(2 * NQ, RG * VROWS)


def kernel(**inputs):
    import concourse.bacc as bacc
    from concourse.bass_utils import run_bass_kernel_spmd

    a = {n: np.asarray(v) for n, v in inputs.items()}
    rows = lambda m: np.ascontiguousarray(m.reshape(m.shape[0] // P, P, m.shape[1]).transpose(1, 0, 2))
    cols = lambda v: np.ascontiguousarray(v.reshape(-1, P).T)
    wide = lambda v: np.ascontiguousarray(np.broadcast_to(v, (S, v.shape[-1])))
    arrays = dict(constants(), x=a["x"],
        self_qkv=rows(a["L0_attn_w_qkv"]), self_proj=rows(a["L0_attn_w_proj"]),
        mix_qkv=rows(a["L0_ffn_in_proj_w"].T), mix_in_b=cols(a["L0_ffn_in_proj_b"]), mix_proj=rows(a["L0_ffn_out_proj_w"].T),
        mix_proj_b=a["L0_ffn_out_proj_b"].reshape(1, D), mix_gate=rows(a["L0_ffn_gate_w"].T), mix_gate_b=a["L0_ffn_gate_b"].reshape(1, NE),
        mix_expert=rows(a["L0_ffn_expert_w"].transpose(2, 0, 1).reshape(D, NE * D)), mix_expert_b=a["L0_ffn_expert_b"],
        mix_ln1_w=wide(a["L0_ffn_ln1_w"]), mix_ln1_b=wide(a["L0_ffn_ln1_b"]), mix_ln2_w=wide(a["L0_ffn_ln2_w"]), mix_ln2_b=wide(a["L0_ffn_ln2_b"]),
        ctx=a["ctx_768"], cross_mask=a["mask_BxS2_bk0"],
        cross_q=rows(a["L0_xattn_Wq"].T), cross_kv0=np.ascontiguousarray(a["L0_xattn_Wkv"].T[0:P]), cross_kv1=np.ascontiguousarray(a["L0_xattn_Wkv"].T[P:CD]),
        cross_lkv=rows(a["L0_xattn_Wlkv"].T), cross_proj=rows(a["L0_xattn_Wo"].T), cross_proj_b=a["L0_xattn_bo"].reshape(1, D),
        cross_ln_l=np.concatenate([cols(a["L0_xattn_ln_l_g"]), cols(a["L0_xattn_ln_l_b"])], 1),
        cross_ln_x0=np.stack([a["L0_xattn_ln_x_g"][0:P], a["L0_xattn_ln_x_b"][0:P]], 1), cross_ln_x1=np.stack([a["L0_xattn_ln_x_g"][P:], a["L0_xattn_ln_x_b"][P:]], 1),
        cross_qn_g=np.tile(a["L0_xattn_qn_g"], P // XD).reshape(P, 1), cross_kn_g=np.tile(a["L0_xattn_kn_g"], P // XD).reshape(P, 1),
        rot_qkv=rows(np.concatenate([a["L1_attn_wq"], a["L1_attn_wk"], a["L1_attn_wv"]], 1)),
        rot_qk_b=np.concatenate([cols(a["L1_attn_bq"]), cols(a["L1_attn_bk"])], 1), rot_v_b=a["L1_attn_bv"].reshape(1, D),
        rot_proj=rows(a["L1_attn_wo"]), rot_proj_b=a["L1_attn_bo"].reshape(1, D), rot_w1=np.tile(a["L1_attn_w1"], (P // HD, 1)),
        rot_b1=cols(a["L1_attn_b1"]), rot_w2T=a["L1_attn_w2"].T,
        rot_b2=a["L1_attn_b2"].reshape(2 * NQ, 1), rot_hadamard=two_blocks(a["L1_attn_hadamard"]),
        rot_rot=np.repeat(a["L1_attn_rot"][:, :NQ // 2, 0][[[head_at(r, e, c) for e in range(2) for c in range(DC)] for r in range(RG)]].transpose(0, 2, 1), ROWS, axis=0),
        ctxT=np.ascontiguousarray(a["ctx_768"].transpose(2, 0, 1)), wide_mask=a["mask_1x1xSxS2_bk0"].reshape(S, CTX),
        wide_q=rows(a["L1_xattn_Wq"]), wide_k0=a["L1_xattn_Wkv"][0:P, 0:WI], wide_k1=a["L1_xattn_Wkv"][P:CD, 0:WI],
        wide_v0=a["L1_xattn_Wkv"][0:P, WI:], wide_v1=a["L1_xattn_Wkv"][P:CD, WI:], wide_proj=rows(a["L1_xattn_Wo"]),
        wide_proj_b=a["L1_xattn_bo"].reshape(1, D), wide_ln=np.concatenate([cols(a["L1_xattn_ln_gamma"]), cols(a["L1_xattn_ln_beta"])], 1),
        moe_shared1=rows(a["L1_ffn_shared_w1"].T), moe_shared2=rows(a["L1_ffn_shared_w2"].T),
        moe_gate=rows(a["L1_ffn_gate_w"].T),
        moe_w1=np.stack([rows(m.T) for m in a["L1_ffn_experts_w1"]]),
        moe_w2=np.stack([rows(m.T) for m in a["L1_ffn_experts_w2"]]),
    )
    arrays = {n: np.ascontiguousarray(v) for n, v in arrays.items()}
    nc = bacc.Bacc("TRN2", target_bir_lowering=False, num_devices=1)
    program(nc, arrays, (B, S, D))
    r = run_bass_kernel_spmd(nc, [{f"in_{n}": v for n, v in arrays.items()}], core_ids=[0])
    return r.results[0]["out"]
```
